# Optimizing a Trainium2 kernel written in Bass

```python
import numpy as np
import jax
import jax.numpy as jnp

def _softmax(x, axis=-1):
    return jax.nn.softmax(x, axis=axis)

def _gelu(x):
    return jax.nn.gelu(x, approximate=True)

def _silu(x):
    return jax.nn.silu(x)

def _sigmoid(x):
    return jax.nn.sigmoid(x)

def _layernorm(x, axis=-1, eps=1e-05):
    m = jnp.mean(x, axis=axis, keepdims=True)
    v = jnp.var(x, axis=axis, keepdims=True)
    return (x - m) / jnp.sqrt(v + eps)

def _scatter_add(tgt, idx, src, axis=0):
    return tgt.at[idx].add(src)

def _segment_sum(src, seg, n):
    return jax.ops.segment_sum(src, seg, n)
kernel_name = 'mk_prb_d2_jaxref_r8_4517a7'

def setup_inputs(seed: int=0):
    np.random.seed(seed)
    _w = jnp.asarray

    def _L0_attn_setup():
        import math
        import jax, jax.numpy as jnp
        import numpy as np
        B, S, D, H = (2, 256, 128, 16)
        HD = D // H
        key = jax.random.key(seed)
        k1, k2, k3 = jax.random.split(key, 3)
        h = jax.random.normal(k1, (B, S, D), dtype=jnp.float32)
        Wqvk = jax.random.normal(k2, (D, 3 * D), dtype=jnp.float32) * (1.0 / math.sqrt(D))
        Wo = jax.random.normal(k3, (D, D), dtype=jnp.float32) * (1.0 / math.sqrt(D))
        return {'h': h, 'Wqvk': Wqvk, 'Wo': Wo}
    _L0_attn_in = _L0_attn_setup()

    def _L0_ffn_setup():
        import jax, jax.numpy as jnp
        import numpy as np
        B, T = (2, 256)
        D_MODEL, D_HIDDEN = (128, 256)
        N_EXPERTS, TOP_K = (8, 2)
        N_TOKENS = B * T
        CAPACITY = 2 * N_TOKENS * TOP_K // N_EXPERTS
        key = jax.random.key(seed)
        k_x, k_rw, k_w, k_v, k_o = jax.random.split(key, 5)
        x = jax.random.normal(k_x, (B, T, D_MODEL), jnp.float32)
        router_w = jax.random.normal(k_rw, (N_EXPERTS, D_MODEL), jnp.float32) * D_MODEL ** (-0.5)
        router_b = jnp.zeros((N_EXPERTS,), jnp.float32)
        W = jax.random.normal(k_w, (N_EXPERTS, D_MODEL, D_HIDDEN), jnp.float32) * D_MODEL ** (-0.5)
        V = jax.random.normal(k_v, (N_EXPERTS, D_MODEL, D_HIDDEN), jnp.float32) * D_MODEL ** (-0.5)
        W_out = jax.random.normal(k_o, (N_EXPERTS, D_HIDDEN, D_MODEL), jnp.float32) * D_HIDDEN ** (-0.5)
        return {'x': x, 'router_w': router_w, 'router_b': router_b, 'W': W, 'V': V, 'W_out': W_out}
    _L0_ffn_in = _L0_ffn_setup()

    def _L1_attn_setup():
        import jax, jax.numpy as jnp
        import numpy as np
        HIDDEN = 128
        HEADS = 8
        HEAD = HIDDEN // HEADS
        EPS = 1e-05

        def _gammas():
            lo = np.log(1.0 / 512.0)
            hi = np.log(1.0 / 32.0)
            lin = np.linspace(lo, hi, HEADS)
            return jnp.asarray(1.0 - np.exp(lin), dtype=jnp.float32)

        def _decay_mask(S, gammas):
            idx = jnp.arange(S)
            diff = idx[:, None] - idx[None, :]
            causal = diff >= 0
            safe = jnp.where(causal, diff, 0).astype(jnp.float32)
            D = jnp.where(causal[None], gammas[:, None, None] ** safe[None], 0.0)
            return D

        def _msr_forward(x, Wq, Wk, Wv, W1, W2, gn_w, gn_b):
            B, S, _ = x.shape
            xh = x.reshape(B, S, HEADS, HEAD)
            q = jnp.einsum('bshd,hde->bshe', xh, Wq)
            k = jnp.einsum('bshd,hde->bshe', xh, Wk)
            v = jnp.einsum('bshd,hde->bshe', xh, Wv)
            D = _decay_mask(S, _gammas())
            scores = jnp.einsum('bnhd,bmhd->bhnm', q, k) * D[None]
            ret = jnp.einsum('bhnm,bmhd->bnhd', scores, v)
            mu = jnp.mean(ret, axis=-1, keepdims=True)
            var = jnp.var(ret, axis=-1, keepdims=True)
            ret = (ret - mu) * jax.lax.rsqrt(var + EPS)
            ret = ret.reshape(B, S, HIDDEN) * gn_w + gn_b
            gated = x @ W1
            out = gated * jax.nn.sigmoid(gated) + ret
            return out @ W2
        key = jax.random.key(seed)
        ks = jax.random.split(key, 7)
        B, S = (2, 256)
        x = jax.random.normal(ks[0], (B, S, HIDDEN), dtype=jnp.float32)
        Wq = jax.random.normal(ks[1], (HEADS, HEAD, HEAD), dtype=jnp.float32) / HEAD
        Wk = jax.random.normal(ks[2], (HEADS, HEAD, HEAD), dtype=jnp.float32) / HEAD
        Wv = jax.random.normal(ks[3], (HEADS, HEAD, HEAD), dtype=jnp.float32) / HEAD
        W1 = jax.random.normal(ks[4], (HIDDEN, HIDDEN), dtype=jnp.float32) / HIDDEN
        W2 = jax.random.normal(ks[5], (HIDDEN, HIDDEN), dtype=jnp.float32) / HIDDEN
        gn_w = jnp.ones((HIDDEN,), dtype=jnp.float32)
        gn_b = jnp.zeros((HIDDEN,), dtype=jnp.float32)
        return {'x': x, 'Wq': Wq, 'Wk': Wk, 'Wv': Wv, 'W1': W1, 'W2': W2, 'gn_w': gn_w, 'gn_b': gn_b}
    _L1_attn_in = _L1_attn_setup()

    def _L1_ffn_setup():
        import jax, jax.numpy as jnp
        import numpy as np
        TOP_P = 0.8
        B, T, H, F, E = (2, 256, 128, 512, 8)
        key = jax.random.key(seed)
        k0, k1, k2, k3 = jax.random.split(key, 4)
        x = jax.random.normal(k0, (B, T, H), jnp.float32)
        Wr = jax.random.normal(k1, (H, E), jnp.float32) * 0.02
        br = jnp.zeros((E,), jnp.float32)
        W1 = jax.random.normal(k2, (E, H, F), jnp.float32) * 0.02
        b1 = jnp.zeros((E, F), jnp.float32)
        W2 = jax.random.normal(k3, (E, F, H), jnp.float32) * 0.02
        b2 = jnp.zeros((E, H), jnp.float32)
        return {'x': x, 'Wr': Wr, 'br': br, 'W1': W1, 'b1': b1, 'W2': W2, 'b2': b2}
    _L1_ffn_in = _L1_ffn_setup()
    _d = {'L0_attn_h': _L0_attn_in['h'], 'L0_attn_Wqvk': _L0_attn_in['Wqvk'], 'L0_attn_Wo': _L0_attn_in['Wo'], 'L0_ffn_router_w': _L0_ffn_in['router_w'], 'L0_ffn_router_b': _L0_ffn_in['router_b'], 'L0_ffn_W': _L0_ffn_in['W'], 'L0_ffn_V': _L0_ffn_in['V'], 'L0_ffn_W_out': _L0_ffn_in['W_out'], 'L1_attn_Wq': _L1_attn_in['Wq'], 'L1_attn_Wk': _L1_attn_in['Wk'], 'L1_attn_Wv': _L1_attn_in['Wv'], 'L1_attn_W1': _L1_attn_in['W1'], 'L1_attn_W2': _L1_attn_in['W2'], 'L1_attn_gn_w': _L1_attn_in['gn_w'], 'L1_attn_gn_b': _L1_attn_in['gn_b'], 'L1_ffn_Wr': _L1_ffn_in['Wr'], 'L1_ffn_br': _L1_ffn_in['br'], 'L1_ffn_W1': _L1_ffn_in['W1'], 'L1_ffn_b1': _L1_ffn_in['b1'], 'L1_ffn_W2': _L1_ffn_in['W2'], 'L1_ffn_b2': _L1_ffn_in['b2']}
    _x0 = _d['L0_attn_h']
    _d['L0_attn_h'] = jax.random.normal(jax.random.fold_in(jax.random.key(seed), 1), (16, 256, 128), dtype=_x0.dtype)
    del _x0
    return _d

def reference(L0_attn_h, L0_attn_Wqvk, L0_attn_Wo, L0_ffn_router_w, L0_ffn_router_b, L0_ffn_W, L0_ffn_V, L0_ffn_W_out, L1_attn_Wq, L1_attn_Wk, L1_attn_Wv, L1_attn_W1, L1_attn_W2, L1_attn_gn_w, L1_attn_gn_b, L1_ffn_Wr, L1_ffn_br, L1_ffn_W1, L1_ffn_b1, L1_ffn_W2, L1_ffn_b2):

    def _L0_attn_ref(h, Wqvk, Wo):
        import math
        import jax, jax.numpy as jnp
        import numpy as np
        B, S, D, H = (2, 256, 128, 16)
        HD = D // H
        b, s, d = h.shape
        qvk = (h @ Wqvk).reshape(b, s, 3, H, HD)
        q, v, k = (qvk[:, :, 0], qvk[:, :, 1], qvk[:, :, 2])
        scores = jnp.einsum('bshi,bthi->bsth', q, k)
        mask = jnp.where(jnp.arange(s)[None, :] > jnp.arange(s)[:, None], jnp.float32(-jnp.inf), jnp.float32(0.0))
        scores = scores + mask[None, :, :, None]
        scores = scores / math.sqrt(d)
        weights = jax.nn.softmax(scores, axis=2)
        wv = jnp.einsum('bsth,bthi->bshi', weights, v).reshape(b, s, d)
        return wv @ Wo

    def _L0_ffn_ref(x, router_w, router_b, W, V, W_out):
        import jax, jax.numpy as jnp
        import numpy as np
        B, T = (2, 256)
        D_MODEL, D_HIDDEN = (128, 256)
        N_EXPERTS, TOP_K = (8, 2)
        N_TOKENS = B * T
        CAPACITY = 2 * N_TOKENS * TOP_K // N_EXPERTS
        Bq, Tq, D = x.shape
        N = Bq * Tq
        x_flat = x.reshape(N, D)
        router_logits = x_flat @ router_w.T + router_b
        top_vals, top_ids = jax.lax.top_k(router_logits, TOP_K)
        top_probs = jax.nn.softmax(top_vals, axis=-1)
        x_pad = jnp.concatenate([x_flat, jnp.zeros((1, D), x_flat.dtype)], axis=0)
        probs_pad = jnp.concatenate([top_probs, jnp.zeros((1, TOP_K), top_probs.dtype)], axis=0)
        out = jnp.zeros((N + 1, D), x_flat.dtype)
        for e in range(N_EXPERTS):
            tok, slot = jnp.nonzero(top_ids == e, size=CAPACITY, fill_value=(N, 0))
            w = probs_pad[tok, slot][:, None]
            xin = x_pad[tok]
            a = xin @ W[e]
            b = xin @ V[e]
            y = a * (b * jax.nn.sigmoid(b)) @ W_out[e]
            out = out.at[tok].add(y * w)
        return out[:N].reshape(Bq, Tq, D)

    def _L1_attn_ref(x, Wq, Wk, Wv, W1, W2, gn_w, gn_b):
        import jax, jax.numpy as jnp
        import numpy as np
        HIDDEN = 128
        HEADS = 8
        HEAD = HIDDEN // HEADS
        EPS = 1e-05

        def _gammas():
            lo = np.log(1.0 / 512.0)
            hi = np.log(1.0 / 32.0)
            lin = np.linspace(lo, hi, HEADS)
            return jnp.asarray(1.0 - np.exp(lin), dtype=jnp.float32)

        def _decay_mask(S, gammas):
            idx = jnp.arange(S)
            diff = idx[:, None] - idx[None, :]
            causal = diff >= 0
            safe = jnp.where(causal, diff, 0).astype(jnp.float32)
            D = jnp.where(causal[None], gammas[:, None, None] ** safe[None], 0.0)
            return D

        def _msr_forward(x, Wq, Wk, Wv, W1, W2, gn_w, gn_b):
            B, S, _ = x.shape
            xh = x.reshape(B, S, HEADS, HEAD)
            q = jnp.einsum('bshd,hde->bshe', xh, Wq)
            k = jnp.einsum('bshd,hde->bshe', xh, Wk)
            v = jnp.einsum('bshd,hde->bshe', xh, Wv)
            D = _decay_mask(S, _gammas())
            scores = jnp.einsum('bnhd,bmhd->bhnm', q, k) * D[None]
            ret = jnp.einsum('bhnm,bmhd->bnhd', scores, v)
            mu = jnp.mean(ret, axis=-1, keepdims=True)
            var = jnp.var(ret, axis=-1, keepdims=True)
            ret = (ret - mu) * jax.lax.rsqrt(var + EPS)
            ret = ret.reshape(B, S, HIDDEN) * gn_w + gn_b
            gated = x @ W1
            out = gated * jax.nn.sigmoid(gated) + ret
            return out @ W2
        return _msr_forward(x, Wq, Wk, Wv, W1, W2, gn_w, gn_b)

    def _L1_ffn_ref(x, Wr, br, W1, b1, W2, b2):
        import jax, jax.numpy as jnp
        import numpy as np
        TOP_P = 0.8
        B, T, H, F, E = (2, 256, 128, 512, 8)
        probs = jax.nn.softmax(x @ Wr + br, axis=-1)
        sorted_idx = jnp.argsort(-probs, axis=-1)
        sorted_probs = jnp.take_along_axis(probs, sorted_idx, axis=-1)
        cum = jnp.cumsum(sorted_probs, axis=-1)
        mask = cum < TOP_P
        mask = mask.at[..., 0].set(True)
        inv = jnp.argsort(sorted_idx, axis=-1)
        keep = jnp.take_along_axis(mask, inv, axis=-1)
        gate = probs * keep
        h = jax.nn.relu(jnp.einsum('bth,ehf->betf', x, W1) + b1[None, :, None, :])
        y = jnp.einsum('betf,efh->beth', h, W2) + b2[None, :, None, :]
        return jnp.einsum('bte,beth->bth', gate, y)
    x = L0_attn_h
    xn = _layernorm(x, axis=-1)
    x = x + _L0_attn_ref(xn, L0_attn_Wqvk, L0_attn_Wo) + _L0_ffn_ref(xn, L0_ffn_router_w, L0_ffn_router_b, L0_ffn_W, L0_ffn_V, L0_ffn_W_out)
    xn = _layernorm(x, axis=-1)
    x = x + _L1_attn_ref(xn, L1_attn_Wq, L1_attn_Wk, L1_attn_Wv, L1_attn_W1, L1_attn_W2, L1_attn_gn_w, L1_attn_gn_b) + _L1_ffn_ref(xn, L1_ffn_Wr, L1_ffn_br, L1_ffn_W1, L1_ffn_b1, L1_ffn_W2, L1_ffn_b2)
    return x

_drawn_inputs = setup_inputs


def setup_inputs(seed=0):
    import zlib

    import numpy as np

    out = dict(_drawn_inputs(seed))
    spreads = {'L0_ffn_router_b': (0.0, 0.1),
     'L1_attn_gn_w': (1.0, 0.6),
     'L1_attn_gn_b': (0.0, 0.8),
     'L1_ffn_br': (0.0, 0.53),
     'L1_ffn_b1': (0.0, 0.8),
     'L1_ffn_b2': (0.0, 0.1)}
    factors = {'L1_attn_W1': 8.0, 'L1_ffn_W1': 2.98}
    for name, (base, spread) in spreads.items():
        noise = np.random.default_rng([zlib.crc32(name.encode()), seed]).standard_normal(out[name].shape)
        drawn = base * np.exp(spread * noise) if base else spread * noise
        out[name] = jnp.asarray(drawn.astype(out[name].dtype))
    for name, factor in factors.items():
        out[name] = (out[name] * factor).astype(out[name].dtype)
    return out
```

```python
from contextlib import ExitStack

import concourse.bass as bass
from concourse import mybir

F32 = mybir.dt.float32
F32R = mybir.dt.float32r
BF16 = mybir.dt.bfloat16
U32 = mybir.dt.uint32
ALU = mybir.AluOpType
ACT = mybir.ActivationFunctionType
AX = mybir.AxisListType
ds = bass.ds

P = 128
B, S, D = 16, 256, 128
N = B * S
NT = N // P
TB = S // P
EPS = 1e-5
H0, HD0 = 16, 8
H1, HD1 = 8, 16
E = 8
FH0 = 256
CAP = 256
SLOTS = E * CAP
FH1 = 512
FC = FH1 // P
TOP_P = 0.8
NEG = -1e30
GH = 4
G0 = B * H0 // GH
G1 = B * H1 // GH
MIDDLE = 5
GPB0 = H0 // GH
RING = 8
PAIRS = RING // 2
R0 = 9 * HD0
R1 = 8 * HD1
BLK = 512
NB = N // BLK
TPB = BLK // P
PROJ1 = 2 * P + E


UNITS = E * FC
AHEAD = 3


def build(nc, a, out):
    ctx = ExitStack()
    with ctx:
        def sb(name, shape, dt=F32, where=ctx):
            return where.enter_context(nc.sbuf_tensor(name, shape, dt))

        def sem(name):
            return ctx.enter_context(nc.semaphore(name))

        def dram(name, shape, dt=F32):
            return nc.dram_tensor(name, shape, dt, kind="Internal").ap()

        q_parts = dram("q_parts", [B, 3, P, S], BF16)
        k_parts = dram("k_parts", [B, 3, P, S], BF16)

        o_rows = dram("o_rows", [B, GPB0, P, S])
        o_heads = o_rows.rearrange("b k (g r) t -> b (k g) r t", r=32)

        x = sb("x", [P, NT, D])
        ident = sb("ident", [P, P])
        upto = sb("upto", [P, P])
        x_slots = dram("x_slots", [SLOTS, D])
        gate_rows = dram("gate_rows", [E, N])
        y_slots = dram("y_slots", [SLOTS + P, D])
        ident_h = sb("ident_h", [P, P], BF16)
        mask_qk = sb("mask_qk", [P, P], BF16)
        mask_kq = sb("mask_kq", [P, P], BF16)
        before = sb("before", [P, P], BF16)
        ones_h = sb("ones_h", [P, P], BF16)
        moments = sb("moments", [P, NT, 2])
        var = sb("var", [P, NT])
        std = sb("std", [P, NT])
        rstd = sb("rstd", [P, NT])

        w1_raw = sb("w1_raw", [P, 2 * P + PROJ1])
        w1_qk = [sb(f"w1_qk_{i}", [P, 2 * P]) for i in ("hi", "lo")]
        w1_p = [sb(f"w1_p_{i}", [P, PROJ1]) for i in ("hi", "lo")]
        w2_a = sb("w2_a", [P, D])
        gn_w = sb("gn_w", [P, D])
        gn_b = sb("gn_b", [P, D])
        rb1 = sb("rb1", [P, E])
        rank_e = sb("rank_e", [P, 2, E])
        earlier_e = sb("earlier_e", [P, E, E])
        rb1_s = sb("rb1_s", [P, H1])
        gates = sb("gates", [P, NT, E])
        pick_p = sb("pick_p", [P, 2, NT])

        era = ExitStack()
        xn = sb("xn", [P, NT, D], where=era)
        v_all = sb("v_all", [P, NT, H0, HD0], where=era)
        logits0 = sb("logits0", [P, NT, E], where=era)
        w_q = sb("w_q", [P, P], where=era)
        w_k = sb("w_k", [P, P], where=era)
        w_vr = sb("w_vr", [P, D + E], where=era)
        rb0 = sb("rb0", [P, E], where=era)
        w_o = sb("w_o", [P, D], where=era)
        zero = sb("zero", [P, D], where=era)
        w_up = sb("w_up", [P, E, 2, FH0], where=era)
        w_dn = sb("w_dn", [P, E, 2, D], where=era)
        picked = sb("picked", [P, 2, NT, E], where=era)
        r_a = sb("r_a", [P, 2, NT, E], where=era)
        r_b = sb("r_b", [P, 2, NT, E], where=era)
        r_s = sb("r_s", [P, 8, 2, NT], where=era)
        rank = sb("rank", [P, NT, E], where=era)
        chosen = sb("chosen", [P, NT, E], BF16, where=era)
        ones_t = sb("ones_t", [P, NT], where=era)
        slot_in = sb("slot_in", [P, 2, NT], U32, where=era)
        slot_out = sb("slot_out", [P, 2, NT], U32, where=era)
        y_more = sb("y_more", [P, NT, D], where=era)
        xg = y_more[:, 0:SLOTS // P, :]
        xgT = y_more[:, SLOTS // P:NT, :].rearrange("p t c -> p (t c)")
        y_sb = xg
        act_s = sb("act_s", [P, 2, FH0], where=era)
        act_t = sb("act_t", [P, 2, FH0], where=era)
        act_g = sb("act_g", [P, 2, 2, FH0], where=era)
        wv_all = sb("wv_all", [P, N], where=era)
        den_all = sb("den_all", [P, N], where=era)
        v_ring = sb("v_ring", [P, 2, TB, H0, 2 * HD0], where=era)
        m8 = sb("m8", [P, 2, GH, TB], where=era)
        m_neg = sb("m_neg", [2 * GH, 4, P], BF16, where=era)
        q_st = sb("q_st", [P, PAIRS, 2 * GH, S], BF16, where=era)
        k_st = sb("k_st", [P, PAIRS, 2 * GH, S], BF16, where=era)
        with ExitStack() as part:
            tables = sb("tables", [P, 3, P], where=part)
            stats = sb("stats", [P, NT, 6], where=part)
            xn_ring = sb("xn_ring", [P, 2, TB, D], where=part)
            xT = sb("xT", [P, 2, S], where=part)
            qp = sb("qp", [P, 2, 3, S], BF16, where=part)
            kp = sb("kp", [P, 2, 3, S], BF16, where=part)
            q_rest = sb("q_rest", [P, 2, S], where=part)
            k_rest = sb("k_rest", [P, 2, S], where=part)
        with ExitStack() as part:
            o_ring = sb("o_ring", [P, 4, S], where=part)
            probs = sb("probs", [P, 2, 3, 512], where=part)
        with ExitStack() as part:
            wvn = sb("wvn", [P, 2, BLK], where=part)
        era.close()

        era = ExitStack()
        xh = sb("xh", [P, N], where=era)
        xl = sb("xl", [P, N], where=era)
        logits1 = sb("logits1", [P, NT, E], where=era)
        gT = sb("gT", [P, 2, P], where=era)
        with ExitStack() as part:
            gam = sb("gam", [P, 2, S], where=part)
            v1 = sb("v1", [P, NT, H1, HD1], where=part)
            sg = sb("sg", [P, NT, D], where=part)
            ret = sb("ret", [P, NT, D], where=part)
            with ExitStack() as sub:
                stats1 = sb("stats1", [P, NT, 6], where=sub)
                xn1_ring = sb("xn1_ring", [P, 2, TB, D], where=sub)
                xr_h = sb("xr_h", [P, 2, S], where=sub)
                xr_l = sb("xr_l", [P, 2, S], where=sub)
                q1_s = sb("q1_s", [P, 2, S], where=sub)
                k1_s = sb("k1_s", [P, 2, S], where=sub)
                q1_rest = sb("q1_rest", [P, 2, S], where=sub)
                k1_rest = sb("k1_rest", [P, 2, S], where=sub)
                q1_p = sb("q1_p", [P, 2, 3, S], BF16, where=sub)
                k1_p = sb("k1_p", [P, 2, 3, S], BF16, where=sub)
                sig1 = sb("sig1", [P, 2, TB, D], where=sub)
            with ExitStack() as sub:
                q1_st = sb("q1_st", [P, PAIRS, H1, S], BF16, where=sub)
                k1_st = sb("k1_st", [P, PAIRS, H1, S], BF16, where=sub)
                sc = sb("sc", [P, 2, 3, 512], where=sub)
                o1_ring = sb("o1_ring", [P, 2, S], where=sub)
                v1_ring = sb("v1_ring", [P, 2, TB, H1, HD1], where=sub)
            with ExitStack() as sub:
                sq = sb("sq", [P, 2, BLK], where=sub)
                ss1 = sb("ss1", [P, NT, H1], where=sub)
                sd1 = sb("sd1", [P, NT, H1], where=sub)
                rs1 = sb("rs1", [P, NT, H1], where=sub)
                z = sb("z", [P, 2, BLK], where=sub)
                zT = sb("zT", [P, 2, BLK], where=sub)
                p1 = sb("p1", [P, NT, E], where=sub)
                p1_s = sb("p1_s", [P, 4, NT], where=sub)
                p1_x = sb("p1_x", [P, 3, NT, E], where=sub)
                ord_a = sb("ord_a", [P, NT, E, E], where=sub)
                ord_b = sb("ord_b", [P, NT, E, E], where=sub)
        with ExitStack() as part:
            w_raw = sb("w_raw", [P, 2, 2, FH1], where=part)
            w1_h = sb("w1_h", [P, E, FH1], where=part)
            w1_l = sb("w1_l", [P, E, FH1], where=part)
            w2_h = sb("w2_h", [P, E, FH1], where=part)
            w2_l = sb("w2_l", [P, E, FH1], where=part)
            b1 = sb("b1", [P, UNITS], where=part)
            b2 = sb("b2", [P, E], where=part)
            f = sb("f", [P, 4, BLK], where=part)
            f_h = sb("f_h", [P, 4, BLK], where=part)
            f_l = sb("f_l", [P, 4, BLK], where=part)
            gate_b = sb("gate_b", [P, E, BLK], where=part)
            yt = sb("yt", [P, 2, BLK], where=part)
            acc = sb("acc", [P, BLK], where=part)
        era.close()

        ps = ctx.enter_context(nc.psum_tensor("ps", [P, 8, 512], F32))

        x_in = sem("x_in")
        w_in = sem("w_in")
        zeroed = sem("zeroed")
        consts_ready = sem("consts_ready")
        stats_done = sem("stats_done")
        moments_done = sem("moments_done")
        var_ready = sem("var_ready")
        std_ready = sem("std_ready")
        rstd_ready = sem("rstd_ready")
        xn_ready = sem("xn_ready")
        xn_kept = [sem(f"xn_kept{u}") for u in range(2)]
        tr_done = sem("tr_done")
        xT_done = sem("xT_done")
        q_mm, k_mm, v_mm = sem("q_mm"), sem("k_mm"), sem("v_mm")
        q_hi, k_hi = sem("q_hi"), sem("k_hi")
        q_res, k_res = sem("q_res"), sem("k_res")
        q_mid, k_mid = sem("q_mid"), sem("k_mid")
        q_lo, k_lo = sem("q_lo"), sem("k_lo")
        v_put, lg_put = sem("v_put"), sem("lg_put")
        q_stored = [sem(f"q_stored{u}") for u in range(2)]
        k_stored = [sem(f"k_stored{u}") for u in range(2)]
        stack_in = [sem(f"stack_in{r}") for r in range(PAIRS)]
        s_done, max_done, mtr_done, mneg_done = sem("s_done"), sem("max_done"), sem("mtr_done"), sem("mneg_done")
        mrow_in = [sem(f"mrow_in{r}") for r in range(4)]
        st_done, exp_done, pv_done, o_evac = sem("st_done"), sem("exp_done"), sem("pv_done"), sem("o_evac")
        o_moved = [sem(f"o_moved{r}") for r in range(4)]
        v_here = sem("v_here")
        wv_in = sem("wv_in")
        rden_done = sem("rden_done")
        wvn_done, wo_mm, x1_done = sem("wvn_done"), sem("wo_mm"), sem("x1_done")
        out_done = sem("out_done")
        slots_zero, scattered, xg_in, xgt_mm, xgt_put = (sem(n) for n in ("slots_zero", "scattered", "xg_in", "xgt_mm", "xgt_put"))
        up_mm, sig_done, gate_s, gated, down_mm, y_put, y_stored = (sem(n) for n in ("up_mm", "sig_done", "gate_s", "gated", "down_mm", "y_put", "y_stored"))
        routed, counted, indexed, pick_d, pick_e, gathered = (sem(n) for n in ("routed", "counted", "indexed", "pick_d", "pick_e", "gathered"))
        x1_attn, x1_half = sem("x1_attn"), sem("x1_half")

        xn1_ready, t1_done, xh_put, xl_put = (sem(n) for n in ("xn1_ready", "t1_done", "xh_put", "xl_put"))
        x_kept = [sem(f"x_kept{u}") for u in range(2)]
        q1_mm, k1_mm, p1_mm, q1_scaled, k1_scaled = (sem(n) for n in ("q1_mm", "k1_mm", "p1_mm", "q1_scaled", "k1_scaled"))
        q1_hi, k1_hi, q1_res, k1_res, q1_mid, k1_mid, q1_lo, k1_lo = (
            sem(n) for n in ("q1_hi", "k1_hi", "q1_res", "k1_res", "q1_mid", "k1_mid", "q1_lo", "k1_lo"))
        q1_stored = [sem(f"q1_stored{u}") for u in range(2)]
        k1_stored = [sem(f"k1_stored{u}") for u in range(2)]
        v1_put, sg_put, lg1_put, sg_done = (sem(n) for n in ("v1_put", "sg_put", "lg1_put", "sg_done"))
        stack1_in = [sem(f"stack1_in{r}") for r in range(PAIRS)]
        s1_done, masked, copied, v1_here, pv1_done, o1_evac, turned1, ret_put = (
            sem(n) for n in ("s1_done", "masked", "copied", "v1_here", "pv1_done", "o1_evac", "turned1", "ret_put"))
        sq_done, ss_done, sd_done, z_b, z_done, zt_mm, zt_put, w2_mm, x2_attn = (
            sem(n) for n in ("sq_done", "ss_done", "sd_done", "z_b", "z_done", "zt_mm", "zt_put", "w2_mm", "x2_attn"))
        gates_done, gt_mm, gt_put, gates_out = (
            sem(n) for n in ("gates_done", "gt_mm", "gt_put", "gates_out"))
        gate_in = [sem(f"gate_in{e}") for e in range(E)]
        raw_in = [sem(f"raw_in{u}") for u in range(2)]
        w1_hi, w1_lo, w2_hi, w2_lo = (sem(n) for n in ("w1_hi", "w1_lo", "w2_hi", "w2_lo"))
        h_mm, f_done, f_hi, y_mm, yv, summed, acc_turned, x2_done = (
            sem(n) for n in ("h_mm", "f_done", "f_hi", "y_mm", "yv", "summed", "acc_turned", "x2_done"))
        f_lo = [sem("f_lo_even"), sem("f_lo_odd")]

        CREDIT = 2
        credits = [q_res, k_res, q_lo, k_lo, v_mm, lg_put, tr_done,
                   xl_put, q1_scaled, k1_scaled, p1_mm, q1_res, k1_res, q1_lo, k1_lo, sg_done]
        singles = [lg1_put]

        block = ctx.enter_context(nc.Block())

        def num(g): return g[0] * RING + g[1]
        def div(g, by): return g[0] * (RING // by) + g[1] // by
        def plus(g, k): return g[0], g[1] + k
        def at(g, size): return g[1] % size

        def known(g): return isinstance(g[0], int)

        def run_slots(eng, total, slot, middle=None):
            for n in range(RING):
                slot((0, n))
            ends = [1, total // RING - 1] if middle is None else [1, MIDDLE, total // RING - 1]
            for first, end in zip(ends, ends[1:]):
                if first != 1:
                    middle()
                with eng.Fori(first, end) as i:
                    for r in range(RING):
                        slot((i, r))
            for n in range(total - RING, total):
                slot((0, n))

        def past(g, n):
            return not known(g) or num(g) >= n

        def within(g, total):
            return not known(g) or num(g) < total

        def known_block(j): return j if isinstance(j, int) else None

        def run_blocks(eng, body):
            body(0)
            with eng.Fori(1, NB - 1) as j:
                body(j)
            body(NB - 1)

        def r32(ap):
            return ap.bitcast(F32R)

        def run_pairs(eng, step):
            with eng.Fori(0, B // 2 - 1) as ii:
                for u in range(2):
                    step(ii * 2 + u, u)
            for u in range(2):
                step(B - 2 + u, u)

        def more(b, k):
            return not isinstance(b, int) or b + k < B

        def ps_t1(u): return ps[:, u, 0:S]
        def ps_q1(u): return ps[:, 2 + u, 0:S]
        def ps_k1(u): return ps[:, 4 + u, 0:S]
        def ps_p1(t): return ps[:, 6 + t, 0:PROJ1]
        p1_both = ps[:, 6:8, 0:PROJ1]
        def ps_sc(u, c): return ps[:, 3 * u + c, :]
        ps_o1 = ps[:, 6, 0:S]
        ps_r1 = ps[:, 7, 0:S]

        def ps_t(u): return ps[:, 4 * u, 0:S]
        def ps_q(u): return ps[:, 4 * u + 1, 0:S]
        def ps_k(u): return ps[:, 4 * u + 2, 0:S]
        def ps_v(u): return ps[:, 4 * u + 3, 0:TB * (D + E)].rearrange("p (t c) -> p t c", t=TB)
        def ps_s(c): return ps[:, c, :]
        def ps_st(c): return ps[:, 3 + c, :]
        ps_o = ps[:, 6, 0:S]
        ps_m = ps[0:2 * GH, 7, 0:P]

        q_rows = q_parts.rearrange("b i (d a h) t -> b (i d) a (h t)", d=HD0, a=2)
        k_rows = k_parts.rearrange("b i (d a h) t -> b i d a (h t)", d=HD0, a=2)

        @block.sync
        def _(sp):
            for c in range(4):
                sp.dma_start(x[:, c * 8:c * 8 + 8, :], a["h"][:, c * 8:c * 8 + 8, :]).then_inc(x_in, 16)
            with sp.Fori(0, B // 2) as ii:
                for u in range(2):
                    b = ii * 2 + u
                    sp.wait_ge(xn_ready, (b + 1) * TB)
                    sp.dma_start(xn[:, ds(b * TB, TB), :], xn_ring[:, u, :, :]).then_inc(xn_kept[u], 16)
                    sp.wait_ge(q_lo, b + 1 + CREDIT)
                    sp.dma_start(q_parts[ds(b, 1)].rearrange("o i p t -> p (o i) t"), qp[:, u, :, :])\
                      .then_inc(q_stored[u], 16)
                    sp.wait_ge(k_lo, b + 1 + CREDIT)
                    sp.dma_start(k_parts[ds(b, 1)].rearrange("o i p t -> p (o i) t"), kp[:, u, :, :])\
                      .then_inc(k_stored[u], 16)
            for u in range(2):
                sp.wait_ge(q_stored[u], 16 * (B // 2 + 1))
                sp.wait_ge(k_stored[u], 16 * (B // 2 + 1))
                sp.wait_ge(xn_kept[u], 16 * (B // 2 + 1))

            def load_pair(b, half, r):
                src = q_rows[ds(b, 1), :, half, :].rearrange("o r c -> (o r) c")
                sp.dma_start(q_st[0:R0, r, :, :].rearrange("p h t -> p (h t)"),
                             src.unsqueeze(0).broadcast_to([3, 3 * HD0, 2 * GH * S])).then_inc(stack_in[r], 16)
                for j in range(3):
                    src = k_rows[ds(b, 1), j, :, half, :].rearrange("o d c -> (o d) c")
                    sp.dma_start(k_st[j * 3 * HD0:(j + 1) * 3 * HD0, r, :, :].rearrange("p h t -> p (h t)"),
                                 src.unsqueeze(0).broadcast_to([3, HD0, 2 * GH * S])).then_inc(stack_in[r], 16)

            def move_max(g):
                r = at(g, RING)
                sp.wait_ge(mneg_done, num(g) + 1)
                sp.dma_start(q_st[R0:R0 + 1, r // 2, (r % 2) * GH:(r % 2) * GH + GH, :]
                             .rearrange("o h (t q) -> o (h t) q", t=TB),
                             m_neg[:, r % 4, :]).then_inc(mrow_in[r % 4], 16)

            def move_out(g):
                sp.wait_ge(o_evac, num(g) + 1)
                sp.dma_start(o_rows[ds(div(g, GPB0), 1), at(g, GPB0)].rearrange("o p t -> (o p) t"), o_ring[:, at(g, 4), :])\
                  .then_inc(o_moved[at(g, 4)], 16)

            def bring_back(b):
                for r in range(4):
                    sp.wait_ge(o_moved[r], b * 16 + 16)
                for part, dst in ((0, wv_all), (1, den_all)):
                    sp.dma_start(dst[:, ds(b * S, S)],
                                 o_heads[ds(b, 1), :, part * HD0:(part + 1) * HD0, :].rearrange("o h d t -> (o h) d t"))\
                      .then_inc(wv_in, 16)

            sp.wait_ge(zeroed, 6)
            for p in range(PAIRS):
                load_pair(p // 2, p % 2, p)
            for n in range(2):
                move_max((0, n))

            def slot(g):
                if within(plus(g, 2), G0):
                    move_max(plus(g, 2))
                if past(g, 1):
                    move_out(plus(g, -1))
                if g[1] % GPB0 == 2 and past(g, 6):
                    bring_back(div(plus(g, -6), GPB0))
                if g[1] % 2 == 1 and within(plus(g, 7), G0):
                    far = plus(g, 7)
                    sp.wait_ge(st_done, num(g) + 1)
                    load_pair(div(far, GPB0), at(far, GPB0) // 2, at(far, RING) // 2)
            def middle():
                sp.wait_ge(scattered, 16 * 2 * NT)
                sp.dma_start(xg, x_slots.rearrange("(c p) d -> p c d", p=P)).then_inc(xg_in, 16)
                sp.wait_ge(y_put, E)
                sp.dma_start(y_slots[0:SLOTS].rearrange("(c p) d -> p c d", p=P), y_sb).then_inc(y_stored, 16)
            run_slots(sp, G0, slot, middle)
            move_out((0, G0 - 1))
            bring_back(B - 1)

            sp.wait_ge(x1_done, NB)
            sp.dma_start(gam[:, :, :], a["gam"]).then_inc(w_in, 16)

            def keep_parts(b, u):
                sp.wait_ge(xl_put, b + 1 + CREDIT)
                for src, dst in ((xr_h, xh), (xr_l, xl)):
                    sp.dma_start(dst[:, ds(b * S, S)], src[:, u, :]).then_inc(x_kept[u], 16)
                for lo, src, dst, done in ((q1_lo, q1_p, q_parts, q1_stored), (k1_lo, k1_p, k_parts, k1_stored)):
                    sp.wait_ge(lo, b + 1 + CREDIT)
                    sp.dma_start(dst[ds(b, 1)].rearrange("o i p t -> p (o i) t"), src[:, u, :, :]).then_inc(done[u], 16)
            run_pairs(sp, keep_parts)
            for u in range(2):
                sp.wait_ge(q1_stored[u], 16 * (B // 2 + 1))
                sp.wait_ge(k1_stored[u], 16 * (B // 2 + 1))
                sp.wait_ge(x_kept[u], 32 * (B // 2 + 1))
            sp.wait_ge(sg_done, B + CREDIT)
            q1_rows = q_parts.rearrange("b i (d h) t -> b (i d) (h t)", d=HD1)
            k1_rows = k_parts.rearrange("b i (d h) t -> b i d (h t)", d=HD1)

            def load_sequence(b, r):
                src = q1_rows[ds(b, 1)].rearrange("o r c -> (o r) c")
                rows = 3 * HD1
                sp.dma_start(q1_st[0:2 * rows, r, :, :].rearrange("p h t -> p (h t)"),
                             src.unsqueeze(0).broadcast_to([2, rows, H1 * S])).then_inc(stack1_in[r], 16)
                sp.dma_start(q1_st[2 * rows:R1, r, :, :].rearrange("p h t -> p (h t)"), src[0:R1 - 2 * rows]).then_inc(stack1_in[r], 16)
                for j in range(3):
                    src = k1_rows[ds(b, 1), j].rearrange("o d c -> (o d) c")
                    n = 3 if j < 2 else 2
                    sp.dma_start(k1_st[j * rows:j * rows + n * HD1, r, :, :].rearrange("p h t -> p (h t)"),
                                 src.unsqueeze(0).broadcast_to([n, HD1, H1 * S])).then_inc(stack1_in[r], 16)
            for b in range(PAIRS):
                load_sequence(b, b)

            def slot(g):
                if g[1] % 2 == 1 and within(plus(g, 7), G1):
                    far = plus(g, 7)
                    sp.wait_ge(s1_done, num(g) + 1)
                    load_sequence(div(far, 2), at(far, RING) // 2)
            run_slots(sp, G1, slot)

            sp.wait_ge(gt_put, 2)
            for c in range(2):
                sp.dma_start(gate_rows[:, c * N // 2:(c + 1) * N // 2].rearrange("e (t k) -> t e k", k=P), gT[:, c, :])\
                  .then_inc(gates_out, 16)
            sp.wait_ge(gates_out, 32)
            sp.wait_ge(x2_attn, NB)

            def load_raw(e):
                sp.dma_start(w_raw[:, e % 2, 0, :], a["w1_e"][:, e, :]).then_inc(raw_in[e % 2], 16)
                sp.dma_start(w_raw[:, e % 2, 1, :], a["w2_e"][:, e, :]).then_inc(raw_in[e % 2], 16)

            def load_gate(j, e):
                sp.dma_start(gate_b[:, e, :], gate_rows[e:e + 1, ds(j * BLK, BLK)].broadcast_to([P, BLK])).then_inc(gate_in[e], 16)

            def store(j):
                sp.wait_ge(x2_done, j + 1)
                sp.dma_start(out[ds(j * BLK, BLK)].rearrange("(t p) d -> p t d", p=P), x[:, ds(j * TPB, TPB), :]).then_inc(out_done, 16)
            load_raw(0)
            load_raw(1)
            sp.dma_start(b1[:, :], a["b1"]).then_inc(w_in, 16)
            sp.dma_start(b2[:, :], a["b2"]).then_inc(w_in, 16)
            for e in range(E):
                load_gate(0, e)

            def body(j):
                for e in range(-2, E):
                    if known_block(j) == 0 and e + 4 < E:
                        sp.wait_ge(w1_lo, e + 3)
                        sp.wait_ge(w2_lo, e + 3)
                        load_raw(e + 4)
                    if e < 0:
                        continue
                    if known_block(j) != NB - 1:
                        sp.wait_ge(yv, j * E + e + 1)
                        load_gate(j + 1, e)
                    if e == 2 and known_block(j) != 0:
                        store(j - 1)
            run_blocks(sp, body)
            store(NB - 1)
            sp.wait_ge(out_done, 16 * NB)

        @block.gpsimd
        def _(pool):
            for s in credits:
                pool.sem_inc(s, CREDIT)
            for s in singles:
                pool.sem_inc(s, 1)
            for u in range(2):
                pool.sem_inc(q_stored[u], 16)
                pool.sem_inc(k_stored[u], 16)
                pool.sem_inc(xn_kept[u], 16)
                pool.sem_inc(q1_stored[u], 16)
                pool.sem_inc(k1_stored[u], 16)
                pool.sem_inc(x_kept[u], 32)
            nc.gpsimd.memset(v_ring[:, :, :, :, :], 1.0).then_inc(zeroed, 1)
            nc.gpsimd.memset(ones_h[:, :], 1.0).then_inc(zeroed, 1)
            nc.gpsimd.memset(zero[:, :], 0.0).then_inc(zeroed, 1)
            nc.gpsimd.memset(ones_t[:, :], 1.0).then_inc(zeroed, 1)
            pool.wait_ge(zeroed, 4)
            nc.gpsimd.memset(q_st[64:P, :, :, :], 0.0).then_inc(zeroed, 1)
            nc.gpsimd.memset(k_st[64:P, :, :, :], 1.0).then_inc(zeroed, 1)
            pool.wait_ge(zeroed, 6)
            pool.dma_start(x_slots.rearrange("(c p) d -> p c d", p=P),
                           zero[:, :].unsqueeze(1).broadcast_to([P, SLOTS // P, D])).then_inc(slots_zero, 16)
            pool.dma_start(y_slots[SLOTS:SLOTS + P], zero[:, :]).then_inc(slots_zero, 16)
            with pool.Fori(0, B // 2) as ii:
                for u in range(2):
                    b = ii * 2 + u
                    pool.wait_ge(q_mid, b + 1)
                    nc.gpsimd.tensor_tensor(qp[:, u, 2, :], q_rest[:, u, :], qp[:, u, 1, :], ALU.subtract).then_inc(q_lo, 1)
                    pool.wait_ge(k_mid, b + 1)
                    nc.gpsimd.tensor_tensor(kp[:, u, 2, :], k_rest[:, u, :], kp[:, u, 1, :], ALU.subtract).then_inc(k_lo, 1)

            def put_values(b, u):
                for t in range(TB):
                    last = nc.gpsimd.tensor_copy(v_ring[:, u, t, :, 0:HD0],
                                                 v_all[:, ds(b * TB + t, 1), :, :].rearrange("p o h d -> p (o h) d"))
                last.then_inc(v_here, 1)
            pool.wait_ge(v_put, B)
            for u in range(2):
                put_values(u, u)

            def next_values(first, end):
                with pool.Fori(first, end) as ii:
                    for u in range(2):
                        pool.wait_ge(pv_done, ii * 2 * GPB0 + (u - 1) * GPB0)
                        put_values(ii * 2 + u, u)
            pool.wait_ge(indexed, 2)
            pool.wait_ge(slots_zero, 32)
            for u in range(2):
                pool.wait_ge(xn_kept[u], 16 * (B // 2 + 1))
            scatters = [(t, c) for t in range(NT) for c in range(2)]
            gathers = [(t, c) for t in range(NT) for c in range(2)]

            def scatter(some):
                for t, c in some:
                    pool.indirect_dma_start(out=x_slots, out_offset=bass.IndirectOffsetOnAxis(ap=slot_in[:, c, t:t + 1], axis=0),
                                            in_=xn[:, t, :], in_offset=None, bounds_check=SLOTS - 1, oob_is_err=False)\
                        .then_inc(scattered, 16)
            half = MIDDLE * RING // GPB0 // 2 - 1
            for k in range(1, half):
                scatter(scatters[(k - 1) * 2 * NT // (half - 1):k * 2 * NT // (half - 1)])
                next_values(k, k + 1)
            next_values(half, MIDDLE * RING // GPB0 // 2 + 1)
            pool.wait_ge(y_stored, 16)
            pool.wait_ge(scattered, 16 * 2 * NT)
            for k, (t, c) in enumerate(gathers):
                pool.indirect_dma_start(out=(xn, y_more)[c][:, t, :], out_offset=None, in_=y_slots,
                                        in_offset=bass.IndirectOffsetOnAxis(ap=slot_out[:, c, t:t + 1], axis=0))\
                    .then_inc(gathered, 16)
                if k == NT:
                    next_values(MIDDLE * RING // GPB0 // 2 + 1, B // 2)

            def last_parts(b, u):
                for mid, lo, rest, part in ((q1_mid, q1_lo, q1_rest, q1_p), (k1_mid, k1_lo, k1_rest, k1_p)):
                    pool.wait_ge(mid, b + 1)
                    nc.gpsimd.tensor_tensor(part[:, u, 2, :], rest[:, u, :], part[:, u, 1, :], ALU.subtract).then_inc(lo, 1)
                pool.wait_ge(sg_put, b + 1)
                nc.gpsimd.tensor_tensor(sg[:, ds(b * TB, TB), :], sg[:, ds(b * TB, TB), :],
                                        gn_b[:, :].unsqueeze(1).broadcast_to([P, TB, D]), ALU.add).then_inc(sg_done, 1)
            run_pairs(pool, last_parts)

            def values(b, u):
                nc.gpsimd.tensor_copy(v1_ring[:, u, :, :, :], v1[:, ds(b * TB, TB), :, :]).then_inc(v1_here, 1)
            pool.wait_ge(v1_put, 2 * B)
            pool.wait_ge(sg_done, B + CREDIT)
            for u in range(2):
                pool.wait_ge(q1_stored[u], 16 * (B // 2 + 1))
                pool.wait_ge(k1_stored[u], 16 * (B // 2 + 1))
                pool.wait_ge(x_kept[u], 32 * (B // 2 + 1))
            for u in range(2):
                values(u, u)
            with pool.Fori(1, B // 2) as ii:
                for u in range(2):
                    pool.wait_ge(pv1_done, ii * 4 + 2 * u - 2)
                    values(ii * 2 + u, u)

            pool.wait_ge(ret_put, G1)
            for j in range(NB):
                tiles = ret[:, j * TPB:(j + 1) * TPB, :].rearrange("p t c -> p (t c)")
                if j >= 2:
                    pool.wait_ge(ss_done, j - 1)
                nc.gpsimd.tensor_tensor(sq[:, j % 2, :], tiles, tiles, ALU.mult).then_inc(sq_done, 1)
            for j in range(NB):
                pool.wait_ge(z_b, j + 1)
                nc.gpsimd.tensor_tensor(z[:, j % 2, :], z[:, j % 2, :], sg[:, j * TPB:(j + 1) * TPB, :].rearrange("p t c -> p (t c)"),
                                        ALU.add).then_inc(z_done, 1)

            def low_w2(e):
                pool.wait_ge(w2_hi, e + 1)
                nc.gpsimd.tensor_tensor(r32(w2_l[:, e, :]), w_raw[:, e % 2, 1, :], w2_h[:, e, :], ALU.subtract).then_inc(w2_lo, 1)

            def add_expert(j, e):
                pool.wait_ge(yv, j * E + e + 1)
                if e:
                    if e > 1:
                        pool.wait_ge(summed, j * (E - 1) + e - 1)
                    nc.gpsimd.tensor_tensor(acc[:, :], acc[:, :], yt[:, e % 2, :], ALU.add).then_inc(summed, 1)
            low_w2(0)
            low_w2(1)

            def body(j):
                for m in range(1, UNITS, 2):
                    if known_block(j) == 0 and m % FC == 1 and m // FC + 2 < E:
                        low_w2(m // FC + 2)
                    n = j * UNITS + m
                    pool.wait_ge(f_hi, n + 1)
                    if known_block(j) != 0 or m >= 4:
                        pool.wait_ge(y_mm, n - 3)
                    nc.gpsimd.tensor_tensor(r32(f_l[:, m % 4, :]), f[:, m % 4, :], f_h[:, m % 4, :], ALU.subtract).then_inc(f_lo[1], 1)
                    if m % FC == 3:
                        if m >= 7:
                            add_expert(j, (m - 7) // FC)
                        elif known_block(j) != 0:
                            add_expert(j - 1, E - 1)
            run_blocks(pool, body)
            add_expert(NB - 1, E - 1)

        @block.scalar
        def _(act):
            act.dma_start(ident[:, :], a["ident"]).then_inc(w_in, 16)
            act.dma_start(tables[:, :, :], a["tables"]).then_inc(w_in, 16)
            for dst, name in ((w_q[:, :], "w_q"), (w_k[:, :], "w_k"), (w_vr[:, :], "w_vr"), (w_o[:, :], "w_o"),
                              (rb0[:, :], "rb0"), (rank_e[:, :, :], "rank_e"), (earlier_e[:, :, :], "earlier_e"),
                              (w1_raw[:, :], "w1_raw"), (upto[:, :], "upto"), (w2_a[:, :], "w2_a"), (gn_w[:, :], "gn_w"), (gn_b[:, :], "gn_b"),
                              (rb1[:, :], "rb1"), (w_up[:, :, :, :], "w_up"), (w_dn[:, :, :, :], "w_dn")):
                act.dma_start(dst, a[name]).then_inc(w_in, 16)
            act.wait_ge(var_ready, 1)
            nc.scalar.activation(std[:, :], var[:, :], ACT.Sqrt).then_inc(std_ready, 1)
            with act.Fori(0, B // 2) as ii:
                for u in range(2):
                    b = ii * 2 + u
                    act.wait_ge(tr_done, b + 1 + CREDIT)
                    act.wait_ge(v_mm, b + 1)
                    nc.scalar.activation(xT[:, u, :], ps_t(u), ACT.Copy).then_inc(xT_done, 1)
                    act.wait_ge(q_mm, b + 1)
                    act.wait_ge(q_stored[u], ii * 16 + 16)
                    nc.scalar.activation(qp[:, u, 0, :], ps_q(u), ACT.Copy).then_inc(q_hi, 1)
                    act.wait_ge(k_mm, b + 1)
                    act.wait_ge(k_stored[u], ii * 16 + 16)
                    nc.scalar.activation(kp[:, u, 0, :], ps_k(u), ACT.Copy).then_inc(k_hi, 1)
                    act.wait_ge(v_mm, b + 1 + CREDIT)
                    nc.scalar.activation(v_all[:, ds(b * TB, TB), :, :].rearrange("p t h d -> p t (h d)"),
                                         ps_v(u)[:, :, 0:D], ACT.Copy).then_inc(v_put, 1)

            def negate_max(g):
                act.wait_ge(mtr_done, num(g) + 1)
                if past(g, 4):
                    act.wait_ge(mrow_in[at(g, 4)], div(g, 4) * 16)
                nc.scalar.activation(m_neg[:, at(g, 4), :], ps_m, ACT.Copy, scale=-1.0).then_inc(mneg_done, 1)

            def evacuate(g):
                act.wait_ge(pv_done, num(g) + 1)
                if past(g, 4):
                    act.wait_ge(o_moved[at(g, 4)], div(g, 4) * 16)
                nc.scalar.activation(o_ring[:, at(g, 4), :], ps_o, ACT.Copy).then_inc(o_evac, 1)

            for n in range(2):
                negate_max((0, n))

            def slot(g):
                if within(plus(g, 2), G0):
                    negate_max(plus(g, 2))
                act.wait_ge(st_done, num(g) + 1)
                if past(g, 2):
                    act.wait_ge(pv_done, num(g) - 1)
                nc.scalar.activation(probs[:, at(g, 2), :, :], ps[:, 3:6, :], ACT.Exp, scale=float(D) ** -0.5)\
                  .then_inc(exp_done, 1)
                if past(g, 1):
                    evacuate(plus(g, -1))
            def middle():
                for c in range(SLOTS // 512):
                    act.wait_ge(xgt_mm, c + 1)
                    nc.scalar.activation(xgT[:, c * 512:(c + 1) * 512], ps[:, c, :], ACT.Copy).then_inc(xgt_put, 1)
                for e in range(E):
                    act.wait_ge(up_mm, e + 1)
                    if e >= 1:
                        act.wait_ge(gate_s, e)
                    nc.scalar.activation(act_s[:, :, :].rearrange("p c t -> p (c t)"), ps[:, 2 + e % 2, :], ACT.Sigmoid)\
                      .then_inc(sig_done, 1)
                    if e >= 1:
                        put_down(e - 1)
                put_down(E - 1)
                act.wait_ge(pick_d, 1)
                nc.scalar.activation(r_s[:, 1, 0, :], r_s[:, 0, 0, :], ACT.Exp).then_inc(pick_e, 1)

            def put_down(e):
                act.wait_ge(down_mm, e + 1)
                nc.scalar.activation(y_sb[:, 2 * e:2 * e + 2, :].rearrange("p c d -> p (c d)"), ps[:, 4 + e % 2, 0:2 * D], ACT.Copy)\
                  .then_inc(y_put, 1)
            run_slots(act, G0, slot, middle)
            evacuate((0, G0 - 1))

            act.wait_ge(var_ready, 2)
            nc.scalar.activation(std[:, :], var[:, :], ACT.Sqrt).then_inc(std_ready, 1)

            def high_x(b, u):
                act.wait_ge(t1_done, b + 1)
                act.wait_ge(p1_mm, b + 1)
                act.wait_ge(x_kept[u], half_of(b, u) * 32 + 32)
                nc.scalar.activation(r32(xr_h[:, u, :]), ps_t1(u), ACT.Copy).then_inc(xh_put, 1)

            def half_of(b, u):
                return b // 2 if isinstance(b, int) else halves[0] + (1 if u == 0 and halves[1] else 0)
            halves = [0, False]

            def parts(b, u, ii):
                if more(b, 1):
                    halves[:] = [ii, u == 1]
                    high_x(b + 1, 1 - u)
                for scaled, hi, src, part, stored in ((q1_scaled, q1_hi, q1_s, q1_p, q1_stored), (k1_scaled, k1_hi, k1_s, k1_p, k1_stored)):
                    act.wait_ge(scaled, b + 1 + CREDIT)
                    act.wait_ge(stored[u], ii * 16 + 16)
                    nc.scalar.activation(part[:, u, 0, :], src[:, u, :], ACT.Copy).then_inc(hi, 1)
                act.wait_ge(p1_mm, b + 1 + CREDIT)
                act.wait_ge(sg_done, b + 1)
                nc.scalar.activation(sig1[:, u, :, :], p1_both[:, :, D:2 * D], ACT.Sigmoid).then_inc(v1_put, 1)
                nc.scalar.activation(v1[:, ds(b * TB, TB), :, :].rearrange("p t h d -> p t (h d)"), p1_both[:, :, 0:D], ACT.Copy)\
                    .then_inc(v1_put, 1)
                for res, mid, rest, part in ((q1_res, q1_mid, q1_rest, q1_p), (k1_res, k1_mid, k1_rest, k1_p)):
                    act.wait_ge(res, b + 1 + CREDIT)
                    nc.scalar.activation(part[:, u, 1, :], rest[:, u, :], ACT.Copy).then_inc(mid, 1)
            high_x(0, 0)
            with act.Fori(0, B // 2 - 1) as ii:
                for u in range(2):
                    parts(ii * 2 + u, u, ii)
            for u in range(2):
                parts(B - 2 + u, u, B // 2 - 1)

            def put_heads(g):
                act.wait_ge(turned1, num(g) + 1)
                nc.scalar.activation(ret[:, ds(div(g, 2) * TB, TB), g[1] % 2 * GH * HD1:(g[1] % 2 + 1) * GH * HD1]
                                     .rearrange("p t (h d) -> p t h d", h=GH),
                                     ps_r1.rearrange("p (t h r) -> p t h r", t=TB, h=GH)[:, :, :, 0:HD1], ACT.Copy).then_inc(ret_put, 1)

            def evacuate1(g):
                act.wait_ge(pv1_done, num(g) + 1)
                if past(g, 2):
                    act.wait_ge(turned1, num(g) - 1)
                nc.scalar.activation(o1_ring[:, at(g, 2), :], ps_o1, ACT.Copy).then_inc(o1_evac, 1)
            for u in range(2):
                act.wait_ge(q1_stored[u], 16 * (B // 2 + 1))
                act.wait_ge(k1_stored[u], 16 * (B // 2 + 1))
                act.wait_ge(x_kept[u], 32 * (B // 2 + 1))
            act.wait_ge(lg1_put, B + 1)

            def slot(g):
                u = at(g, 2)
                act.wait_ge(s1_done, num(g) + 1)
                if past(g, 2):
                    act.wait_ge(pv1_done, num(g) - 1)
                nc.scalar.activation(sc[:, u, 2, :], ps_sc(u, 2), ACT.Copy).then_inc(copied, 1)
                if past(g, 1):
                    evacuate1(plus(g, -1))
                if past(g, 2):
                    put_heads(plus(g, -2))
            run_slots(act, G1, slot)
            evacuate1((0, G1 - 1))
            put_heads((0, G1 - 2))
            put_heads((0, G1 - 1))

            act.wait_ge(pick_d, 2)
            nc.scalar.activation(p1_x[:, 1, :, :], p1_x[:, 0, :, :], ACT.Exp).then_inc(pick_e, 1)
            act.wait_ge(ss_done, NB + 1)
            nc.scalar.activation(sd1[:, :, :], ss1[:, :, :], ACT.Sqrt).then_inc(sd_done, 1)
            for c in range(2):
                act.wait_ge(gt_mm, c + 1)
                nc.scalar.activation(gT[:, c, :], ps[:, 4 + c, 0:P], ACT.Copy).then_inc(gt_put, 1)
            for j in range(NB):
                act.wait_ge(zt_mm, j + 1)
                if j >= 2:
                    act.wait_ge(w2_mm, j - 1)
                nc.scalar.activation(zT[:, j % 2, :], ps[:, j % 2, :], ACT.Copy).then_inc(zt_put, 1)

            act.wait_ge(w_in, 20 * 16)
            act.wait_ge(x2_attn, NB)

            def body(j):
                for m in range(UNITS):
                    n = j * UNITS + m
                    act.wait_ge(h_mm, n + 1)
                    if known_block(j) != 0 or m >= 4:
                        act.wait_ge(f_hi, n - 3)
                        act.wait_ge(f_lo[m % 2], j * (UNITS // 2) + m // 2 - 1)
                    nc.scalar.activation(f[:, m % 4, :], ps[:, m % 4, :], ACT.Relu, bias=b1[:, m:m + 1]).then_inc(f_done, 1)
            run_blocks(act, body)

        @block.vector
        def _(dve):
            dve.wait_ge(w_in, 17 * 16)
            nc.vector.tensor_copy(ident_h[:, :], ident[:, :]).then_inc(consts_ready, 1)
            nc.vector.tensor_copy(mask_qk[:, :], tables[:, 0, :]).then_inc(consts_ready, 1)
            nc.vector.tensor_copy(mask_kq[:, :], tables[:, 1, :]).then_inc(consts_ready, 1)
            nc.vector.tensor_copy(before[:, :], tables[:, 2, :]).then_inc(consts_ready, 1)
            nc.vector.memset(ps[:, 6, :], 0.0).then_inc(consts_ready, 1)
            dve.wait_ge(x_in, 64)
            with dve.Fori(0, NT // 4) as i:
                for u in range(4):
                    nc.vector.bn_stats(stats[:, ds(i * 4 + u, 1), :].rearrange("p o c -> p (o c)"),
                                       x[:, ds(i * 4 + u, 1), :].rearrange("p o c -> p (o c)")).then_inc(stats_done, 1)
            dve.wait_ge(stats_done, NT)
            for t in range(NT):
                nc.vector.bn_aggr(moments[:, t, :], stats[:, t, :]).then_inc(moments_done, 1)
            dve.wait_ge(moments_done, NT)
            nc.vector.tensor_scalar(var[:, :], moments[:, :, 1], EPS, None, ALU.add).then_inc(var_ready, 1)
            dve.wait_ge(std_ready, 1)
            nc.vector.reciprocal(rstd[:, :], std[:, :]).then_inc(rstd_ready, 1)
            dve.wait_ge(rstd_ready, 1)
            with dve.Fori(0, B // 2) as ii:
                for v in range(2 * TB):
                    t = ii * (2 * TB) + v
                    if v % TB == 0:
                        dve.wait_ge(xn_kept[v // TB], ii * 16 + 16)
                        dve.wait_ge(tr_done, ii * 2 + v // TB + 1)
                    nc.vector.tensor_scalar(xn_ring[:, v // TB, v % TB, :],
                                            x[:, ds(t, 1), :].rearrange("p o c -> p (o c)"),
                                            moments[:, ds(t, 1), 0], rstd[:, ds(t, 1)],
                                            ALU.subtract, ALU.mult).then_inc(xn_ready, 1)
                for u in range(2):
                    b = ii * 2 + u
                    for hi, lo, part, rest, bank, res, mid in ((q_hi, q_lo, qp, q_rest, ps_q, q_res, q_mid),
                                                               (k_hi, k_lo, kp, k_rest, ps_k, k_res, k_mid)):
                        dve.wait_ge(hi, b + 1)
                        dve.wait_ge(lo, b + 1)
                        nc.vector.tensor_tensor(rest[:, u, :], bank(u), part[:, u, 0, :], ALU.subtract).then_inc(res, 1)
                        dve.wait_ge(res, b + 1 + CREDIT)
                        nc.vector.tensor_copy(part[:, u, 1, :], rest[:, u, :]).then_inc(mid, 1)
                    dve.wait_ge(v_put, b + 1)
                    nc.vector.tensor_tensor(logits0[:, ds(b * TB, TB), :], ps_v(u)[:, :, D:D + E],
                                            rb0[:, :].unsqueeze(1).broadcast_to([P, TB, E]), ALU.add).then_inc(lg_put, 1)

            step = [0]

            def then(instruction):
                step[0] += 1
                instruction.then_inc(routed, 1)
                dve.wait_ge(routed, step[0])
            by_expert = [P, NT, E]
            dve.wait_ge(lg_put, B + CREDIT)
            left = logits0
            for c in range(2):
                best = r_s[:, 2 + c, 0, :]
                then(nc.vector.tensor_reduce(best, left[:, :, :], AX.X, ALU.max))
                then(nc.vector.tensor_tensor(r_a[:, 0, :, :], left[:, :, :], best.unsqueeze(2).broadcast_to(by_expert), ALU.is_equal))
                then(nc.vector.tensor_tensor(r_a[:, 1, :, :], r_a[:, 0, :, :], rank_e[:, 1, :].unsqueeze(1).broadcast_to(by_expert), ALU.mult))
                then(nc.vector.tensor_reduce(r_s[:, 4, 0, :], r_a[:, 1, :, :], AX.X, ALU.max))
                then(nc.vector.tensor_tensor(picked[:, c, :, :], r_a[:, 1, :, :], r_s[:, 4, 0, :].unsqueeze(2).broadcast_to(by_expert), ALU.is_equal))
                if c == 0:
                    left = r_b[:, 0, :, :]
                    then(nc.vector.scalar_tensor_tensor(out=left, in0=picked[:, 0, :, :], scalar=-3e38, in1=logits0[:, :, :],
                                                        op0=ALU.mult, op1=ALU.add))
            nc.vector.tensor_tensor(chosen[:, :, :], picked[:, 0, :, :], picked[:, 1, :, :], ALU.add).then_inc(counted, 1)
            nc.vector.tensor_tensor(r_s[:, 0, 0, :], r_s[:, 3, 0, :], r_s[:, 2, 0, :], ALU.subtract).then_inc(pick_d, 1)
            dve.wait_ge(counted, 2)
            ahead = ps[:, 0, 0:NT * E].rearrange("p (t e) -> p t e", e=E)
            totals = ps[:, 0, NT * E:2 * NT * E].rearrange("p (t e) -> p t e", e=E)
            then(nc.vector.tensor_copy(r_a[:, 0, :, :], totals))
            for e in range(E):
                scan = nc.vector.tensor_tensor_scan(r_a[:, 1, :, e], ones_t[:, :], r_a[:, 0, :, e], 0.0, ALU.mult, ALU.add)
            then(scan)
            then(nc.vector.tensor_tensor(r_b[:, 1, :, :], r_a[:, 1, :, :], r_a[:, 0, :, :], ALU.subtract))
            then(nc.vector.tensor_tensor(rank[:, :, :], ahead, r_b[:, 1, :, :], ALU.add))
            for c in range(2):
                then(nc.vector.tensor_tensor(r_a[:, c, :, :], picked[:, c, :, :], rank[:, :, :], ALU.mult))
                then(nc.vector.tensor_tensor(r_b[:, c, :, :], picked[:, c, :, :], rank_e[:, 0, :].unsqueeze(1).broadcast_to(by_expert), ALU.mult))
            place, expert, full, row, keep = (r_s[:, k, :, :] for k in (3, 4, 5, 6, 7))
            then(nc.vector.tensor_reduce(place, r_a[:, :, :, :], AX.X, ALU.add))
            then(nc.vector.tensor_reduce(expert, r_b[:, :, :, :], AX.X, ALU.add))
            then(nc.vector.scalar_tensor_tensor(out=row, in0=expert, scalar=float(CAP), in1=place, op0=ALU.mult, op1=ALU.add))
            then(nc.vector.tensor_scalar(full, place, CAP - 0.5, float(2 * SLOTS), ALU.is_gt, ALU.mult))
            nc.vector.tensor_tensor(slot_in[:, :, :], row, full, ALU.add).then_inc(indexed, 1)
            then(nc.vector.tensor_scalar(keep, place, CAP - 0.5, None, ALU.is_lt))
            then(nc.vector.tensor_scalar(full, row, float(-SLOTS), None, ALU.add))
            then(nc.vector.tensor_tensor(row, full, keep, ALU.mult))
            nc.vector.tensor_scalar(slot_out[:, :, :], row, float(SLOTS), None, ALU.add).then_inc(indexed, 1)

            def row_max(g):
                dve.wait_ge(s_done, num(g) + 1)
                if past(g, 2):
                    dve.wait_ge(mtr_done, num(g) - 1)
                nc.vector.tensor_reduce(m8[:, at(g, 2), :, 0], ps_s(0).rearrange("p (h k) -> p h k", h=GH), AX.X, ALU.max)
                nc.vector.tensor_reduce(m8[:, at(g, 2), :, 1], ps[:, 1:3, :].rearrange("p c (h k) -> p (c h) k", h=2),
                                        AX.X, ALU.max).then_inc(max_done, 1)
            for n in range(3):
                row_max((0, n))

            def slot(g):
                if within(plus(g, 3), G0):
                    row_max(plus(g, 3))
            def middle():
                for e in range(E):
                    dve.wait_ge(sig_done, e + 1)
                    if e >= 1:
                        dve.wait_ge(gated, e)
                    nc.vector.tensor_tensor(act_t[:, :, :].rearrange("p c t -> p (c t)"), ps[:, 2 + e % 2, :],
                                            act_s[:, :, :].rearrange("p c t -> p (c t)"), ALU.mult).then_inc(gate_s, 1)
                    dve.wait_ge(gate_s, e + 1)
                    if e >= 2:
                        dve.wait_ge(down_mm, e - 1)
                    nc.vector.tensor_tensor(act_g[:, e % 2, :, :].rearrange("p c t -> p (c t)"), ps[:, e % 2, :],
                                            act_t[:, :, :].rearrange("p c t -> p (c t)"), ALU.mult).then_inc(gated, 1)
                dve.wait_ge(pick_e, 1)
                then(nc.vector.tensor_scalar(r_s[:, 2, 0, :], r_s[:, 1, 0, :], 1.0, None, ALU.add))
                then(nc.vector.reciprocal(pick_p[:, 0, :], r_s[:, 2, 0, :]))
                then(nc.vector.tensor_tensor(pick_p[:, 1, :], r_s[:, 1, 0, :], pick_p[:, 0, :], ALU.mult))
            run_slots(dve, G0, slot, middle)

            dve.wait_ge(wv_in, 32 * B)
            dve.wait_ge(gathered, 16 * 2 * NT)
            for j in range(NB):
                u = j % 2
                nc.vector.reciprocal(den_all[:, j * BLK:(j + 1) * BLK], den_all[:, j * BLK:(j + 1) * BLK]).then_inc(rden_done, 1)
                dve.wait_ge(rden_done, j + 1)
                if j >= 2:
                    dve.wait_ge(wo_mm, j - 1)
                nc.vector.tensor_tensor(wvn[:, u, :], wv_all[:, j * BLK:(j + 1) * BLK], den_all[:, j * BLK:(j + 1) * BLK],
                                        ALU.mult).then_inc(wvn_done, 1)
                dve.wait_ge(wo_mm, j + 1)
                nc.vector.tensor_tensor(x[:, j * TPB:(j + 1) * TPB, :], x[:, j * TPB:(j + 1) * TPB, :],
                                        ps[:, u, :].rearrange("p (t c) -> p t c", t=TPB), ALU.add).then_inc(x1_attn, 1)
                dve.wait_ge(x1_attn, j + 1)
                for c, y in ((0, xn), (1, y_more)):
                    for t in range(j * TPB, (j + 1) * TPB):
                        last = nc.vector.scalar_tensor_tensor(out=x[:, t, :], in0=y[:, t, :], scalar=pick_p[:, c, t:t + 1], in1=x[:, t, :],
                                                              op0=ALU.mult, op1=ALU.add)
                    if c == 0:
                        last.then_inc(x1_half, 1)
                        dve.wait_ge(x1_half, j + 1)
                    else:
                        last.then_inc(x1_done, 1)

            w_v = w1_raw[:, 2 * P:3 * P].rearrange("p (h d) -> p h d", h=H1)
            then(nc.vector.tensor_reduce(rb1_s[:, 0:H1], w_v, AX.X, ALU.add))
            then(nc.vector.scalar_tensor_tensor(out=w_v, in0=rb1_s[:, 0:H1].unsqueeze(2).broadcast_to([P, H1, HD1]), scalar=-1.0 / HD1,
                                                    in1=w_v, op0=ALU.mult, op1=ALU.add))
            for (hi, lo), src in ((w1_qk, w1_raw[:, 0:2 * P]), (w1_p, w1_raw[:, 2 * P:])):
                then(nc.vector.tensor_copy(r32(hi[:, :]), src))
                nc.vector.tensor_tensor(r32(lo[:, :]), src, hi[:, :], ALU.subtract).then_inc(consts_ready, 1)

            dve.wait_ge(x1_done, NB)
            with dve.Fori(0, NT // 4) as i:
                for u in range(4):
                    nc.vector.bn_stats(stats1[:, ds(i * 4 + u, 1), :].rearrange("p o c -> p (o c)"),
                                       x[:, ds(i * 4 + u, 1), :].rearrange("p o c -> p (o c)")).then_inc(stats_done, 1)
            dve.wait_ge(stats_done, 2 * NT)
            for t in range(NT):
                nc.vector.bn_aggr(moments[:, t, :], stats1[:, t, :]).then_inc(moments_done, 1)
            dve.wait_ge(moments_done, 2 * NT)
            nc.vector.tensor_scalar(var[:, :], moments[:, :, 1], EPS, None, ALU.add).then_inc(var_ready, 1)
            dve.wait_ge(std_ready, 2)
            nc.vector.reciprocal(rstd[:, :], std[:, :]).then_inc(rstd_ready, 1)
            dve.wait_ge(rstd_ready, 2)

            def normalise(b, u):
                for v in range(TB):
                    t = b * TB + v
                    nc.vector.tensor_scalar(xn1_ring[:, u, v, :], x[:, ds(t, 1), :].rearrange("p o c -> p (o c)"),
                                            moments[:, ds(t, 1), 0], rstd[:, ds(t, 1)], ALU.subtract, ALU.mult).then_inc(xn1_ready, 1)

            def low_x(b, u):
                dve.wait_ge(xh_put, b + 1)
                nc.vector.tensor_tensor(r32(xr_l[:, u, :]), ps_t1(u), xr_h[:, u, :], ALU.subtract).then_inc(xl_put, 1)
            normalise(0, 0)
            normalise(1, 1)
            low_x(0, 0)
            dve.wait_ge(w_in, 18 * 16)

            def parts(b, u):
                for mm, res, src, bank, scaled, c in ((q1_mm, q1_res, q1_s, ps_q1, q1_scaled, 0), (k1_mm, k1_res, k1_s, ps_k1, k1_scaled, 1)):
                    dve.wait_ge(mm, b + 1)
                    dve.wait_ge(res, b + 1)
                    nc.vector.tensor_tensor(src[:, u, :], bank(u), gam[:, c, :], ALU.mult).then_inc(scaled, 1)
                if more(b, 1):
                    low_x(b + 1, 1 - u)
                if more(b, 2):
                    dve.wait_ge(t1_done, b + 1)
                    normalise(b + 2, u)
                for hi, lo, src, part, rest, res in ((q1_hi, q1_lo, q1_s, q1_p, q1_rest, q1_res), (k1_hi, k1_lo, k1_s, k1_p, k1_rest, k1_res)):
                    dve.wait_ge(hi, b + 1)
                    dve.wait_ge(lo, b + 1)
                    nc.vector.tensor_tensor(rest[:, u, :], src[:, u, :], part[:, u, 0, :], ALU.subtract).then_inc(res, 1)
                dve.wait_ge(v1_put, 2 * b + 2)
                nc.vector.tensor_tensor(sg[:, ds(b * TB, TB), :], p1_both[:, :, D:2 * D], sig1[:, u, :, :], ALU.mult).then_inc(sg_put, 1)
                nc.vector.tensor_tensor(logits1[:, ds(b * TB, TB), :], p1_both[:, :, 2 * D:PROJ1],
                                        rb1[:, :].unsqueeze(1).broadcast_to([P, TB, E]), ALU.add).then_inc(lg1_put, 1)
            run_pairs(dve, parts)

            for u in range(2):
                dve.wait_ge(q1_stored[u], 16 * (B // 2 + 1))
                dve.wait_ge(k1_stored[u], 16 * (B // 2 + 1))
                dve.wait_ge(x_kept[u], 32 * (B // 2 + 1))

            def slot(g):
                u = at(g, 2)
                dve.wait_ge(s1_done, num(g) + 1)
                if past(g, 2):
                    dve.wait_ge(pv1_done, num(g) - 1)
                nc.vector.tensor_tensor(sc[:, u, 0:2, :].rearrange("p c (h t) -> p (c h) t", h=GH),
                                        ps[:, 3 * u:3 * u + 2, :].rearrange("p c (h t) -> p (c h) t", h=GH),
                                        upto[:, :].unsqueeze(1).broadcast_to([P, 2 * GH, P]), ALU.mult).then_inc(masked, 1)
            run_slots(dve, G1, slot)

            dve.wait_ge(ret_put, G1)
            pairs = [P, NT, E, E]
            then(nc.vector.tensor_reduce(p1_s[:, 0, :], logits1[:, :, :], AX.X, ALU.max))
            nc.vector.tensor_tensor(p1_x[:, 0, :, :], logits1[:, :, :], p1_s[:, 0, :].unsqueeze(2).broadcast_to(by_expert), ALU.subtract)\
                .then_inc(pick_d, 1)
            for j in range(NB):
                dve.wait_ge(sq_done, j + 1)
                nc.vector.tensor_reduce(ss1[:, j * TPB:(j + 1) * TPB, :],
                                        sq[:, j % 2, :].rearrange("p (t h d) -> p t h d", t=TPB, h=H1), AX.X, ALU.add).then_inc(ss_done, 1)
            dve.wait_ge(ss_done, NB)
            nc.vector.tensor_scalar(ss1[:, :, :], ss1[:, :, :], 1.0 / HD1, EPS, ALU.mult, ALU.add).then_inc(ss_done, 1)
            dve.wait_ge(pick_e, 2)
            then(nc.vector.tensor_reduce(p1_s[:, 1, :], p1_x[:, 1, :, :], AX.X, ALU.add))
            then(nc.vector.reciprocal(p1_s[:, 2, :], p1_s[:, 1, :]))
            then(nc.vector.tensor_tensor(p1[:, :, :], p1_x[:, 1, :, :], p1_s[:, 2, :].unsqueeze(2).broadcast_to(by_expert), ALU.mult))
            other = p1[:, :, :].unsqueeze(2).broadcast_to(pairs)
            own = p1[:, :, :].unsqueeze(3).broadcast_to(pairs)
            then(nc.vector.tensor_tensor(ord_a[:, :, :, :], other, own, ALU.is_equal))
            then(nc.vector.tensor_tensor(ord_a[:, :, :, :], ord_a[:, :, :, :], earlier_e[:, :, :].unsqueeze(1).broadcast_to(pairs), ALU.mult))
            then(nc.vector.tensor_tensor(ord_b[:, :, :, :], other, own, ALU.is_gt))
            then(nc.vector.tensor_tensor(ord_a[:, :, :, :], ord_a[:, :, :, :], ord_b[:, :, :, :], ALU.add))
            then(nc.vector.tensor_tensor(ord_b[:, :, :, :], ord_a[:, :, :, :], other, ALU.mult))
            then(nc.vector.tensor_reduce(p1_x[:, 0, :, :], ord_b[:, :, :, :], AX.X, ALU.add))
            then(nc.vector.tensor_reduce(p1_x[:, 1, :, :], ord_a[:, :, :, :], AX.X, ALU.add))
            then(nc.vector.tensor_scalar(p1_x[:, 1, :, :], p1_x[:, 1, :, :], 1.5, None, ALU.is_lt))
            then(nc.vector.scalar_tensor_tensor(out=p1_x[:, 2, :, :], in0=p1_x[:, 0, :, :], scalar=TOP_P, in1=p1_x[:, 1, :, :],
                                                op0=ALU.is_lt, op1=ALU.max))
            nc.vector.tensor_tensor(gates[:, :, :], p1_x[:, 2, :, :], p1[:, :, :], ALU.mult).then_inc(gates_done, 1)

            dve.wait_ge(sd_done, 1)
            then(nc.vector.reciprocal(rs1[:, :, :], sd1[:, :, :]))

            def add_retention(j):
                dve.wait_ge(w2_mm, j + 1)
                tiles = x[:, j * TPB:(j + 1) * TPB, :]
                nc.vector.tensor_tensor(tiles, tiles, ps[:, 2 + j % 2, :].rearrange("p (t c) -> p t c", t=TPB), ALU.add).then_inc(x2_attn, 1)
            for j in range(NB):
                tiles = slice(j * TPB, (j + 1) * TPB)
                if j >= 2:
                    dve.wait_ge(zt_mm, j - 1)
                then(nc.vector.tensor_tensor(z[:, j % 2, :].rearrange("p (t h d) -> p t h d", t=TPB, h=H1),
                                        ret[:, tiles, :].rearrange("p t (h d) -> p t h d", h=H1),
                                        rs1[:, tiles, :].unsqueeze(3).broadcast_to([P, TPB, H1, HD1]), ALU.mult))
                by_token = z[:, j % 2, :].rearrange("p (t c) -> p t c", t=TPB)
                nc.vector.tensor_tensor(by_token, by_token, gn_w[:, :].unsqueeze(1).broadcast_to([P, TPB, D]), ALU.mult).then_inc(z_b, 1)
                if j >= 1:
                    add_retention(j - 1)
            add_retention(NB - 1)

            def split_weights(e):
                dve.wait_ge(raw_in[e % 2], e // 2 * 32 + 32)
                nc.vector.tensor_copy(r32(w1_h[:, e, :]), w_raw[:, e % 2, 0, :]).then_inc(w1_hi, 1)
                nc.vector.tensor_copy(r32(w2_h[:, e, :]), w_raw[:, e % 2, 1, :]).then_inc(w2_hi, 1)
                dve.wait_ge(w1_hi, e + 1)
                nc.vector.tensor_tensor(r32(w1_l[:, e, :]), w_raw[:, e % 2, 0, :], w1_h[:, e, :], ALU.subtract).then_inc(w1_lo, 1)

            def gate_expert(j, e):
                dve.wait_ge(y_mm, j * UNITS + e * FC + FC)
                dve.wait_ge(gate_in[e], j * 16 + 16)
                if e == 0:
                    if known_block(j) != 0:
                        dve.wait_ge(acc_turned, j)
                elif e >= 3:
                    dve.wait_ge(summed, j * (E - 1) + e - 2)
                elif known_block(j) != 0:
                    dve.wait_ge(summed, j * (E - 1))
                nc.vector.scalar_tensor_tensor(out=acc[:, :] if e == 0 else yt[:, e % 2, :], in0=ps[:, 4 + e % 2, :], scalar=b2[:, e:e + 1],
                                               in1=gate_b[:, e, :], op0=ALU.add, op1=ALU.mult).then_inc(yv, 1)

            def finish(j):
                dve.wait_ge(acc_turned, j + 1)
                tiles = x[:, ds(j * TPB, TPB), :]
                nc.vector.tensor_tensor(tiles, tiles, ps[:, 6, :].rearrange("p (t c) -> p t c", t=TPB), ALU.add).then_inc(x2_done, 1)
            split_weights(0)
            split_weights(1)
            dve.wait_ge(w_in, 20 * 16)

            def body(j):
                for m in range(UNITS):
                    if known_block(j) == 0 and m % FC == 0 and m // FC + 2 < E:
                        split_weights(m // FC + 2)
                    n = j * UNITS + m
                    dve.wait_ge(f_done, n + 1)
                    if known_block(j) != 0 or m >= 4:
                        dve.wait_ge(y_mm, n - 3)
                    nc.vector.tensor_copy(r32(f_h[:, m % 4, :]), f[:, m % 4, :]).then_inc(f_hi, 1)
                    if m % 2 == 0:
                        dve.wait_ge(f_hi, n + 1)
                        nc.vector.tensor_tensor(r32(f_l[:, m % 4, :]), f[:, m % 4, :], f_h[:, m % 4, :], ALU.subtract).then_inc(f_lo[0], 1)
                    if m % FC == 2:
                        if m >= 6:
                            gate_expert(j, (m - 6) // FC)
                        elif known_block(j) != 0:
                            gate_expert(j - 1, E - 1)
                    if m == 8 and known_block(j) != 0:
                        finish(j - 1)
            run_blocks(dve, body)
            gate_expert(NB - 1, E - 1)
            finish(NB - 1)

        @block.tensor
        def _(pe):
            pe.wait_ge(consts_ready, 5)
            with pe.Fori(0, B // 2) as ii:
                for u in range(2):
                    b = ii * 2 + u
                    pe.wait_ge(xn_ready, (b + 1) * TB)
                    for t in range(TB):
                        last = nc.tensor.transpose(ps_t(u)[:, t * P:(t + 1) * P], xn_ring[:, u, t, :], ident[:, :])
                    last.then_inc(tr_done, 1)
                    pe.wait_ge(xT_done, b + 1)
                    pe.wait_ge(q_res, b + 1)
                    nc.tensor.matmul(ps_q(u), w_q[:, :], xT[:, u, :], start=True, stop=True).then_inc(q_mm, 1)
                    pe.wait_ge(k_res, b + 1)
                    nc.tensor.matmul(ps_k(u), w_k[:, :], xT[:, u, :], start=True, stop=True).then_inc(k_mm, 1)
                    pe.wait_ge(lg_put, b + 1)
                    for t in range(TB):
                        last = nc.tensor.matmul(ps_v(u)[:, t, :], xT[:, u, t * P:(t + 1) * P], w_vr[:, :], start=True, stop=True)
                    last.then_inc(v_mm, 1)

            pe.wait_ge(counted, 1)
            for n, lhs in enumerate((before, ones_h)):
                last = nc.tensor.matmul(ps[:, 0, n * NT * E:(n + 1) * NT * E], lhs[:, :], chosen[:, :, :].rearrange("p t e -> p (t e)"),
                                        start=True, stop=True)
            last.then_inc(counted, 1)
            pe.wait_ge(indexed, 1)

            def scores(g):
                r = at(g, RING)
                qs, ks = (st[:, r // 2, (r % 2) * GH:(r % 2) * GH + GH, :] for st in (q_st, k_st))
                if r % 2 == 0:
                    pe.wait_ge(stack_in[r // 2], div(g, RING) * 64 + 64)
                if past(g, 1):
                    pe.wait_ge(max_done, num(g))
                nc.tensor.matmul(ps_s(0).rearrange("p (h k) -> p h k", h=GH), ident_h[:, :],
                                 mask_qk[:, :].unsqueeze(1).broadcast_to([P, GH, P]), start=True, stop=False, skip_group_check=True)
                for c in (1, 2):
                    nc.tensor.matmul(ps_s(c).rearrange("p (h k) -> p h k", h=2)[:, :, P:S], ident_h[:, :],
                                     mask_qk[:, :].unsqueeze(1).broadcast_to([P, 2, P]), start=True, stop=False, skip_group_check=True)
                for h in range(GH):
                    nc.tensor.matmul(ps_s(0)[:, h * P:(h + 1) * P], qs[0:R0, h, 0:P], ks[0:R0, h, 0:P],
                                     start=False, stop=True, skip_group_check=True)
                for h in range(GH):
                    last = nc.tensor.matmul(ps_s(1 + h // 2)[:, h % 2 * S:(h % 2 + 1) * S], qs[0:R0, h, P:S], ks[0:R0, h, :],
                                            start=False, stop=True, skip_group_check=True)
                last.then_inc(s_done, 1)

            def turn_max(g):
                pe.wait_ge(max_done, num(g) + 1)
                if past(g, 1):
                    pe.wait_ge(mneg_done, num(g))
                nc.tensor.transpose(ps_m, m8[:, at(g, 2), :, :].rearrange("p h t -> p (h t)"), ident[:, :]).then_inc(mtr_done, 1)

            def scores_t(g):
                r = at(g, RING)
                qs, ks = (st[0:R0 + 1, r // 2, (r % 2) * GH:(r % 2) * GH + GH, :] for st in (q_st, k_st))
                if past(g, 1):
                    pe.wait_ge(exp_done, num(g))
                nc.tensor.matmul(ps_st(0).rearrange("p (h k) -> p h k", h=GH), ident_h[:, :],
                                 mask_kq[:, :].unsqueeze(1).broadcast_to([P, GH, P]), start=True, stop=False, skip_group_check=True)
                for c in (1, 2):
                    nc.tensor.matmul(ps_st(c).rearrange("p (h k) -> p h k", h=2)[:, :, 0:P], ident_h[:, :],
                                     mask_kq[:, :].unsqueeze(1).broadcast_to([P, 2, P]), start=True, stop=False, skip_group_check=True)
                pe.wait_ge(mrow_in[r % 4], div(g, 4) * 16 + 16)
                for h in range(GH):
                    nc.tensor.matmul(ps_st(0)[:, h * P:(h + 1) * P], ks[:, h, P:S], qs[:, h, P:S],
                                     start=False, stop=True, skip_group_check=True)
                for h in range(GH):
                    last = nc.tensor.matmul(ps_st(1 + h // 2)[:, h % 2 * S:(h % 2 + 1) * S], ks[:, h, 0:P], qs[:, h, :],
                                            start=False, stop=True, skip_group_check=True)
                last.then_inc(st_done, 1)

            def weigh(g):
                k, u = at(g, GPB0), at(g, RING) // GPB0
                pe.wait_ge(exp_done, num(g) + 1)
                if k == 0:
                    pe.wait_ge(v_here, div(g, GPB0) + 1)
                if past(g, 1):
                    pe.wait_ge(o_evac, num(g))
                for h in range(GH):
                    nc.tensor.matmul(ps_o[32 * h:32 * h + 2 * HD0, :], v_ring[:, u, 0, k * GH + h, :],
                                     probs[:, at(g, 2), 1 + h // 2, h % 2 * S:(h % 2 + 1) * S],
                                     start=True, stop=False, skip_group_check=True)
                for h in range(GH):
                    last = nc.tensor.matmul(ps_o[32 * h:32 * h + 2 * HD0, P:S], v_ring[:, u, 1, k * GH + h, :],
                                            probs[:, at(g, 2), 0, h * P:(h + 1) * P],
                                            start=False, stop=True, skip_group_check=True)
                last.then_inc(pv_done, 1)

            for n in range(3):
                scores((0, n))
                if n:
                    turn_max((0, n - 1))

            def slot(g):
                if within(plus(g, 3), G0):
                    scores(plus(g, 3))
                if within(plus(g, 2), G0):
                    turn_max(plus(g, 2))
                scores_t(g)
                if past(g, 1):
                    weigh(plus(g, -1))
            def middle():
                n = MIDDLE * RING
                pe.wait_ge(xg_in, 16)
                pe.wait_ge(max_done, n + 3)
                pe.wait_ge(exp_done, n)
                for c in range(SLOTS // P):
                    last = nc.tensor.transpose(ps[:, c // 4, c % 4 * P:(c % 4 + 1) * P], xg[:, c, :], ident[:, :])
                    if c % 4 == 3:
                        last.then_inc(xgt_mm, 1)
                pe.wait_ge(xgt_put, SLOTS // 512)

                def up(e):
                    if e >= 2:
                        pe.wait_ge(gated, e - 1)
                    for m, bank in ((0, e % 2), (1, 2 + e % 2)):
                        for c in range(2):
                            last = nc.tensor.matmul(ps[:, bank, c * CAP:(c + 1) * CAP], w_up[:, e, m, c * P:(c + 1) * P],
                                                    xgT[:, e * CAP:(e + 1) * CAP], start=True, stop=True)
                    last.then_inc(up_mm, 1)

                def down(e):
                    pe.wait_ge(gated, e + 1)
                    if e >= 2:
                        pe.wait_ge(y_put, e - 1)
                    for t in range(CAP // P):
                        for c in range(2):
                            last = nc.tensor.matmul(ps[:, 4 + e % 2, t * D:(t + 1) * D], act_g[:, e % 2, c, t * P:(t + 1) * P],
                                                    w_dn[:, e, c, :], start=(c == 0), stop=(c == 1))
                    last.then_inc(down_mm, 1)
                up(0)
                for e in range(E):
                    if e + 1 < E:
                        up(e + 1)
                    down(e)
                pe.wait_ge(y_put, E)
            run_slots(pe, G0, slot, middle)
            weigh((0, G0 - 1))
            for j in range(NB):
                u = j % 2
                pe.wait_ge(wvn_done, j + 1)
                if j >= 2:
                    pe.wait_ge(x1_done, j - 1)
                for t in range(TPB):
                    last = nc.tensor.matmul(ps[:, u, t * P:(t + 1) * P], wvn[:, u, t * P:(t + 1) * P], w_o[:, :], start=True, stop=True)
                last.then_inc(wo_mm, 1)

            def transposes(b, u):
                pe.wait_ge(xn1_ready, (b + 1) * TB)
                pe.wait_ge(xl_put, b + 1)
                for t in range(TB):
                    last = nc.tensor.transpose(ps_t1(u)[:, t * P:(t + 1) * P], xn1_ring[:, u, t, :], ident[:, :])
                last.then_inc(t1_done, 1)

            def three(dst, lhs, rhs):
                for k, (i, j) in enumerate(((0, 0), (1, 0), (0, 1))):
                    last = nc.tensor.matmul(dst, r32(lhs[i]), r32(rhs[j]), start=(k == 0), stop=(k == 2))
                return last

            def products(b, u):
                pe.wait_ge(xl_put, b + 1 + CREDIT)
                rhs = (xr_h[:, u, :], xr_l[:, u, :])
                pe.wait_ge(q1_scaled, b + 1)
                three(ps_q1(u), [w[:, 0:P] for w in w1_qk], rhs).then_inc(q1_mm, 1)
                pe.wait_ge(k1_scaled, b + 1)
                three(ps_k1(u), [w[:, P:2 * P] for w in w1_qk], rhs).then_inc(k1_mm, 1)
                pe.wait_ge(lg1_put, b + 1)
                for t in range(TB):
                    last = three(ps_p1(t), [x_[:, t * P:(t + 1) * P] for x_ in rhs], [w[:, :] for w in w1_p])
                last.then_inc(p1_mm, 1)
            pe.wait_ge(consts_ready, 7)
            transposes(0, 0)
            transposes(1, 1)

            def step(b, u):
                products(b, u)
                if more(b, 2):
                    transposes(b + 2, u)
            run_pairs(pe, step)

            def scores1(g):
                r, u = at(g, RING), at(g, 2)
                qs, ks = (st[:, r // 2, u * GH:(u + 1) * GH, :] for st in (q1_st, k1_st))
                if r % 2 == 0:
                    pe.wait_ge(stack1_in[r // 2], div(g, RING) * 80 + 80)
                if past(g, 2):
                    pe.wait_ge(masked, num(g) - 1)
                    pe.wait_ge(copied, num(g) - 1)
                for c, (k, q) in enumerate(((1, 1), (0, 0), (0, 1))):
                    for h in range(GH):
                        last = nc.tensor.matmul(ps_sc(u, c)[:, h * P:(h + 1) * P], ks[:, h, k * P:(k + 1) * P], qs[:, h, q * P:(q + 1) * P],
                                                start=True, stop=True)
                last.then_inc(s1_done, 1)

            def weigh1(g):
                u, half = at(g, RING) // 2 % 2, g[1] % 2
                pe.wait_ge(masked, num(g) + 1)
                pe.wait_ge(copied, num(g) + 1)
                if half == 0:
                    pe.wait_ge(v1_here, div(g, 2) + 1)
                if past(g, 1):
                    pe.wait_ge(o1_evac, num(g))
                for h in range(GH):
                    nc.tensor.matmul(ps_o1[32 * h:32 * h + HD1, :].rearrange("p (c t) -> p c t", c=2), v1_ring[:, u, 0, half * GH + h, :],
                                     sc[:, at(g, 2), 1:3, h * P:(h + 1) * P], start=True, stop=False, skip_group_check=True)
                for h in range(GH):
                    last = nc.tensor.matmul(ps_o1[32 * h:32 * h + HD1, P:S], v1_ring[:, u, 1, half * GH + h, :],
                                            sc[:, at(g, 2), 0, h * P:(h + 1) * P], start=False, stop=True, skip_group_check=True)
                last.then_inc(pv1_done, 1)

            def turn1(g):
                pe.wait_ge(o1_evac, num(g) + 1)
                if past(g, 1):
                    pe.wait_ge(ret_put, num(g))
                for t in range(TB):
                    last = nc.tensor.transpose(ps_r1[:, t * P:(t + 1) * P], o1_ring[:, at(g, 2), t * P:(t + 1) * P], ident[:, :])
                last.then_inc(turned1, 1)

            pe.wait_ge(lg1_put, B + 1)

            def slot(g):
                scores1(g)
                if past(g, 1):
                    weigh1(plus(g, -1))
                if past(g, 2):
                    turn1(plus(g, -2))
            run_slots(pe, G1, slot)
            weigh1((0, G1 - 1))
            turn1((0, G1 - 2))
            turn1((0, G1 - 1))

            pe.wait_ge(gates_done, 1)
            for c in range(2):
                nc.tensor.transpose(ps[:, 4 + c, 0:P], gates[:, c * NT // 2:(c + 1) * NT // 2, :].rearrange("p t e -> p (t e)"), ident[:, :])\
                    .then_inc(gt_mm, 1)

            def project(j):
                pe.wait_ge(zt_put, j + 1)
                if j >= 2:
                    pe.wait_ge(x2_attn, j - 1)
                for t in range(TPB):
                    last = nc.tensor.matmul(ps[:, 2 + j % 2, t * P:(t + 1) * P], zT[:, j % 2, t * P:(t + 1) * P], w2_a[:, :], start=True, stop=True)
                last.then_inc(w2_mm, 1)
            for j in range(NB):
                pe.wait_ge(z_done, j + 1)
                if j >= 2:
                    pe.wait_ge(zt_put, j - 1)
                for t in range(TPB):
                    last = nc.tensor.transpose(ps[:, j % 2, t * P:(t + 1) * P], z[:, j % 2, t * P:(t + 1) * P], ident[:, :])
                last.then_inc(zt_mm, 1)
                if j >= 1:
                    project(j - 1)
            project(NB - 1)

            def hidden(j, m):
                if m >= UNITS:
                    j, m = j + 1, m - UNITS
                n, (e, c) = j * UNITS + m, divmod(m, FC)
                if known_block(j) == 0 and c == 0:
                    pe.wait_ge(w1_lo, e + 1)
                if known_block(j) != 0 or m >= 4:
                    pe.wait_ge(f_done, n - 3)
                three(ps[:, m % 4, :], [w[:, e, c * P:(c + 1) * P] for w in (w1_h, w1_l)],
                      [x_[:, ds(j * BLK, BLK)] for x_ in (xh, xl)]).then_inc(h_mm, 1)

            def output(j, m):
                n, (e, c) = j * UNITS + m, divmod(m, FC)
                if c == 0:
                    if known_block(j) == 0:
                        pe.wait_ge(w2_lo, e + 1)
                    if known_block(j) != 0 or e >= 2:
                        pe.wait_ge(yv, j * E + e - 1)
                pe.wait_ge(f_lo[m % 2], j * (UNITS // 2) + m // 2 + 1)
                w = [w_[:, e, c * P:(c + 1) * P] for w_ in (w2_h, w2_l)]
                for k, (i, fs) in enumerate(((0, f_h), (1, f_h), (0, f_l))):
                    last = nc.tensor.matmul(ps[:, 4 + e % 2, :], r32(w[i]), r32(fs[:, m % 4, :]), start=(c == 0 and k == 0),
                                            stop=(c == FC - 1 and k == 2))
                last.then_inc(y_mm, 1)

            def turn_sum(j):
                pe.wait_ge(summed, (j + 1) * (E - 1))
                if known_block(j) != 0:
                    pe.wait_ge(x2_done, j)
                for t in range(TPB):
                    last = nc.tensor.transpose(ps[:, 6, t * P:(t + 1) * P], acc[:, t * P:(t + 1) * P], ident[:, :])
                last.then_inc(acc_turned, 1)
            pe.wait_ge(x2_attn, NB)
            for m in range(AHEAD):
                hidden(0, m)

            def body(j):
                for m in range(UNITS):
                    if known_block(j) != NB - 1 or m + AHEAD < UNITS:
                        hidden(j, m + AHEAD)
                    output(j, m)
                    if m == 4 and known_block(j) != 0:
                        turn_sum(j - 1)
            run_blocks(pe, body)
            turn_sum(NB - 1)


_OUT = ((B, S, D), "float32")


def kernel(**inputs):
    import numpy as np
    import concourse.bacc as bacc
    from concourse.bass_utils import run_bass_kernel_spmd

    arrays = prepare(inputs, np)
    nc = bacc.Bacc("TRN2", target_bir_lowering=False, num_devices=1)
    aps = {k: nc.dram_tensor(f"in_{k}", v.shape, mybir.dt.from_np(v.dtype), kind="ExternalInput").ap() for k, v in arrays.items()}
    out = nc.dram_tensor("out_0", (N, D), F32, kind="ExternalOutput").ap()
    build(nc, aps, out)
    r = run_bass_kernel_spmd(nc, [{f"in_{k}": v for k, v in arrays.items()}], core_ids=[0])
    return r.results[0]["out_0"].reshape(B, S, D)


def prepare(inputs, np):
    i = {k: np.ascontiguousarray(v) for k, v in inputs.items()}
    at = np.arange(P)
    tables = np.zeros((P, 3, P), np.float32)
    tables[:, 0, :] = np.where(at[None, :] > at[:, None], np.float32(NEG), np.float32(0))
    tables[:, 1, :] = tables[:, 0, :].T
    tables[:, 2, :] = (at[:, None] < at[None, :])
    ex = np.arange(E)
    gamma = (1.0 - np.exp(np.linspace(np.log(1.0 / 512.0), np.log(1.0 / 32.0), H1))).astype(np.float32).astype(np.float64)
    place = np.arange(S)
    gam = np.stack([np.tile(gamma[:, None] ** k, (HD1, 1)) for k in (place[None, :], -place[None, :])], axis=1)

    def rows(v):
        return np.ascontiguousarray(np.broadcast_to(v, (P,) + v.shape))

    def by_depth(w, heads):
        return np.ascontiguousarray(w.reshape(P, heads, -1).transpose(0, 2, 1).reshape(P, P))

    def diagonal(w):
        m = np.zeros((H1, HD1, H1, HD1), np.float32)
        for h in range(H1):
            m[h, :, h, :] = w[h]
        return m.reshape(P, P)
    qvk = i["L0_attn_Wqvk"]
    return {
        "h": np.ascontiguousarray(i["L0_attn_h"].reshape(NT, P, D).transpose(1, 0, 2)),
        "ident": np.eye(P, dtype=np.float32),
        "tables": tables,
        "upto": (at[:, None] <= at[None, :]).astype(np.float32),
        "w_q": by_depth(qvk[:, 0:D], H0),
        "w_k": by_depth(qvk[:, 2 * D:3 * D], H0),
        "w_vr": np.concatenate([qvk[:, D:2 * D], i["L0_ffn_router_w"].T], axis=1),
        "w_o": i["L0_attn_Wo"],
        "rb0": rows(i["L0_ffn_router_b"]),
        "rank_e": rows(np.stack([ex, E - ex]).astype(np.float32)),
        "earlier_e": rows((ex[None, :] <= ex[:, None]).astype(np.float32)),
        "w_up": np.ascontiguousarray(np.stack([i["L0_ffn_W"], i["L0_ffn_V"]], axis=1).transpose(2, 0, 1, 3)),
        "w_dn": np.ascontiguousarray(i["L0_ffn_W_out"].reshape(E, 2, P, D).transpose(2, 0, 1, 3)),
        "w1_raw": np.concatenate([by_depth(diagonal(i["L1_attn_Wq"]), H1), by_depth(diagonal(i["L1_attn_Wk"]), H1),
                                  diagonal(i["L1_attn_Wv"]), i["L1_attn_W1"], i["L1_ffn_Wr"]], axis=1),
        "w2_a": i["L1_attn_W2"],
        "gn_w": rows(i["L1_attn_gn_w"]),
        "gn_b": rows(i["L1_attn_gn_b"]),
        "rb1": rows(i["L1_ffn_br"]),
        "gam": gam.astype(np.float32),
        "w1_e": np.ascontiguousarray(i["L1_ffn_W1"].transpose(1, 0, 2)),
        "w2_e": np.ascontiguousarray(i["L1_ffn_W2"].reshape(E, FC, P, D).transpose(2, 0, 1, 3).reshape(P, E, FC * D)),
        "b1": np.ascontiguousarray(i["L1_ffn_b1"].reshape(UNITS, P).T),
        "b2": np.ascontiguousarray(i["L1_ffn_b2"].T),
    }
```

```python
from contextlib import ExitStack

import concourse.bass as bass
from concourse import mybir

F32 = mybir.dt.float32
F32R = mybir.dt.float32r
BF16 = mybir.dt.bfloat16
U32 = mybir.dt.uint32
ALU = mybir.AluOpType
ACT = mybir.ActivationFunctionType
AX = mybir.AxisListType
ds = bass.ds

P = 128
B, S, D = 16, 256, 128
N = B * S
NT = N // P
TB = S // P
EPS = 1e-5
H0, HD0 = 16, 8
H1, HD1 = 8, 16
E = 8
FH0 = 256
CAP = 256
SLOTS = E * CAP
FH1 = 512
FC = FH1 // P
TOP_P = 0.8
NEG = -1e30
GH = 4
G0 = B * H0 // GH
G1 = B * H1 // GH
MIDDLE = 4
GPB0 = H0 // GH
RING = 8
PAIRS = RING // 2
R0 = 9 * HD0
R1 = 8 * HD1
BLK = 512
NB = N // BLK
TPB = BLK // P
LN0 = 4
PROJ1 = 2 * P + E


UNITS = E * FC
AHEAD = 3


def build(nc, a, out):
    ctx = ExitStack()
    with ctx:
        def sb(name, shape, dt=F32, where=ctx):
            return where.enter_context(nc.sbuf_tensor(name, shape, dt))

        def sem(name):
            return ctx.enter_context(nc.semaphore(name))

        def dram(name, shape, dt=F32):
            return nc.dram_tensor(name, shape, dt, kind="Internal").ap()

        q_parts = dram("q_parts", [B, 3, P, S], BF16)
        k_parts = dram("k_parts", [B, 3, 3, P, S], BF16)

        o_rows = dram("o_rows", [B, GPB0, P, S])
        o_heads = o_rows.rearrange("b k (g r) t -> b (k g) r t", r=32)

        x = sb("x", [P, NT, D])
        ident = sb("ident", [P, P])
        upto = sb("upto", [P, P])
        rden_rows = dram("rden_rows", [B, H0, S])
        x_slots = dram("x_slots", [SLOTS, D])
        gate_rows = dram("gate_rows", [E, N])
        y_slots = dram("y_slots", [SLOTS + P, D])
        ident_h = sb("ident_h", [P, P], BF16)
        mask_qk = sb("mask_qk", [P, P], BF16)
        mask_kq = sb("mask_kq", [P, P], BF16)
        before = sb("before", [P, P], BF16)
        ones_h = sb("ones_h", [P, P], BF16)
        moments = sb("moments", [P, NT, 2])
        var = sb("var", [P, NT])
        std = sb("std", [P, NT])
        rstd = sb("rstd", [P, NT])

        w1_raw = sb("w1_raw", [P, 2 * P + PROJ1])
        w1_qk = [sb(f"w1_qk_{i}", [P, 2 * P]) for i in ("hi", "lo")]
        w1_p = [sb(f"w1_p_{i}", [P, PROJ1]) for i in ("hi", "lo")]
        w2_a = sb("w2_a", [P, D])
        gn_w = sb("gn_w", [P, D])
        gn_b = sb("gn_b", [P, D])
        rb1 = sb("rb1", [P, E])
        rank_e = sb("rank_e", [P, 2, E])
        eps = sb("eps", [P, 1])
        rb1_s = sb("rb1_s", [P, H1])
        gates = sb("gates", [P, NT, E])
        pick_p = sb("pick_p", [P, 2, NT])

        era = ExitStack()
        xn = sb("xn", [P, NT, D], where=era)
        v_all = sb("v_all", [P, NT, H0, HD0], where=era)
        logits0 = sb("logits0", [P, NT, E], where=era)
        w_q = sb("w_q", [P, P], where=era)
        w_k = sb("w_k", [P, P], where=era)
        w_vr = sb("w_vr", [P, D + E], where=era)
        rb0 = sb("rb0", [P, E], where=era)
        w_o = sb("w_o", [P, D], where=era)
        zero = sb("zero", [P, D], where=era)
        w_up = sb("w_up", [P, E, 2, FH0], where=era)
        w_dn = sb("w_dn", [P, E, 2, D], where=era)
        picked = sb("picked", [P, 2, NT, E], where=era)
        r_a = sb("r_a", [P, 2, NT, E], where=era)
        r_b = sb("r_b", [P, 2, NT, E], where=era)
        r_s = sb("r_s", [P, 8, 2, NT], where=era)
        rank = sb("rank", [P, NT, E], where=era)
        chosen = sb("chosen", [P, NT, E], BF16, where=era)
        ones_t = sb("ones_t", [P, NT], where=era)
        slot_in = sb("slot_in", [P, 2, NT], U32, where=era)
        slot_out = sb("slot_out", [P, 2, NT], U32, where=era)
        y_more = sb("y_more", [P, NT, D], where=era)
        xg = y_more[:, 0:SLOTS // P, :]
        xgT = y_more[:, SLOTS // P:NT, :].rearrange("p t c -> p (t c)")
        y_sb = xg
        act_s = sb("act_s", [P, 2, FH0], where=era)
        act_t = sb("act_t", [P, 2, FH0], where=era)
        act_g = sb("act_g", [P, 2, 2, FH0], where=era)
        den = sb("den", [P, S * H0 // P], where=era)
        rden = sb("rden", [P, S * H0 // P], where=era)
        rden_ring = sb("rden_ring", [P, 2, S], where=era)
        wv_ring = sb("wv_ring", [P, 2, S], where=era)
        wvn = sb("wvn", [P, 2, S], where=era)
        at_ring = sb("at_ring", [P, 2, TB, D], where=era)
        v_ring = sb("v_ring", [P, 2, TB, H0, 2 * HD0], where=era)
        m8 = sb("m8", [P, 2, GH, TB], where=era)
        m_neg = sb("m_neg", [2 * GH, 4, P], BF16, where=era)
        q_st = sb("q_st", [P, PAIRS, 2 * GH, S], BF16, where=era)
        k_st = sb("k_st", [P, PAIRS, 2 * GH, S], BF16, where=era)
        with ExitStack() as part:
            tables = sb("tables", [P, 3, P], where=part)
            stats = sb("stats", [P, NT, 6], where=part)
            xn_ring = sb("xn_ring", [P, 2, TB, D], where=part)
            xT = sb("xT", [P, 2, S], where=part)
            qp = sb("qp", [P, 2, 3, S], BF16, where=part)
            kp = sb("kp", [P, 2, 3, S], BF16, where=part)
            q_rest = sb("q_rest", [P, 2, S], where=part)
            k_rest = sb("k_rest", [P, 2, S], where=part)
        with ExitStack() as part:
            o_ring = sb("o_ring", [P, 4, S], where=part)
            probs = sb("probs", [P, 2, 3, 512], where=part)
            stats1 = sb("stats1", [P, NT, 6], where=part)
        era.close()

        era = ExitStack()
        xh = sb("xh", [P, N], where=era)
        xl = sb("xl", [P, N], where=era)
        w1_h = sb("w1_h", [P, E, FH1], where=era)
        w1_l = sb("w1_l", [P, E, FH1], where=era)
        w_raw = sb("w_raw", [P, 2, FH1], where=era)
        gT = sb("gT", [P, 2 * P], where=era)
        with ExitStack() as part:
            logits1 = sb("logits1", [P, NT, E], where=part)
            gam = sb("gam", [P, 2, S], where=part)
            v1 = sb("v1", [P, NT, H1, HD1], where=part)
            sg = sb("sg", [P, NT, D], where=part)
            with ExitStack() as sub:
                xn1_ring = sb("xn1_ring", [P, 2, TB, D], where=sub)
                xr_h = sb("xr_h", [P, 2, S], where=sub)
                xr_l = sb("xr_l", [P, 2, S], where=sub)
                q1_s = sb("q1_s", [P, 2, S], where=sub)
                k1_s = sb("k1_s", [P, 2, S], where=sub)
                q1_rest = sb("q1_rest", [P, 2, S], where=sub)
                k1_rest = sb("k1_rest", [P, 2, S], where=sub)
                q1_p = sb("q1_p", [P, 2, 3, S], BF16, where=sub)
                k1_p = sb("k1_p", [P, 2, 3, S], BF16, where=sub)
                sig1 = sb("sig1", [P, 2, TB, D], where=sub)
            with ExitStack() as sub:
                q1_st = sb("q1_st", [P, PAIRS, H1, S], BF16, where=sub)
                k1_st = sb("k1_st", [P, PAIRS, H1, S], BF16, where=sub)
                sc = sb("sc", [P, 2, 3, 512], where=sub)
                o1_ring = sb("o1_ring", [P, 2, S], where=sub)
                v1_ring = sb("v1_ring", [P, 2, TB, H1, HD1], where=sub)
                ret = sb("ret", [P, 4, TB, D], where=sub)
                sq = sb("sq", [P, 2, TB, D], where=sub)
                ss1, sd1, rs1 = (sb(n, [P, 2, TB, H1], where=sub) for n in ("ss1", "sd1", "rs1"))
                z = sb("z", [P, 2, TB, D], where=sub)
                zT = sb("zT", [P, 2, S], where=sub)
                at1_ring = sb("at1_ring", [P, 2, TB, D], where=sub)
                p1 = sb("p1", [P, NT, E], where=sub)
                p1_s = sb("p1_s", [P, 3, NT], where=sub)
                p1_x = sb("p1_x", [P, 2, NT, E], where=sub)
                order = sb("order", [P, NT, E, E], where=sub)
        with ExitStack() as part:
            w2_h = sb("w2_h", [P, E, FH1], where=part)
            w2_l = sb("w2_l", [P, E, FH1], where=part)
            b1 = sb("b1", [P, UNITS], where=part)
            b2 = sb("b2", [P, E], where=part)
            f = sb("f", [P, 4, BLK], where=part)
            f_h = sb("f_h", [P, 4, BLK], where=part)
            f_l = sb("f_l", [P, 4, BLK], where=part)
            gate_b = sb("gate_b", [P, E, BLK], where=part)
            yt = sb("yt", [P, 2, BLK], where=part)
            acc = sb("acc", [P, BLK], where=part)
        era.close()

        ps = ctx.enter_context(nc.psum_tensor("ps", [P, 8, 512], F32))

        x_in = [sem(f"x_in{c}") for c in range(LN0)]
        w_in, late_in = sem("w_in"), sem("late_in")
        zeroed = sem("zeroed")
        consts_ready = sem("consts_ready")
        stats_done = sem("stats_done")
        moments_done = sem("moments_done")
        var_ready = sem("var_ready")
        std_ready = sem("std_ready")
        rstd_ready = sem("rstd_ready")
        xn_ready = sem("xn_ready")
        xn_kept = sem("xn_kept")
        tr_done = sem("tr_done")
        xT_done = sem("xT_done")
        q_mm, k_mm, v_mm = sem("q_mm"), sem("k_mm"), sem("v_mm")
        q_hi, k_hi = sem("q_hi"), sem("k_hi")
        q_res, k_res = sem("q_res"), sem("k_res")
        q_mid, k_mid = sem("q_mid"), sem("k_mid")
        q_lo, k_lo = sem("q_lo"), sem("k_lo")
        v_put, lg_put = sem("v_put"), sem("lg_put")
        q_stored = [sem(f"q_stored{u}") for u in range(2)]
        k_stored = [sem(f"k_stored{u}") for u in range(2)]
        stack_in = [sem(f"stack_in{r}") for r in range(PAIRS)]
        s_done, max_done, mtr_done, mneg_done = sem("s_done"), sem("max_done"), sem("mtr_done"), sem("mneg_done")
        mrow_in = [sem(f"mrow_in{r}") for r in range(4)]
        st_done, exp_done, pv_done, o_evac = sem("st_done"), sem("exp_done"), sem("pv_done"), sem("o_evac")
        o_moved = [sem(f"o_moved{r}") for r in range(4)]
        v_here = sem("v_here")
        wv_in = [sem(f"wv_in{u}") for u in range(2)]
        den_in, rden_done, rden_out = sem("den_in"), sem("rden_done"), sem("rden_out")
        wvn_done, wo_mm, at_put, x_attn, x1_done = (sem(n) for n in ("wvn_done", "wo_mm", "at_put", "x_attn", "x1_done"))
        out_done = sem("out_done")
        scattered, expert_rows, xgt_mm, xgt_put = (sem(n) for n in ("scattered", "expert_rows", "xgt_mm", "xgt_put"))
        up_mm, sig_done, gate_s, gated, down_mm, y_put = (sem(n) for n in ("up_mm", "sig_done", "gate_s", "gated", "down_mm", "y_put"))
        routed, counted, indexed, pick_d, pick_e = (sem(n) for n in ("routed", "counted", "indexed", "pick_d", "pick_e"))
        gathered = [sem(f"gathered{u}") for u in range(2)]
        x1_half = sem("x1_half")

        xh_put, xl_put = sem("xh_put"), sem("xl_put")
        x_kept = [sem(f"x_kept{u}") for u in range(2)]
        q1_mm, k1_mm, p1_mm, q1_scaled, k1_scaled = (sem(n) for n in ("q1_mm", "k1_mm", "p1_mm", "q1_scaled", "k1_scaled"))
        q1_hi, k1_hi, q1_res, k1_res, q1_mid, k1_mid, q1_lo, k1_lo = (
            sem(n) for n in ("q1_hi", "k1_hi", "q1_res", "k1_res", "q1_mid", "k1_mid", "q1_lo", "k1_lo"))
        q1_stored = [sem(f"q1_stored{u}") for u in range(2)]
        k1_stored = [sem(f"k1_stored{u}") for u in range(2)]
        v1_put, sg_put, lg1_put, sg_done = (sem(n) for n in ("v1_put", "sg_put", "lg1_put", "sg_done"))
        stack1_in = [sem(f"stack1_in{r}") for r in range(PAIRS)]
        s1_done, masked, copied, v1_here, pv1_done, o1_evac, turned1, ret_put = (
            sem(n) for n in ("s1_done", "masked", "copied", "v1_here", "pv1_done", "o1_evac", "turned1", "ret_put"))
        ss_done, sd_done, z_a, z_b, z_done, zt_mm, zt_put = (
            sem(n) for n in ("ss_done", "sd_done", "z_a", "z_b", "z_done", "zt_mm", "zt_put"))
        gates_done, gt_mm, gt_put, gates_out = (
            sem(n) for n in ("gates_done", "gt_mm", "gt_put", "gates_out"))
        gate_in = [sem(f"gate_in{e}") for e in range(E)]
        raw_in = [sem(f"raw_in{u}") for u in range(2)]
        w1_hi, w1_lo, w2_hi, w2_lo = (sem(n) for n in ("w1_hi", "w1_lo", "w2_hi", "w2_lo"))
        h_mm, f_done, f_hi, y_mm, yv, summed, acc_turned, x2_done = (
            sem(n) for n in ("h_mm", "f_done", "f_hi", "y_mm", "yv", "summed", "acc_turned", "x2_done"))
        f_lo = [sem("f_lo_even"), sem("f_lo_odd")]

        CREDIT = 2
        credits = [q_res, k_res, q_lo, k_lo, v_mm, lg_put,
                   xl_put, q1_scaled, k1_scaled, p1_mm, q1_res, k1_res, q1_lo, k1_lo, sg_done]
        singles = [lg1_put]

        block = ctx.enter_context(nc.Block())

        def num(g): return g[0] * RING + g[1]
        def div(g, by): return g[0] * (RING // by) + g[1] // by
        def plus(g, k): return g[0], g[1] + k
        def at(g, size): return g[1] % size

        def known(g): return isinstance(g[0], int)

        def run_slots(eng, total, slot, middle=None, peel=1, tail=0):
            for n in range(peel * RING):
                slot((0, n))
            last = total // RING - 1
            stretches = [(peel, last)] if middle is None else [(peel, MIDDLE), (MIDDLE, MIDDLE + 1), (MIDDLE + 1, last)]
            for k, (first, end) in enumerate(stretches):
                if k == 1:
                    middle()
                with eng.Fori(first, end) as i:
                    for r in range(RING):
                        slot((i, r), late=k == 2)
            for n in range(total - RING, total + tail):
                slot((0, n), late=True)

        def half_ring(g, after):
            return (g[1] - after) // 2 % 2

        def past(g, n):
            return not known(g) or num(g) >= n

        def due(g, after):
            if (g[1] - after) % 2 or not past(g, after) or known(g) and num(g) - after >= 2 * B:
                return None
            return div(plus(g, -after), 2)

        def within(g, total):
            return not known(g) or num(g) < total

        def known_block(j): return j if isinstance(j, int) else None

        def run_blocks(eng, body):
            body(0)
            with eng.Fori(1, NB - 1) as j:
                body(j)
            body(NB - 1)

        def r32(ap):
            return ap.bitcast(F32R)

        def run_pairs(eng, step, peel=0):
            for b in range(peel):
                step(b, b % 2)
            with eng.Fori(peel // 2, B // 2 - 1) as ii:
                for u in range(2):
                    step(ii * 2 + u, u)
            for u in range(2):
                step(B - 2 + u, u)

        def more(b, k):
            return not isinstance(b, int) or b + k < B

        def ps_t1(u): return ps[:, u, 0:S]
        def ps_q1(u): return ps[:, 2 + u, 0:S]
        def ps_k1(u): return ps[:, 4 + u, 0:S]
        def ps_p1(t): return ps[:, 6 + t, 0:PROJ1]
        p1_both = ps[:, 6:8, 0:PROJ1]
        def ps_sc(u, c): return ps[:, 3 * u + c, :]
        ps_o1 = ps[:, 6, 0:S]
        ps_at1 = ps[:, 6, S:2 * S]
        ps_r1 = ps[:, 7, 0:S]
        ps_zt = ps[:, 7, S:2 * S]
        TAIL1 = 7
        GATES = G1 - 5

        def ps_t(u): return ps[:, 4 * u, 0:S]
        def ps_q(u): return ps[:, 4 * u + 1, 0:S]
        def ps_k(u): return ps[:, 4 * u + 2, 0:S]
        def ps_v(u): return ps[:, 4 * u + 3, 0:TB * (D + E)].rearrange("p (t c) -> p t c", t=TB)
        def ps_s(c): return ps[:, c, :]
        def ps_st(c): return ps[:, 3 + c, :]
        ps_o = ps[:, 6, 0:S]
        ps_at = ps[:, 6, S:2 * S]
        ps_m = ps[0:2 * GH, 7, 0:P]

        q_rows = q_parts.rearrange("b i (d a h) t -> b (i d) a (h t)", d=HD0, a=2)
        k_rows = k_parts.rearrange("b j i (d a h) t -> b (j i d) a (h t)", d=HD0, a=2)

        @block.sync
        def _(sp):
            per = NT // LN0
            for c in range(LN0):
                sp.dma_start(x[:, c * per:(c + 1) * per, :], a["h"][:, c * per:(c + 1) * per, :]).then_inc(x_in[c], 16)
            for dst, name in ((tables[:, :, :], "tables"), (rank_e[:, :, :], "rank_e"), (w_o[:, :], "w_o"),
                              (w1_raw[:, :], "w1_raw"), (upto[:, :], "upto"), (w2_a[:, :], "w2_a"), (gn_w[:, :], "gn_w"),
                              (gn_b[:, :], "gn_b"), (rb1[:, :], "rb1")):
                sp.dma_start(dst, a[name]).then_inc(late_in, 16)

            def keep_parts(b, u):
                sp.wait_ge(q_lo, b + 1 + CREDIT)
                sp.dma_start(q_parts[ds(b, 1)].rearrange("o i p t -> p (o i) t"), qp[:, u, :, :]).then_inc(q_stored[u], 16)
                sp.wait_ge(k_lo, b + 1 + CREDIT)
                for i in range(3):
                    sp.dma_start(k_parts[ds(b, 1), :, i].rearrange("o j p t -> p (o j) t"), kp[:, u, :, :]).then_inc(k_stored[u], 16)
            keep_parts(0, 0)
            keep_parts(1, 1)
            sp.dma_start(w_up[:, :, :, :], a["w_up"]).then_inc(late_in, 16)
            sp.dma_start(w_dn[:, :, :, :], a["w_dn"]).then_inc(late_in, 16)
            with sp.Fori(1, B // 2) as ii:
                for u in range(2):
                    keep_parts(ii * 2 + u, u)
            for u in range(2):
                sp.wait_ge(q_stored[u], 16 * (B // 2 + 1))
                sp.wait_ge(k_stored[u], 48 * (B // 2 + 1))

            def load_pair(b, half, r):
                for st, rows in ((q_st, q_rows), (k_st, k_rows)):
                    src = rows[ds(b, 1), :, half, :].rearrange("o r c -> (o r) c")
                    if st is q_st:
                        src = src.unsqueeze(0).broadcast_to([3, 3 * HD0, 2 * GH * S])
                    sp.dma_start(st[0:R0, r, :, :].rearrange("p h t -> p (h t)"), src).then_inc(stack_in[r], 16)

            def move_max(g):
                r = at(g, RING)
                sp.wait_ge(mneg_done, num(g) + 1)
                sp.dma_start(q_st[R0:R0 + 1, r // 2, (r % 2) * GH:(r % 2) * GH + GH, :]
                             .rearrange("o h (t q) -> o (h t) q", t=TB),
                             m_neg[:, r % 4, :]).then_inc(mrow_in[r % 4], 16)

            def move_out(g):
                sp.wait_ge(o_evac, num(g) + 1)
                sp.dma_start(o_rows[ds(div(g, GPB0), 1), at(g, GPB0)].rearrange("o p t -> (o p) t"), o_ring[:, at(g, 4), :])\
                  .then_inc(o_moved[at(g, 4)], 16)

            def bring_back(b, u):
                for r in range(4):
                    sp.wait_ge(o_moved[r], b * 16 + 16)
                if not isinstance(b, int) or b >= 2:
                    sp.wait_ge(wvn_done, b - 1)
                sp.dma_start(den[:, :], o_heads[ds(b, 1), :, HD0, :].rearrange("o h (a t) -> (o h) a t", t=S * H0 // P)).then_inc(den_in, 16)
                sp.dma_start(wv_ring[:, u, :], o_heads[ds(b, 1), :, 0:HD0, :].rearrange("o h d t -> (o h) d t")).then_inc(wv_in[u], 16)

            def keep_inverse(b):
                sp.wait_ge(rden_done, b + 1)
                sp.dma_start(rden_rows[ds(b, 1)].rearrange("o h (a t) -> (o h) a t", t=S * H0 // P), rden[:, :]).then_inc(rden_out, 16)

            def spread_inverse(b, u):
                sp.wait_ge(rden_out, b * 16 + 16)
                sp.dma_start(rden_ring[:, u, :], rden_rows[ds(b, 1)].rearrange("o h t -> (o h) t").unsqueeze(1).broadcast_to([H0, HD0, S]))\
                  .then_inc(wv_in[u], 16)

            sp.wait_ge(zeroed, 6)
            for p in range(PAIRS):
                load_pair(p // 2, p % 2, p)
            for n in range(2):
                move_max((0, n))

            def slot(g, late=False):
                if within(plus(g, 2), G0):
                    move_max(plus(g, 2))
                if past(g, 1):
                    move_out(plus(g, -1))
                k, u = g[1] % GPB0, g[1] // GPB0 % 2
                if k == 2 and past(g, 6):
                    bring_back(div(plus(g, -6), GPB0), 1 - u)
                if k == 0 and past(g, 8):
                    keep_inverse(div(plus(g, -8), GPB0))
                if k == 1 and past(g, 9):
                    spread_inverse(div(plus(g, -9), GPB0), u)
                if g[1] % 2 == 1 and within(plus(g, 7), G0):
                    far = plus(g, 7)
                    sp.wait_ge(st_done, num(g) + 1)
                    load_pair(div(far, GPB0), at(far, GPB0) // 2, at(far, RING) // 2)
            run_slots(sp, G0, slot, lambda: None, peel=2)
            move_out((0, G0 - 1))
            keep_inverse(B - 2)
            spread_inverse(B - 2, 0)
            bring_back(B - 1, 1)
            keep_inverse(B - 1)
            spread_inverse(B - 1, 1)

            sp.wait_ge(x1_done, 8)
            sp.dma_start(gam[:, :, :], a["gam"]).then_inc(late_in, 16)

            def keep_parts1(b, u):
                sp.wait_ge(xl_put, b + 1 + CREDIT)
                for src, dst in ((xr_h, xh), (xr_l, xl)):
                    sp.dma_start(dst[:, ds(b * S, S)], src[:, u, :]).then_inc(x_kept[u], 16)
                sp.wait_ge(q1_lo, b + 1 + CREDIT)
                sp.dma_start(q_parts[ds(b, 1)].rearrange("o i p t -> p (o i) t"), q1_p[:, u, :, :]).then_inc(q1_stored[u], 16)
                sp.wait_ge(k1_lo, b + 1 + CREDIT)
                for i, parts in enumerate((3, 3, 2)):
                    sp.dma_start(k_parts[ds(b, 1), 0:parts, i].rearrange("o j p t -> p (o j) t"), k1_p[:, u, 0:parts, :]).then_inc(k1_stored[u], 16)
            run_pairs(sp, keep_parts1)
            for u in range(2):
                sp.wait_ge(q1_stored[u], 16 * (B // 2 + 1))
                sp.wait_ge(k1_stored[u], 48 * (B // 2 + 1))
                sp.wait_ge(x_kept[u], 32 * (B // 2 + 1))
            sp.wait_ge(sg_done, B + CREDIT)
            q1_rows = q_parts.rearrange("b i (d h) t -> b (i d) (h t)", d=HD1)
            k1_rows = k_parts.rearrange("b j i (d h) t -> b (j i d) (h t)", d=HD1)

            def load_sequence(b, r):
                src, rows = q1_rows[ds(b, 1)].rearrange("o r c -> (o r) c"), 3 * HD1
                sp.dma_start(q1_st[0:2 * rows, r, :, :].rearrange("p h t -> p (h t)"),
                             src.unsqueeze(0).broadcast_to([2, rows, H1 * S])).then_inc(stack1_in[r], 16)
                sp.dma_start(q1_st[2 * rows:R1, r, :, :].rearrange("p h t -> p (h t)"), src[0:R1 - 2 * rows]).then_inc(stack1_in[r], 16)
                sp.dma_start(k1_st[:, r, :, :].rearrange("p h t -> p (h t)"), k1_rows[ds(b, 1), 0:R1].rearrange("o r c -> (o r) c"))\
                  .then_inc(stack1_in[r], 16)
            for b in range(PAIRS):
                load_sequence(b, b)

            def slot(g, late=False):
                if g[1] % 2 == 1 and within(plus(g, 7), G1):
                    far = plus(g, 7)
                    sp.wait_ge(s1_done, num(g) + 1)
                    load_sequence(div(far, 2), at(far, RING) // 2)
                if g[1] % 4 == 3 and past(g, 7) and within(plus(g, 8), G1 + 7):
                    e = div(plus(g, 1), 4)
                    sp.wait_ge(w1_lo, e - 1)
                    load_raw("w1_e", e, g[1] // 4 % 2 ^ 1)

            def load_raw(name, e, u):
                sp.dma_start(w_raw[:, u, :], a[name][:, ds(e, 1), :].rearrange("p o f -> p (o f)")).then_inc(raw_in[u], 16)
            for u in range(2):
                load_raw("w1_e", u, u)
            run_slots(sp, G1, slot)
            for u in range(2):
                sp.wait_ge(w1_lo, E - 1 + u)
                load_raw("w2_e", u, u)

            sp.wait_ge(gt_put, 1)
            for c in range(2):
                sp.dma_start(gate_rows[:, c * N // 2:(c + 1) * N // 2].rearrange("e (t k) -> t e k", k=P), gT[:, c * P:(c + 1) * P])\
                  .then_inc(gates_out, 16)
            sp.wait_ge(gates_out, 32)
            sp.wait_ge(x_attn, 2 * B)

            def load_gate(j, e):
                sp.dma_start(gate_b[:, e, :], gate_rows[e:e + 1, ds(j * BLK, BLK)].broadcast_to([P, BLK])).then_inc(gate_in[e], 16)

            def store(j):
                sp.wait_ge(x2_done, j + 1)
                sp.dma_start(out[ds(j * BLK, BLK)].rearrange("(t p) d -> p t d", p=P), x[:, ds(j * TPB, TPB), :]).then_inc(out_done, 16)
            sp.dma_start(b1[:, :], a["b1"]).then_inc(late_in, 16)
            sp.dma_start(b2[:, :], a["b2"]).then_inc(late_in, 16)
            for e in range(E):
                load_gate(0, e)

            def body(j):
                for e in range(-2, E):
                    if known_block(j) == 0 and e + 4 < E:
                        sp.wait_ge(w2_lo, e + 3)
                        load_raw("w2_e", e + 4, e % 2)
                    if e < 0:
                        continue
                    if known_block(j) != NB - 1:
                        sp.wait_ge(yv, j * E + e + 1)
                        load_gate(j + 1, e)
                    if e == 2 and known_block(j) != 0:
                        store(j - 1)
            run_blocks(sp, body)
            store(NB - 1)
            sp.wait_ge(out_done, 16 * NB)

        @block.gpsimd
        def _(pool):
            for s in credits:
                pool.sem_inc(s, CREDIT)
            for s in singles:
                pool.sem_inc(s, 1)
            for u in range(2):
                pool.sem_inc(q_stored[u], 16)
                pool.sem_inc(k_stored[u], 48)
                pool.sem_inc(q1_stored[u], 16)
                pool.sem_inc(k1_stored[u], 48)
                pool.sem_inc(x_kept[u], 32)
            nc.gpsimd.memset(v_ring[:, :, :, :, :], 1.0).then_inc(zeroed, 1)
            nc.gpsimd.memset(ones_h[:, :], 1.0).then_inc(zeroed, 1)
            nc.gpsimd.memset(zero[:, :], 0.0).then_inc(zeroed, 1)
            nc.gpsimd.memset(ones_t[:, :], 1.0).then_inc(zeroed, 1)
            nc.gpsimd.memset(eps[:, :], EPS).then_inc(zeroed, 1)
            pool.wait_ge(zeroed, 5)
            nc.gpsimd.memset(k_st[64:P, :, :, :], 1.0).then_inc(zeroed, 1)
            pool.wait_ge(zeroed, 6)

            def last_parts0(b, u):
                pool.wait_ge(xn_ready, (b + 1) * TB)
                nc.gpsimd.tensor_copy(xn[:, ds(b * TB, TB), :], xn_ring[:, u, :, :]).then_inc(xn_kept, 1)
                pool.wait_ge(q_mid, b + 1)
                nc.gpsimd.tensor_tensor(qp[:, u, 2, :], q_rest[:, u, :], qp[:, u, 1, :], ALU.subtract).then_inc(q_lo, 1)
                pool.wait_ge(k_mid, b + 1)
                nc.gpsimd.tensor_tensor(kp[:, u, 2, :], k_rest[:, u, :], kp[:, u, 1, :], ALU.subtract).then_inc(k_lo, 1)
            run_pairs(pool, last_parts0)
            pool.dma_start(x_slots.rearrange("(c p) d -> p c d", p=P),
                           zero[:, :].unsqueeze(1).broadcast_to([P, SLOTS // P, D])).then_inc(scattered, 16)
            pool.dma_start(y_slots[SLOTS:SLOTS + P], zero[:, :]).then_inc(scattered, 16)

            def put_values(b, u):
                for t in range(TB):
                    last = nc.gpsimd.tensor_copy(v_ring[:, u, t, :, 0:HD0],
                                                 v_all[:, ds(b * TB + t, 1), :, :].rearrange("p o h d -> p (o h) d"))
                last.then_inc(v_here, 1)
            pool.wait_ge(v_put, B)
            for u in range(2):
                put_values(u, u)

            def scatter(k):
                for t in range(k * NT // 8, (k + 1) * NT // 8):
                    for c in range(2):
                        pool.indirect_dma_start(out=x_slots, out_offset=bass.IndirectOffsetOnAxis(ap=slot_in[:, c, t:t + 1], axis=0),
                                                in_=xn[:, t, :], in_offset=None, bounds_check=SLOTS - 1, oob_is_err=False)\
                            .then_inc(scattered, 16)

            def gather(k):
                if k >= 2:
                    pool.wait_ge(gathered[k % 2], k // 2 * 16 * 2 * NT // 8)
                for t in range(k * NT // 8, (k + 1) * NT // 8):
                    for c in range(2):
                        pool.indirect_dma_start(out=(xn, y_more)[c][:, t, :], out_offset=None, in_=y_slots,
                                                in_offset=bass.IndirectOffsetOnAxis(ap=slot_out[:, c, t:t + 1], axis=0))\
                            .then_inc(gathered[k % 2], 16)

            pool.wait_ge(indexed, 2)
            pool.wait_ge(scattered, 32)
            pool.wait_ge(xn_kept, B)
            scatter(0)
            for b in range(B - 1):
                if b + 2 < B:
                    pool.wait_ge(pv_done, (b + 1) * GPB0)
                    put_values(b + 2, b % 2)
                if b < 7:
                    scatter(b + 1)
                if b == 6:
                    pool.wait_ge(scattered, 32 + 16 * 2 * NT)
                    pool.dma_start(xg, x_slots.rearrange("(c p) d -> p c d", p=P)).then_inc(expert_rows, 16)
                if b == 8:
                    pool.wait_ge(y_put, E)
                    pool.dma_start(y_slots[0:SLOTS].rearrange("(c p) d -> p c d", p=P), y_sb).then_inc(expert_rows, 16)
                    pool.wait_ge(expert_rows, 32)
                    pool.wait_ge(xgt_put, SLOTS // 512)
                    gather(0)
                if 8 <= b < 15:
                    gather(b - 7)

            def last_parts(b, u):
                for mid, lo, rest, part in ((q1_mid, q1_lo, q1_rest, q1_p), (k1_mid, k1_lo, k1_rest, k1_p)):
                    pool.wait_ge(mid, b + 1)
                    nc.gpsimd.tensor_tensor(part[:, u, 2, :], rest[:, u, :], part[:, u, 1, :], ALU.subtract).then_inc(lo, 1)
                pool.wait_ge(sg_put, b + 1)
                nc.gpsimd.tensor_tensor(sg[:, ds(b * TB, TB), :], sg[:, ds(b * TB, TB), :],
                                        gn_b[:, :].unsqueeze(1).broadcast_to([P, TB, D]), ALU.add).then_inc(sg_done, 1)
            run_pairs(pool, last_parts)

            def values(b, u):
                nc.gpsimd.tensor_copy(v1_ring[:, u, :, :, :], v1[:, ds(b * TB, TB), :, :]).then_inc(v1_here, 1)
            pool.wait_ge(v1_put, 2 * B)
            pool.wait_ge(sg_done, B + CREDIT)
            for u in range(2):
                pool.wait_ge(q1_stored[u], 16 * (B // 2 + 1))
                pool.wait_ge(k1_stored[u], 48 * (B // 2 + 1))
                pool.wait_ge(x_kept[u], 32 * (B // 2 + 1))
            for u in range(2):
                values(u, u)

            def step(b, u):
                if more(b, 2):
                    pool.wait_ge(pv1_done, b * 2 + 2)
                    values(b + 2, u % 2)
                if more(b, -1) and (not isinstance(b, int) or b >= 1):
                    pool.wait_ge(z_a, b)
                    tiles = z[:, 1 - u % 2, :, :]
                    nc.gpsimd.tensor_tensor(tiles, tiles, gn_w[:, :].unsqueeze(1).broadcast_to([P, TB, D]), ALU.mult).then_inc(z_b, 1)
                    pool.wait_ge(z_b, b)
                    nc.gpsimd.tensor_tensor(tiles, tiles, sg[:, ds((b - 1) * TB, TB), :], ALU.add).then_inc(z_done, 1)
                if u % 2 == 0 and more(b, 0):
                    e = b // 2 if isinstance(b, int) else halves[0] * 2 + u // 2
                    pool.wait_ge(w1_hi, e + 1)
                    nc.gpsimd.tensor_tensor(r32(w1_l[:, ds(e, 1), :].rearrange("p o f -> p (o f)")), w_raw[:, u // 2, :],
                                            w1_h[:, ds(e, 1), :].rearrange("p o f -> p (o f)"), ALU.subtract).then_inc(w1_lo, 1)
            halves = [0]
            for b in range(4):
                step(b, b)
            pool.wait_ge(gates_done, 1)
            nc.gpsimd.tensor_tensor(order[:, :, :, :], order[:, :, :, :], p1[:, :, :].unsqueeze(2).broadcast_to([P, NT, E, E]), ALU.mult)\
                .then_inc(gates_done, 1)
            with pool.Fori(1, 3) as ii:
                halves[0] = ii
                for u in range(4):
                    step(ii * 4 + u, u)
            for b in range(12, B + 1):
                step(b, b % 4)

            def low_w2(e):
                pool.wait_ge(w2_hi, e + 1)
                nc.gpsimd.tensor_tensor(r32(w2_l[:, e, :]), w_raw[:, e % 2, :], w2_h[:, e, :], ALU.subtract).then_inc(w2_lo, 1)

            def add_expert(j, e):
                pool.wait_ge(yv, j * E + e + 1)
                if e:
                    if e > 1:
                        pool.wait_ge(summed, j * (E - 1) + e - 1)
                    nc.gpsimd.tensor_tensor(acc[:, :], acc[:, :], yt[:, e % 2, :], ALU.add).then_inc(summed, 1)
            low_w2(0)
            low_w2(1)

            def body(j):
                for m in range(1, UNITS, 2):
                    if known_block(j) == 0 and m % FC == 1 and m // FC + 2 < E:
                        low_w2(m // FC + 2)
                    n = j * UNITS + m
                    pool.wait_ge(f_hi, n + 1)
                    if known_block(j) != 0 or m >= 4:
                        pool.wait_ge(y_mm, n - 3)
                    nc.gpsimd.tensor_tensor(r32(f_l[:, m % 4, :]), f[:, m % 4, :], f_h[:, m % 4, :], ALU.subtract).then_inc(f_lo[1], 1)
                    if m % FC == 3:
                        if m >= 7:
                            add_expert(j, (m - 7) // FC)
                        elif known_block(j) != 0:
                            add_expert(j - 1, E - 1)
            run_blocks(pool, body)
            add_expert(NB - 1, E - 1)

        @block.scalar
        def _(act):
            for dst, name in ((ident[:, :], "ident"), (w_q[:, :], "w_q"), (w_k[:, :], "w_k"), (w_vr[:, :], "w_vr"), (rb0[:, :], "rb0")):
                act.dma_start(dst, a[name]).then_inc(w_in, 16)

            def deviation(c):
                act.wait_ge(var_ready, c + 1)
                tiles = slice(c * NT // LN0, (c + 1) * NT // LN0)
                nc.scalar.activation(std[:, tiles], var[:, tiles], ACT.Sqrt).then_inc(std_ready, 1)

            def turn_x(b, u):
                act.wait_ge(tr_done, b + 1)
                act.wait_ge(v_mm, b + 1)
                nc.scalar.activation(xT[:, u, :], ps_t(u), ACT.Copy).then_inc(xT_done, 1)

            def parts0(b, u):
                if more(b, 1):
                    turn_x(b + 1, 1 - u)
                for mm, hi, bank, part, stored, n in ((q_mm, q_hi, ps_q, qp, q_stored, 16), (k_mm, k_hi, ps_k, kp, k_stored, 48)):
                    act.wait_ge(mm, b + 1)
                    act.wait_ge(stored[u], pair_of(b, u) * n + n)
                    nc.scalar.activation(part[:, u, 0, :], bank(u), ACT.Copy).then_inc(hi, 1)
                act.wait_ge(v_mm, b + 1 + CREDIT)
                nc.scalar.activation(v_all[:, ds(b * TB, TB), :, :].rearrange("p t h d -> p t (h d)"),
                                     ps_v(u)[:, :, 0:D], ACT.Copy).then_inc(v_put, 1)
                for res, mid, rest, part in ((q_res, q_mid, q_rest, qp), (k_res, k_mid, k_rest, kp)):
                    act.wait_ge(res, b + 1 + CREDIT)
                    nc.scalar.activation(part[:, u, 1, :], rest[:, u, :], ACT.Copy).then_inc(mid, 1)
                if isinstance(b, int) and b + 1 < LN0:
                    deviation(b + 1)

            def pair_of(b, u):
                return b // 2 if isinstance(b, int) else pair[0]
            pair = [0]
            deviation(0)
            turn_x(0, 0)
            for b in range(LN0):
                parts0(b, b % 2)
            with act.Fori(LN0 // 2, B // 2 - 1) as ii:
                pair[0] = ii
                for u in range(2):
                    parts0(ii * 2 + u, u)
            for u in range(2):
                parts0(B - 2 + u, u)

            def negate_max(g):
                act.wait_ge(mtr_done, num(g) + 1)
                if past(g, 4):
                    act.wait_ge(mrow_in[at(g, 4)], div(g, 4) * 16)
                nc.scalar.activation(m_neg[:, at(g, 4), :], ps_m, ACT.Copy, scale=-1.0).then_inc(mneg_done, 1)

            def put_attention(b, u):
                act.wait_ge(wo_mm, b + 1)
                if not isinstance(b, int) or b >= 2:
                    act.wait_ge(x_attn, b - 1)
                nc.scalar.activation(at_ring[:, u, :, :].rearrange("p t c -> p (t c)"), ps_at, ACT.Copy).then_inc(at_put, 1)

            def evacuate(g):
                act.wait_ge(pv_done, num(g) + 1)
                if past(g, 4):
                    act.wait_ge(o_moved[at(g, 4)], div(g, 4) * 16)
                nc.scalar.activation(o_ring[:, at(g, 4), :], ps_o, ACT.Copy).then_inc(o_evac, 1)

            for n in range(2):
                negate_max((0, n))

            def slot(g, late=False):
                if within(plus(g, 2), G0):
                    negate_max(plus(g, 2))
                act.wait_ge(st_done, num(g) + 1)
                if past(g, 2):
                    act.wait_ge(pv_done, num(g) - 1)
                nc.scalar.activation(probs[:, at(g, 2), :, :], ps[:, 3:6, :], ACT.Exp, scale=float(D) ** -0.5)\
                  .then_inc(exp_done, 1)
                if past(g, 1):
                    evacuate(plus(g, -1))
                if g[1] % GPB0 == 2 and past(g, 14):
                    put_attention(div(plus(g, -14), GPB0), 1 - g[1] // GPB0 % 2)

            def middle():
                for c in range(SLOTS // 512):
                    act.wait_ge(xgt_mm, c + 1)
                    nc.scalar.activation(xgT[:, c * 512:(c + 1) * 512], ps[:, c, :], ACT.Copy).then_inc(xgt_put, 1)
                for e in range(E):
                    act.wait_ge(up_mm, e + 1)
                    if e >= 1:
                        act.wait_ge(gate_s, e)
                    nc.scalar.activation(act_s[:, :, :].rearrange("p c t -> p (c t)"), ps[:, 2 + e % 2, :], ACT.Sigmoid)\
                      .then_inc(sig_done, 1)
                    if e >= 1:
                        put_down(e - 1)
                put_down(E - 1)
                act.wait_ge(pick_d, 1)
                nc.scalar.activation(r_s[:, 1, 0, :], r_s[:, 0, 0, :], ACT.Exp).then_inc(pick_e, 1)

            def put_down(e):
                act.wait_ge(down_mm, e + 1)
                nc.scalar.activation(y_sb[:, 2 * e:2 * e + 2, :].rearrange("p c d -> p (c d)"), ps[:, 4 + e % 2, 0:2 * D], ACT.Copy)\
                  .then_inc(y_put, 1)
            run_slots(act, G0, slot, middle, peel=2)
            evacuate((0, G0 - 1))
            for b in range(B - 3, B):
                put_attention(b, b % 2)

            act.wait_ge(var_ready, LN0 + 1)
            nc.scalar.activation(std[:, :], var[:, :], ACT.Sqrt).then_inc(std_ready, 1)

            def high_x(b, u):
                act.wait_ge(tr_done, B + b + 1)
                act.wait_ge(p1_mm, b + 1)
                act.wait_ge(x_kept[u], half_of(b, u) * 32 + 32)
                nc.scalar.activation(r32(xr_h[:, u, :]), ps_t1(u), ACT.Copy).then_inc(xh_put, 1)

            def half_of(b, u):
                return b // 2 if isinstance(b, int) else halves[0] + (1 if u == 0 and halves[1] else 0)
            halves = [0, False]

            def parts(b, u, ii):
                if more(b, 1):
                    halves[:] = [ii, u == 1]
                    high_x(b + 1, 1 - u)
                for scaled, hi, src, part, stored, n in ((q1_scaled, q1_hi, q1_s, q1_p, q1_stored, 16),
                                                         (k1_scaled, k1_hi, k1_s, k1_p, k1_stored, 48)):
                    act.wait_ge(scaled, b + 1 + CREDIT)
                    act.wait_ge(stored[u], ii * n + n)
                    nc.scalar.activation(part[:, u, 0, :], src[:, u, :], ACT.Copy).then_inc(hi, 1)
                act.wait_ge(p1_mm, b + 1 + CREDIT)
                act.wait_ge(sg_done, b + 1)
                nc.scalar.activation(sig1[:, u, :, :], p1_both[:, :, D:2 * D], ACT.Sigmoid).then_inc(v1_put, 1)
                nc.scalar.activation(v1[:, ds(b * TB, TB), :, :].rearrange("p t h d -> p t (h d)"), p1_both[:, :, 0:D], ACT.Copy)\
                    .then_inc(v1_put, 1)
                for res, mid, rest, part in ((q1_res, q1_mid, q1_rest, q1_p), (k1_res, k1_mid, k1_rest, k1_p)):
                    act.wait_ge(res, b + 1 + CREDIT)
                    nc.scalar.activation(part[:, u, 1, :], rest[:, u, :], ACT.Copy).then_inc(mid, 1)
            high_x(0, 0)
            with act.Fori(0, B // 2 - 1) as ii:
                for u in range(2):
                    parts(ii * 2 + u, u, ii)
            for u in range(2):
                parts(B - 2 + u, u, B // 2 - 1)

            def put_heads(g):
                heads = ps_r1.rearrange("p (t h r) -> p t h r", t=TB, h=GH)[:, :, :, 0:HD1]
                act.wait_ge(turned1, num(g) + 1)
                if past(g, 8):
                    act.wait_ge(z_a, div(g, 2) - 3)
                nc.scalar.activation(ret[:, g[1] // 2 % 4, :, g[1] % 2 * GH * HD1:(g[1] % 2 + 1) * GH * HD1]
                                     .rearrange("p t (h d) -> p t h d", h=GH),
                                     heads, ACT.Copy)
                u = g[1] // 2 % 2
                if past(g, 4):
                    act.wait_ge(ss_done, div(g, 2) - 1)
                nc.scalar.activation(sq[:, u, :, g[1] % 2 * GH * HD1:(g[1] % 2 + 1) * GH * HD1]
                                     .rearrange("p t (h d) -> p t h d", h=GH), heads, ACT.Square).then_inc(ret_put, 1)

            def evacuate1(g):
                act.wait_ge(pv1_done, num(g) + 1)
                if past(g, 2):
                    act.wait_ge(turned1, num(g) - 1)
                nc.scalar.activation(o1_ring[:, at(g, 2), :], ps_o1, ACT.Copy).then_inc(o1_evac, 1)
            for u in range(2):
                act.wait_ge(q1_stored[u], 16 * (B // 2 + 1))
                act.wait_ge(k1_stored[u], 48 * (B // 2 + 1))
                act.wait_ge(x_kept[u], 32 * (B // 2 + 1))
            act.wait_ge(lg1_put, B + 1)

            def slot(g, late=False):
                u = at(g, 2)
                b = due(g, 5)
                if b is not None:
                    act.wait_ge(ss_done, b + 1)
                    if past(g, 9):
                        act.wait_ge(rden_done, B + b - 1)
                    nc.scalar.activation(sd1[:, half_ring(g, 5), :, :], ss1[:, half_ring(g, 5), :, :], ACT.Sqrt,
                                         bias=eps[:, 0:1], scale=1.0 / HD1).then_inc(sd_done, 1)
                if within(g, G1):
                    act.wait_ge(s1_done, num(g) + 1)
                    if past(g, 2):
                        act.wait_ge(pv1_done, num(g) - 1)
                    nc.scalar.activation(sc[:, u, 2, :], ps_sc(u, 2), ACT.Copy).then_inc(copied, 1)
                if past(g, 1) and within(plus(g, -1), G1):
                    evacuate1(plus(g, -1))
                b = due(g, 8)
                if b is not None:
                    act.wait_ge(wo_mm, B + b + 1)
                    if past(g, 12):
                        act.wait_ge(x_attn, B + b - 1)
                    nc.scalar.activation(at1_ring[:, half_ring(g, 8), :, :].rearrange("p t c -> p (t c)"), ps_at1, ACT.Copy).then_inc(at_put, 1)
                if known(g) and num(g) == GATES:
                    act.wait_ge(gt_mm, 1)
                    nc.scalar.activation(gT[:, :], ps_at1, ACT.Copy).then_inc(gt_put, 1)
                if past(g, 2) and within(plus(g, -2), G1):
                    put_heads(plus(g, -2))
                b = due(g, 7)
                if b is not None:
                    act.wait_ge(zt_mm, b + 1)
                    if past(g, 11):
                        act.wait_ge(wo_mm, B + b - 1)
                    nc.scalar.activation(zT[:, half_ring(g, 7), :], ps_zt, ACT.Copy).then_inc(zt_put, 1)
                if g[1] % 4 == 2 and within(g, G1):
                    e, v = div(g, 4), g[1] // 4 % 2
                    act.wait_ge(raw_in[v], div(g, RING) * 16 + 16)
                    nc.scalar.activation(r32(w1_h[:, ds(e, 1), :].rearrange("p o f -> p (o f)")), w_raw[:, v, :], ACT.Copy).then_inc(w1_hi, 1)
            act.wait_ge(pick_d, 2)
            nc.scalar.activation(p1_x[:, 1, :, :], p1_x[:, 0, :, :], ACT.Exp).then_inc(pick_e, 1)
            run_slots(act, G1, slot, tail=TAIL1)

            act.wait_ge(late_in, 14 * 16)
            act.wait_ge(x_attn, 2 * B)

            def body(j):
                for m in range(UNITS):
                    n = j * UNITS + m
                    act.wait_ge(h_mm, n + 1)
                    if known_block(j) != 0 or m >= 4:
                        act.wait_ge(f_hi, n - 3)
                        act.wait_ge(f_lo[m % 2], j * (UNITS // 2) + m // 2 - 1)
                    nc.scalar.activation(f[:, m % 4, :], ps[:, m % 4, :], ACT.Relu, bias=b1[:, m:m + 1]).then_inc(f_done, 1)
            run_blocks(act, body)

        @block.vector
        def _(dve):
            def moments_of(c):
                dve.wait_ge(x_in[c], 16)
                tiles = range(c * NT // LN0, (c + 1) * NT // LN0)
                for t in tiles:
                    nc.vector.bn_stats(stats[:, t, :], x[:, t, :]).then_inc(stats_done, 1)
                dve.wait_ge(stats_done, tiles.stop)
                for t in tiles:
                    nc.vector.bn_aggr(moments[:, t, :], stats[:, t, :]).then_inc(moments_done, 1)
                dve.wait_ge(moments_done, tiles.stop)
                nc.vector.tensor_scalar(var[:, tiles.start:tiles.stop], moments[:, tiles.start:tiles.stop, 1], EPS, None, ALU.add).then_inc(var_ready, 1)

            def scale_of(c):
                tiles = slice(c * NT // LN0, (c + 1) * NT // LN0)
                dve.wait_ge(std_ready, c + 1)
                nc.vector.reciprocal(rstd[:, tiles], std[:, tiles]).then_inc(rstd_ready, 1)
                dve.wait_ge(rstd_ready, c + 1)

            def normalise0(b, u):
                for v in range(TB):
                    t = b * TB + v
                    nc.vector.tensor_scalar(xn_ring[:, u, v, :], x[:, ds(t, 1), :].rearrange("p o c -> p (o c)"),
                                            moments[:, ds(t, 1), 0], rstd[:, ds(t, 1)], ALU.subtract, ALU.mult).then_inc(xn_ready, 1)

            def parts0(b, u):
                for hi, lo, part, rest, bank, res in ((q_hi, q_lo, qp, q_rest, ps_q, q_res), (k_hi, k_lo, kp, k_rest, ps_k, k_res)):
                    dve.wait_ge(hi, b + 1)
                    dve.wait_ge(lo, b + 1)
                    nc.vector.tensor_tensor(rest[:, u, :], bank(u), part[:, u, 0, :], ALU.subtract).then_inc(res, 1)
                if more(b, 2):
                    dve.wait_ge(tr_done, b + 1)
                    dve.wait_ge(xn_kept, b + 1)
                    normalise0(b + 2, u)
                dve.wait_ge(v_put, b + 1)
                nc.vector.tensor_tensor(logits0[:, ds(b * TB, TB), :], ps_v(u)[:, :, D:D + E],
                                        rb0[:, :].unsqueeze(1).broadcast_to([P, TB, E]), ALU.add).then_inc(lg_put, 1)
                if isinstance(b, int) and b + 1 < LN0:
                    moments_of(b + 1)
                    scale_of(b + 1)
                if isinstance(b, int) and b == LN0 - 1:
                    dve.wait_ge(late_in, 9 * 16)
                    for dst, src in ((ident_h, ident[:, :]), (mask_qk, tables[:, 0, :]), (mask_kq, tables[:, 1, :]), (before, tables[:, 2, :])):
                        nc.vector.tensor_copy(dst[:, :], src).then_inc(consts_ready, 1)
            moments_of(0)
            scale_of(0)
            normalise0(0, 0)
            normalise0(1, 1)
            dve.wait_ge(w_in, 5 * 16)
            run_pairs(dve, parts0, peel=LN0)

            step = [0]

            def then(instruction):
                step[0] += 1
                instruction.then_inc(routed, 1)
                dve.wait_ge(routed, step[0])
            by_expert = [P, NT, E]
            dve.wait_ge(lg_put, B + CREDIT)
            left = logits0
            for c in range(2):
                best = r_s[:, 2 + c, 0, :]
                then(nc.vector.tensor_reduce(best, left[:, :, :], AX.X, ALU.max))
                then(nc.vector.tensor_tensor(r_a[:, 0, :, :], left[:, :, :], best.unsqueeze(2).broadcast_to(by_expert), ALU.is_equal))
                then(nc.vector.tensor_tensor(r_a[:, 1, :, :], r_a[:, 0, :, :], rank_e[:, 1, :].unsqueeze(1).broadcast_to(by_expert), ALU.mult))
                then(nc.vector.tensor_reduce(r_s[:, 4, 0, :], r_a[:, 1, :, :], AX.X, ALU.max))
                then(nc.vector.tensor_tensor(picked[:, c, :, :], r_a[:, 1, :, :], r_s[:, 4, 0, :].unsqueeze(2).broadcast_to(by_expert), ALU.is_equal))
                if c == 0:
                    left = r_b[:, 0, :, :]
                    then(nc.vector.scalar_tensor_tensor(out=left, in0=picked[:, 0, :, :], scalar=-3e38, in1=logits0[:, :, :],
                                                        op0=ALU.mult, op1=ALU.add))
            nc.vector.tensor_tensor(chosen[:, :, :], picked[:, 0, :, :], picked[:, 1, :, :], ALU.add).then_inc(counted, 1)
            nc.vector.tensor_tensor(r_s[:, 0, 0, :], r_s[:, 3, 0, :], r_s[:, 2, 0, :], ALU.subtract).then_inc(pick_d, 1)
            dve.wait_ge(counted, 2)
            ahead, totals, so_far = r_b[:, 0, :, :], r_a[:, 0, :, :], r_a[:, 1, :, :]
            for n, dst in enumerate((ahead, totals)):
                last = nc.vector.tensor_copy(dst, ps[:, 0, n * NT * E:(n + 1) * NT * E].rearrange("p (t e) -> p t e", e=E))
            last.then_inc(counted, 1)
            place, expert, full, row, keep = (r_s[:, k, :, :] for k in (3, 4, 5, 6, 7))

            def count_ahead():
                dve.wait_ge(counted, 3)
                for e in range(E):
                    scan = nc.vector.tensor_tensor_scan(so_far[:, :, e], ones_t[:, :], totals[:, :, e], 0.0, ALU.mult, ALU.add)
                then(scan)
                then(nc.vector.tensor_tensor(r_b[:, 1, :, :], so_far, totals, ALU.subtract))
                then(nc.vector.tensor_tensor(rank[:, :, :], ahead, r_b[:, 1, :, :], ALU.add))

            def pick_places():
                for c in range(2):
                    nc.vector.tensor_tensor(r_a[:, c, :, :], picked[:, c, :, :], rank[:, :, :], ALU.mult)
                    last = nc.vector.tensor_tensor(r_b[:, c, :, :], picked[:, c, :, :], rank_e[:, 0, :].unsqueeze(1).broadcast_to(by_expert), ALU.mult)
                then(last)

            def index_in():
                nc.vector.tensor_reduce(place, r_a[:, :, :, :], AX.X, ALU.add)
                then(nc.vector.tensor_reduce(expert, r_b[:, :, :, :], AX.X, ALU.add))
                nc.vector.scalar_tensor_tensor(out=row, in0=expert, scalar=float(CAP), in1=place, op0=ALU.mult, op1=ALU.add)
                then(nc.vector.tensor_scalar(full, place, CAP - 0.5, float(2 * SLOTS), ALU.is_gt, ALU.mult))
                nc.vector.tensor_tensor(slot_in[:, :, :], row, full, ALU.add).then_inc(indexed, 1)

            def index_out():
                dve.wait_ge(indexed, 1)
                nc.vector.tensor_scalar(keep, place, CAP - 0.5, None, ALU.is_lt)
                then(nc.vector.tensor_scalar(full, row, float(-SLOTS), None, ALU.add))
                then(nc.vector.tensor_tensor(row, full, keep, ALU.mult))
                nc.vector.tensor_scalar(slot_out[:, :, :], row, float(SLOTS), None, ALU.add).then_inc(indexed, 1)

            def row_max(g):
                dve.wait_ge(s_done, num(g) + 1)
                if past(g, 2):
                    dve.wait_ge(mtr_done, num(g) - 1)
                nc.vector.tensor_reduce(m8[:, at(g, 2), :, 0], ps_s(0).rearrange("p (h k) -> p h k", h=GH), AX.X, ALU.max)
                nc.vector.tensor_reduce(m8[:, at(g, 2), :, 1], ps[:, 1:3, :].rearrange("p c (h k) -> p (c h) k", h=2),
                                        AX.X, ALU.max).then_inc(max_done, 1)
            for n in range(3):
                row_max((0, n))

            def slot(g, late=False):
                if within(plus(g, 3), G0):
                    row_max(plus(g, 3))
                if known(g) and num(g) == 0:
                    count_ahead()
                if known(g) and num(g) == 1:
                    pick_places()
                if known(g) and num(g) == 2:
                    index_in()
                if known(g) and num(g) == 3:
                    index_out()
                if g[1] % GPB0 == 3 and past(g, 7):
                    invert(div(plus(g, -7), GPB0))
                if g[1] % GPB0 == 3 and past(g, 11):
                    divide(div(plus(g, -11), GPB0), g[1] // GPB0 % 2)
                if g[1] % GPB0 == 3 and past(g, 15):
                    add_attention(div(plus(g, -15), GPB0), 1 - g[1] // GPB0 % 2)
                if late and g[1] % GPB0 == 1:
                    add_experts(div(plus(g, -(MIDDLE + 1) * RING), GPB0), g[1] // GPB0 % 2)

            def invert(b):
                dve.wait_ge(den_in, b * 16 + 16)
                if not isinstance(b, int) or b >= 1:
                    dve.wait_ge(rden_out, b * 16)
                nc.vector.reciprocal(rden[:, :], den[:, :]).then_inc(rden_done, 1)

            def divide(b, u):
                dve.wait_ge(wv_in[u], (b - u) * 16 + 32)
                if not isinstance(b, int) or b >= 2:
                    dve.wait_ge(wo_mm, b - 1)
                nc.vector.tensor_tensor(wvn[:, u, :], wv_ring[:, u, :], rden_ring[:, u, :], ALU.mult).then_inc(wvn_done, 1)

            def add_attention(b, u):
                dve.wait_ge(at_put, b + 1)
                tiles = x[:, ds(b * TB, TB), :]
                nc.vector.tensor_tensor(tiles, tiles, at_ring[:, u, :, :], ALU.add).then_inc(x_attn, 1)

            def add_experts(k, u):
                dve.wait_ge(x_attn, k * 2 + 2)
                dve.wait_ge(gathered[u], (k - u) * 64 + 128)
                for c, y in ((0, xn), (1, y_more)):
                    for v in range(NT // 8):
                        tile = ds(k * (NT // 8) + v, 1)
                        row = x[:, tile, :].rearrange("p o c -> p (o c)")
                        nc.vector.scalar_tensor_tensor(out=row, in0=y[:, tile, :].rearrange("p o c -> p (o c)"), scalar=pick_p[:, c, tile],
                                                       in1=row, op0=ALU.mult, op1=ALU.add).then_inc(x1_half, 1)
                    dve.wait_ge(x1_half, k * (NT // 4) + (c + 1) * (NT // 8))
                for v in range(NT // 8):
                    tile = ds(k * (NT // 8) + v, 1)
                    last = nc.vector.bn_stats(stats1[:, tile, :].rearrange("p o c -> p (o c)"), x[:, tile, :].rearrange("p o c -> p (o c)"))
                last.then_inc(x1_done, 1)

            def middle():
                for e in range(E):
                    dve.wait_ge(sig_done, e + 1)
                    if e >= 1:
                        dve.wait_ge(gated, e)
                    nc.vector.tensor_tensor(act_t[:, :, :].rearrange("p c t -> p (c t)"), ps[:, 2 + e % 2, :],
                                            act_s[:, :, :].rearrange("p c t -> p (c t)"), ALU.mult).then_inc(gate_s, 1)
                    dve.wait_ge(gate_s, e + 1)
                    if e >= 2:
                        dve.wait_ge(down_mm, e - 1)
                    nc.vector.tensor_tensor(act_g[:, e % 2, :, :].rearrange("p c t -> p (c t)"), ps[:, e % 2, :],
                                            act_t[:, :, :].rearrange("p c t -> p (c t)"), ALU.mult).then_inc(gated, 1)
                dve.wait_ge(pick_e, 1)
                then(nc.vector.tensor_scalar(r_s[:, 2, 0, :], r_s[:, 1, 0, :], 1.0, None, ALU.add))
                then(nc.vector.reciprocal(pick_p[:, 0, :], r_s[:, 2, 0, :]))
                then(nc.vector.tensor_tensor(pick_p[:, 1, :], r_s[:, 1, 0, :], pick_p[:, 0, :], ALU.mult))
                w_v = w1_raw[:, 2 * P:3 * P].rearrange("p (h d) -> p h d", h=H1)
                then(nc.vector.tensor_reduce(rb1_s[:, 0:H1], w_v, AX.X, ALU.add))
                then(nc.vector.scalar_tensor_tensor(out=w_v, in0=rb1_s[:, 0:H1].unsqueeze(2).broadcast_to([P, H1, HD1]), scalar=-1.0 / HD1,
                                                        in1=w_v, op0=ALU.mult, op1=ALU.add))
                for (hi, lo), src in ((w1_qk, w1_raw[:, 0:2 * P]), (w1_p, w1_raw[:, 2 * P:])):
                    then(nc.vector.tensor_copy(r32(hi[:, :]), src))
                    nc.vector.tensor_tensor(r32(lo[:, :]), src, hi[:, :], ALU.subtract).then_inc(consts_ready, 1)
            run_slots(dve, G0, slot, middle, peel=2)

            divide(B - 2, 0)
            add_attention(B - 3, 1)
            invert(B - 1)
            add_attention(B - 2, 0)
            add_experts(6, 0)
            divide(B - 1, 1)
            add_attention(B - 1, 1)
            add_experts(7, 1)

            dve.wait_ge(x1_done, 8)
            for t in range(NT):
                nc.vector.bn_aggr(moments[:, t, :], stats1[:, t, :]).then_inc(moments_done, 1)
            dve.wait_ge(moments_done, 2 * NT)
            nc.vector.tensor_scalar(var[:, :], moments[:, :, 1], EPS, None, ALU.add).then_inc(var_ready, 1)
            dve.wait_ge(std_ready, LN0 + 1)
            nc.vector.reciprocal(rstd[:, :], std[:, :]).then_inc(rstd_ready, 1)
            dve.wait_ge(rstd_ready, LN0 + 1)

            def normalise(b, u):
                for v in range(TB):
                    t = b * TB + v
                    nc.vector.tensor_scalar(xn1_ring[:, u, v, :], x[:, ds(t, 1), :].rearrange("p o c -> p (o c)"),
                                            moments[:, ds(t, 1), 0], rstd[:, ds(t, 1)], ALU.subtract, ALU.mult).then_inc(xn_ready, 1)

            def low_x(b, u):
                dve.wait_ge(xh_put, b + 1)
                nc.vector.tensor_tensor(r32(xr_l[:, u, :]), ps_t1(u), xr_h[:, u, :], ALU.subtract).then_inc(xl_put, 1)
            normalise(0, 0)
            normalise(1, 1)
            low_x(0, 0)
            dve.wait_ge(late_in, 12 * 16)

            def parts(b, u):
                for mm, res, src, bank, scaled, c in ((q1_mm, q1_res, q1_s, ps_q1, q1_scaled, 0), (k1_mm, k1_res, k1_s, ps_k1, k1_scaled, 1)):
                    dve.wait_ge(mm, b + 1)
                    dve.wait_ge(res, b + 1)
                    nc.vector.tensor_tensor(src[:, u, :], bank(u), gam[:, c, :], ALU.mult).then_inc(scaled, 1)
                if more(b, 1):
                    low_x(b + 1, 1 - u)
                if more(b, 2):
                    dve.wait_ge(tr_done, B + b + 1)
                    normalise(b + 2, u)
                for hi, lo, src, part, rest, res in ((q1_hi, q1_lo, q1_s, q1_p, q1_rest, q1_res), (k1_hi, k1_lo, k1_s, k1_p, k1_rest, k1_res)):
                    dve.wait_ge(hi, b + 1)
                    dve.wait_ge(lo, b + 1)
                    nc.vector.tensor_tensor(rest[:, u, :], src[:, u, :], part[:, u, 0, :], ALU.subtract).then_inc(res, 1)
                dve.wait_ge(v1_put, 2 * b + 2)
                nc.vector.tensor_tensor(sg[:, ds(b * TB, TB), :], p1_both[:, :, D:2 * D], sig1[:, u, :, :], ALU.mult).then_inc(sg_put, 1)
                nc.vector.tensor_tensor(logits1[:, ds(b * TB, TB), :], p1_both[:, :, 2 * D:PROJ1],
                                        rb1[:, :].unsqueeze(1).broadcast_to([P, TB, E]), ALU.add).then_inc(lg1_put, 1)
            run_pairs(dve, parts)

            for u in range(2):
                dve.wait_ge(q1_stored[u], 16 * (B // 2 + 1))
                dve.wait_ge(k1_stored[u], 48 * (B // 2 + 1))
                dve.wait_ge(x_kept[u], 32 * (B // 2 + 1))

            def slot(g, late=False):
                u = at(g, 2)
                if within(g, G1):
                    dve.wait_ge(s1_done, num(g) + 1)
                    if past(g, 2):
                        dve.wait_ge(pv1_done, num(g) - 1)
                    nc.vector.tensor_tensor(sc[:, u, 0:2, :].rearrange("p c (h t) -> p (c h) t", h=GH),
                                            ps[:, 3 * u:3 * u + 2, :].rearrange("p c (h t) -> p (c h) t", h=GH),
                                            upto[:, :].unsqueeze(1).broadcast_to([P, 2 * GH, P]), ALU.mult).then_inc(masked, 1)
                b, v = due(g, 4), half_ring(g, 4)
                if b is not None:
                    dve.wait_ge(ret_put, b * 2 + 2)
                    if past(g, 8):
                        dve.wait_ge(sd_done, b - 1)
                    nc.vector.tensor_reduce(ss1[:, v, :, :], sq[:, v, :, :].rearrange("p t (h d) -> p t h d", h=H1), AX.X, ALU.add)\
                        .then_inc(ss_done, 1)
                b, v = due(g, 5), half_ring(g, 5)
                if b is not None:
                    dve.wait_ge(sd_done, b + 1)
                    if past(g, 9):
                        dve.wait_ge(z_a, b - 1)
                        dve.wait_ge(zt_mm, b - 1)
                    nc.vector.reciprocal(rs1[:, v, :, :], sd1[:, v, :, :]).then_inc(rden_done, 1)
                    dve.wait_ge(rden_done, B + b + 1)
                    nc.vector.tensor_tensor(z[:, v, :, :].rearrange("p t (h d) -> p t h d", h=H1),
                                            ret[:, (g[1] - 5) // 2 % 4, :, :].rearrange("p t (h d) -> p t h d", h=H1),
                                            rs1[:, v, :, :].unsqueeze(3).broadcast_to([P, TB, H1, HD1]), ALU.mult).then_inc(z_a, 1)
                b, v = due(g, 8), half_ring(g, 8)
                if b is not None:
                    dve.wait_ge(at_put, B + b + 1)
                    tiles = x[:, ds(b * TB, TB), :]
                    nc.vector.tensor_tensor(tiles, tiles, at1_ring[:, v, :, :], ALU.add).then_inc(x_attn, 1)
                if known(g) and num(g) < E:
                    compare(num(g))
                if known(g) and num(g) == GATES - 3:
                    keep_experts()

            dve.wait_ge(lg1_put, B + 1)
            then(nc.vector.tensor_reduce(p1_s[:, 0, :], logits1[:, :, :], AX.X, ALU.max))
            nc.vector.tensor_tensor(p1_x[:, 0, :, :], logits1[:, :, :], p1_s[:, 0, :].unsqueeze(2).broadcast_to(by_expert), ALU.subtract)\
                .then_inc(pick_d, 1)
            dve.wait_ge(pick_e, 2)
            then(nc.vector.tensor_reduce(p1_s[:, 1, :], p1_x[:, 1, :, :], AX.X, ALU.add))
            then(nc.vector.reciprocal(p1_s[:, 2, :], p1_s[:, 1, :]))
            then(nc.vector.tensor_tensor(p1[:, :, :], p1_x[:, 1, :, :], p1_s[:, 2, :].unsqueeze(2).broadcast_to(by_expert), ALU.mult))

            def compare(j):
                if j:
                    nc.vector.tensor_tensor(order[:, :, 0:j, j], p1[:, :, j:j + 1].broadcast_to([P, NT, j]), p1[:, :, 0:j], ALU.is_gt)
                last = nc.vector.tensor_tensor(order[:, :, j:E, j], p1[:, :, j:j + 1].broadcast_to([P, NT, E - j]), p1[:, :, j:E], ALU.is_ge)
                if j == E - 1:
                    last.then_inc(gates_done, 1)

            def keep_experts():
                dve.wait_ge(gates_done, 2)
                up_to = p1_x[:, 0, :, :]
                then(nc.vector.tensor_reduce(up_to, order[:, :, :, :], AX.X, ALU.add))
                then(nc.vector.tensor_tensor(p1_x[:, 1, :, :], up_to, p1[:, :, :], ALU.is_equal))
                then(nc.vector.scalar_tensor_tensor(out=up_to, in0=up_to, scalar=TOP_P, in1=p1_x[:, 1, :, :], op0=ALU.is_lt, op1=ALU.max))
                nc.vector.tensor_tensor(gates[:, :, :], up_to, p1[:, :, :], ALU.mult).then_inc(gates_done, 1)
            run_slots(dve, G1, slot, tail=TAIL1)

            def split_weights(e):
                dve.wait_ge(raw_in[e % 2], E // 2 * 16 + e // 2 * 16 + 16)
                nc.vector.tensor_copy(r32(w2_h[:, e, :]), w_raw[:, e % 2, :]).then_inc(w2_hi, 1)

            def gate_expert(j, e):
                dve.wait_ge(y_mm, j * UNITS + e * FC + FC)
                dve.wait_ge(gate_in[e], j * 16 + 16)
                if e == 0:
                    if known_block(j) != 0:
                        dve.wait_ge(acc_turned, j)
                elif e >= 3:
                    dve.wait_ge(summed, j * (E - 1) + e - 2)
                elif known_block(j) != 0:
                    dve.wait_ge(summed, j * (E - 1))
                nc.vector.scalar_tensor_tensor(out=acc[:, :] if e == 0 else yt[:, e % 2, :], in0=ps[:, 4 + e % 2, :], scalar=b2[:, e:e + 1],
                                               in1=gate_b[:, e, :], op0=ALU.add, op1=ALU.mult).then_inc(yv, 1)

            def finish(j):
                dve.wait_ge(acc_turned, j + 1)
                tiles = x[:, ds(j * TPB, TPB), :]
                nc.vector.tensor_tensor(tiles, tiles, ps[:, 6, :].rearrange("p (t c) -> p t c", t=TPB), ALU.add).then_inc(x2_done, 1)
            dve.wait_ge(x_attn, 2 * B)
            split_weights(0)
            split_weights(1)
            dve.wait_ge(late_in, 14 * 16)

            def body(j):
                for m in range(UNITS):
                    if known_block(j) == 0 and m % FC == 0 and m // FC + 2 < E:
                        split_weights(m // FC + 2)
                    n = j * UNITS + m
                    dve.wait_ge(f_done, n + 1)
                    if known_block(j) != 0 or m >= 4:
                        dve.wait_ge(y_mm, n - 3)
                    nc.vector.tensor_copy(r32(f_h[:, m % 4, :]), f[:, m % 4, :]).then_inc(f_hi, 1)
                    if m % 2 == 0:
                        dve.wait_ge(f_hi, n + 1)
                        nc.vector.tensor_tensor(r32(f_l[:, m % 4, :]), f[:, m % 4, :], f_h[:, m % 4, :], ALU.subtract).then_inc(f_lo[0], 1)
                    if m % FC == 2:
                        if m >= 6:
                            gate_expert(j, (m - 6) // FC)
                        elif known_block(j) != 0:
                            gate_expert(j - 1, E - 1)
                    if m == 8 and known_block(j) != 0:
                        finish(j - 1)
            run_blocks(dve, body)
            gate_expert(NB - 1, E - 1)
            finish(NB - 1)

        @block.tensor
        def _(pe):
            def transposes0(b, u):
                pe.wait_ge(xn_ready, (b + 1) * TB)
                for t in range(TB):
                    last = nc.tensor.transpose(ps_t(u)[:, t * P:(t + 1) * P], xn_ring[:, u, t, :], ident[:, :])
                last.then_inc(tr_done, 1)

            def products0(b, u):
                pe.wait_ge(xT_done, b + 1)
                pe.wait_ge(q_res, b + 1)
                nc.tensor.matmul(ps_q(u), w_q[:, :], xT[:, u, :], start=True, stop=True).then_inc(q_mm, 1)
                pe.wait_ge(k_res, b + 1)
                nc.tensor.matmul(ps_k(u), w_k[:, :], xT[:, u, :], start=True, stop=True).then_inc(k_mm, 1)
                pe.wait_ge(lg_put, b + 1)
                for t in range(TB):
                    last = nc.tensor.matmul(ps_v(u)[:, t, :], xT[:, u, t * P:(t + 1) * P], w_vr[:, :], start=True, stop=True)
                last.then_inc(v_mm, 1)
                if more(b, 2):
                    transposes0(b + 2, u)
            pe.wait_ge(w_in, 5 * 16)
            transposes0(0, 0)
            transposes0(1, 1)
            run_pairs(pe, products0)
            pe.wait_ge(consts_ready, 4)

            pe.wait_ge(counted, 1)
            for n, lhs in enumerate((before, ones_h)):
                last = nc.tensor.matmul(ps[:, 0, n * NT * E:(n + 1) * NT * E], lhs[:, :], chosen[:, :, :].rearrange("p t e -> p (t e)"),
                                        start=True, stop=True)
            last.then_inc(counted, 1)
            pe.wait_ge(counted, 3)

            def scores(g):
                r = at(g, RING)
                qs, ks = (st[:, r // 2, (r % 2) * GH:(r % 2) * GH + GH, :] for st in (q_st, k_st))
                if r % 2 == 0:
                    pe.wait_ge(stack_in[r // 2], div(g, RING) * 32 + 32)
                if past(g, 1):
                    pe.wait_ge(max_done, num(g))
                nc.tensor.matmul(ps_s(0).rearrange("p (h k) -> p h k", h=GH), ident_h[:, :],
                                 mask_qk[:, :].unsqueeze(1).broadcast_to([P, GH, P]), start=True, stop=False, skip_group_check=True)
                for c in (1, 2):
                    nc.tensor.matmul(ps_s(c).rearrange("p (h k) -> p h k", h=2)[:, :, P:S], ident_h[:, :],
                                     mask_qk[:, :].unsqueeze(1).broadcast_to([P, 2, P]), start=True, stop=False, skip_group_check=True)
                for h in range(GH):
                    nc.tensor.matmul(ps_s(0)[:, h * P:(h + 1) * P], qs[0:R0, h, 0:P], ks[0:R0, h, 0:P],
                                     start=False, stop=True, skip_group_check=True)
                for h in range(GH):
                    last = nc.tensor.matmul(ps_s(1 + h // 2)[:, h % 2 * S:(h % 2 + 1) * S], qs[0:R0, h, P:S], ks[0:R0, h, :],
                                            start=False, stop=True, skip_group_check=True)
                last.then_inc(s_done, 1)

            def turn_max(g):
                pe.wait_ge(max_done, num(g) + 1)
                if past(g, 1):
                    pe.wait_ge(mneg_done, num(g))
                nc.tensor.transpose(ps_m, m8[:, at(g, 2), :, :].rearrange("p h t -> p (h t)"), ident[:, :]).then_inc(mtr_done, 1)

            def scores_t(g):
                r = at(g, RING)
                qs, ks = (st[0:R0 + 1, r // 2, (r % 2) * GH:(r % 2) * GH + GH, :] for st in (q_st, k_st))
                if past(g, 1):
                    pe.wait_ge(exp_done, num(g))
                nc.tensor.matmul(ps_st(0).rearrange("p (h k) -> p h k", h=GH), ident_h[:, :],
                                 mask_kq[:, :].unsqueeze(1).broadcast_to([P, GH, P]), start=True, stop=False, skip_group_check=True)
                for c in (1, 2):
                    nc.tensor.matmul(ps_st(c).rearrange("p (h k) -> p h k", h=2)[:, :, 0:P], ident_h[:, :],
                                     mask_kq[:, :].unsqueeze(1).broadcast_to([P, 2, P]), start=True, stop=False, skip_group_check=True)
                pe.wait_ge(mrow_in[r % 4], div(g, 4) * 16 + 16)
                for h in range(GH):
                    nc.tensor.matmul(ps_st(0)[:, h * P:(h + 1) * P], ks[:, h, P:S], qs[:, h, P:S],
                                     start=False, stop=True, skip_group_check=True)
                for h in range(GH):
                    last = nc.tensor.matmul(ps_st(1 + h // 2)[:, h % 2 * S:(h % 2 + 1) * S], ks[:, h, 0:P], qs[:, h, :],
                                            start=False, stop=True, skip_group_check=True)
                last.then_inc(st_done, 1)

            def weigh(g):
                k, u = at(g, GPB0), at(g, RING) // GPB0
                pe.wait_ge(exp_done, num(g) + 1)
                if k == 0:
                    pe.wait_ge(v_here, div(g, GPB0) + 1)
                if past(g, 1):
                    pe.wait_ge(o_evac, num(g))
                if k == 2 and past(g, 14):
                    pe.wait_ge(at_put, div(plus(g, -14), GPB0) + 1)
                for h in range(GH):
                    nc.tensor.matmul(ps_o[32 * h:32 * h + 2 * HD0, :], v_ring[:, u, 0, k * GH + h, :],
                                     probs[:, at(g, 2), 1 + h // 2, h % 2 * S:(h % 2 + 1) * S],
                                     start=True, stop=False, skip_group_check=True)
                for h in range(GH):
                    last = nc.tensor.matmul(ps_o[32 * h:32 * h + 2 * HD0, P:S], v_ring[:, u, 1, k * GH + h, :],
                                            probs[:, at(g, 2), 0, h * P:(h + 1) * P],
                                            start=False, stop=True, skip_group_check=True)
                last.then_inc(pv_done, 1)

            for n in range(3):
                scores((0, n))
                if n:
                    turn_max((0, n - 1))

            def slot(g, late=False):
                if within(plus(g, 3), G0):
                    scores(plus(g, 3))
                if within(plus(g, 2), G0):
                    turn_max(plus(g, 2))
                scores_t(g)
                if g[1] % GPB0 == 2 and past(g, 14):
                    pe.wait_ge(o_evac, num(g) - 1)
                    attention_out(div(plus(g, -14), GPB0), 1 - g[1] // GPB0 % 2)
                if past(g, 1):
                    weigh(plus(g, -1))

            def attention_out(b, u):
                pe.wait_ge(wvn_done, b + 1)
                for t in range(TB):
                    last = nc.tensor.matmul(ps_at[:, t * P:(t + 1) * P], wvn[:, u, t * P:(t + 1) * P], w_o[:, :], start=True, stop=True)
                last.then_inc(wo_mm, 1)

            def middle():
                n = MIDDLE * RING
                pe.wait_ge(late_in, 11 * 16)
                pe.wait_ge(expert_rows, 16)
                pe.wait_ge(max_done, n + 3)
                pe.wait_ge(exp_done, n)
                for c in range(SLOTS // P):
                    last = nc.tensor.transpose(ps[:, c // 4, c % 4 * P:(c % 4 + 1) * P], xg[:, c, :], ident[:, :])
                    if c % 4 == 3:
                        last.then_inc(xgt_mm, 1)
                pe.wait_ge(xgt_put, SLOTS // 512)

                def up(e):
                    if e >= 2:
                        pe.wait_ge(gated, e - 1)
                    for m, bank in ((0, e % 2), (1, 2 + e % 2)):
                        for c in range(2):
                            last = nc.tensor.matmul(ps[:, bank, c * CAP:(c + 1) * CAP], w_up[:, e, m, c * P:(c + 1) * P],
                                                    xgT[:, e * CAP:(e + 1) * CAP], start=True, stop=True)
                    last.then_inc(up_mm, 1)

                def down(e):
                    pe.wait_ge(gated, e + 1)
                    if e >= 2:
                        pe.wait_ge(y_put, e - 1)
                    for t in range(CAP // P):
                        for c in range(2):
                            last = nc.tensor.matmul(ps[:, 4 + e % 2, t * D:(t + 1) * D], act_g[:, e % 2, c, t * P:(t + 1) * P],
                                                    w_dn[:, e, c, :], start=(c == 0), stop=(c == 1))
                    last.then_inc(down_mm, 1)
                up(0)
                for e in range(E):
                    if e + 1 < E:
                        up(e + 1)
                    down(e)
                pe.wait_ge(y_put, E)
            run_slots(pe, G0, slot, middle, peel=2)
            weigh((0, G0 - 1))
            pe.wait_ge(o_evac, G0)
            for b in range(B - 3, B):
                attention_out(b, b % 2)
                pe.wait_ge(at_put, b + 1)

            def transposes(b, u):
                pe.wait_ge(xn_ready, (B + b + 1) * TB)
                pe.wait_ge(xl_put, b + 1)
                for t in range(TB):
                    last = nc.tensor.transpose(ps_t1(u)[:, t * P:(t + 1) * P], xn1_ring[:, u, t, :], ident[:, :])
                last.then_inc(tr_done, 1)

            def three(dst, lhs, rhs):
                for k, (i, j) in enumerate(((0, 0), (1, 0), (0, 1))):
                    last = nc.tensor.matmul(dst, r32(lhs[i]), r32(rhs[j]), start=(k == 0), stop=(k == 2))
                return last

            def products(b, u):
                pe.wait_ge(xl_put, b + 1 + CREDIT)
                rhs = (xr_h[:, u, :], xr_l[:, u, :])
                pe.wait_ge(q1_scaled, b + 1)
                three(ps_q1(u), [w[:, 0:P] for w in w1_qk], rhs).then_inc(q1_mm, 1)
                pe.wait_ge(k1_scaled, b + 1)
                three(ps_k1(u), [w[:, P:2 * P] for w in w1_qk], rhs).then_inc(k1_mm, 1)
                pe.wait_ge(lg1_put, b + 1)
                for t in range(TB):
                    last = three(ps_p1(t), [x_[:, t * P:(t + 1) * P] for x_ in rhs], [w[:, :] for w in w1_p])
                last.then_inc(p1_mm, 1)
            pe.wait_ge(consts_ready, 6)
            transposes(0, 0)
            transposes(1, 1)

            def step(b, u):
                products(b, u)
                if more(b, 2):
                    transposes(b + 2, u)
            run_pairs(pe, step)

            def scores1(g):
                r, u = at(g, RING), at(g, 2)
                qs, ks = (st[:, r // 2, u * GH:(u + 1) * GH, :] for st in (q1_st, k1_st))
                if r % 2 == 0:
                    pe.wait_ge(stack1_in[r // 2], div(g, RING) * 48 + 48)
                if past(g, 2):
                    pe.wait_ge(masked, num(g) - 1)
                    pe.wait_ge(copied, num(g) - 1)
                for c, (k, q) in enumerate(((1, 1), (0, 0), (0, 1))):
                    for h in range(GH):
                        last = nc.tensor.matmul(ps_sc(u, c)[:, h * P:(h + 1) * P], ks[:, h, k * P:(k + 1) * P], qs[:, h, q * P:(q + 1) * P],
                                                start=True, stop=True)
                last.then_inc(s1_done, 1)

            def weigh1(g):
                u, half = at(g, RING) // 2 % 2, g[1] % 2
                pe.wait_ge(masked, num(g) + 1)
                pe.wait_ge(copied, num(g) + 1)
                if half == 0:
                    pe.wait_ge(v1_here, div(g, 2) + 1)
                if past(g, 1):
                    pe.wait_ge(o1_evac, num(g))
                for h in range(GH):
                    nc.tensor.matmul(ps_o1[32 * h:32 * h + HD1, :].rearrange("p (c t) -> p c t", c=2), v1_ring[:, u, 0, half * GH + h, :],
                                     sc[:, at(g, 2), 1:3, h * P:(h + 1) * P], start=True, stop=False, skip_group_check=True)
                for h in range(GH):
                    last = nc.tensor.matmul(ps_o1[32 * h:32 * h + HD1, P:S], v1_ring[:, u, 1, half * GH + h, :],
                                            sc[:, at(g, 2), 0, h * P:(h + 1) * P], start=False, stop=True, skip_group_check=True)
                last.then_inc(pv1_done, 1)

            def turn1(g):
                pe.wait_ge(o1_evac, num(g) + 1)
                if past(g, 1):
                    pe.wait_ge(ret_put, num(g))
                for t in range(TB):
                    last = nc.tensor.transpose(ps_r1[:, t * P:(t + 1) * P], o1_ring[:, at(g, 2), t * P:(t + 1) * P], ident[:, :])
                last.then_inc(turned1, 1)

            pe.wait_ge(lg1_put, B + 1)

            def slot(g, late=False):
                if within(g, G1):
                    scores1(g)
                b = due(g, 8)
                if b is not None:
                    pe.wait_ge(o1_evac, G1 if not within(plus(g, -2), G1) else num(g) - 1)
                    pe.wait_ge(zt_put, b + 1)
                    if known(g) and num(g) == GATES + 1:
                        pe.wait_ge(gt_put, 1)
                    u = half_ring(g, 8)
                    for t in range(TB):
                        last = nc.tensor.matmul(ps_at1[:, t * P:(t + 1) * P], zT[:, u, t * P:(t + 1) * P], w2_a[:, :], start=True, stop=True)
                    last.then_inc(wo_mm, 1)
                b = due(g, 9)
                if b is not None:
                    pe.wait_ge(at_put, B + b + 1)
                if known(g) and num(g) == GATES:
                    pe.wait_ge(gates_done, 3)
                    pe.wait_ge(o1_evac, num(g) - 1)
                    for c in range(2):
                        last = nc.tensor.transpose(ps_at1[:, c * P:(c + 1) * P],
                                                   gates[:, c * NT // 2:(c + 1) * NT // 2, :].rearrange("p t e -> p (t e)"), ident[:, :])
                    last.then_inc(gt_mm, 1)
                if past(g, 1) and within(plus(g, -1), G1):
                    if known(g) and num(g) == GATES + 1:
                        pe.wait_ge(gt_put, 1)
                    weigh1(plus(g, -1))
                b = due(g, 7)
                if b is not None:
                    pe.wait_ge(z_done, b + 1)
                    pe.wait_ge(ret_put, G1 if not within(plus(g, -3), G1) else num(g) - 2)
                    for t in range(TB):
                        last = nc.tensor.transpose(ps_zt[:, t * P:(t + 1) * P], z[:, half_ring(g, 7), t, :], ident[:, :])
                    last.then_inc(zt_mm, 1)
                b = due(g, 8)
                if b is not None:
                    pe.wait_ge(zt_put, b + 1)
                if past(g, 2) and within(plus(g, -2), G1):
                    turn1(plus(g, -2))
            run_slots(pe, G1, slot, tail=TAIL1)

            def hidden(j, m):
                if m >= UNITS:
                    j, m = j + 1, m - UNITS
                n, (e, c) = j * UNITS + m, divmod(m, FC)
                if known_block(j) != 0 or m >= 4:
                    pe.wait_ge(f_done, n - 3)
                three(ps[:, m % 4, :], [w[:, e, c * P:(c + 1) * P] for w in (w1_h, w1_l)],
                      [x_[:, ds(j * BLK, BLK)] for x_ in (xh, xl)]).then_inc(h_mm, 1)

            def output(j, m):
                n, (e, c) = j * UNITS + m, divmod(m, FC)
                if c == 0:
                    if known_block(j) == 0:
                        pe.wait_ge(w2_lo, e + 1)
                    if known_block(j) != 0 or e >= 2:
                        pe.wait_ge(yv, j * E + e - 1)
                pe.wait_ge(f_lo[m % 2], j * (UNITS // 2) + m // 2 + 1)
                w = [w_[:, e, c * P:(c + 1) * P] for w_ in (w2_h, w2_l)]
                for k, (i, fs) in enumerate(((0, f_h), (1, f_h), (0, f_l))):
                    last = nc.tensor.matmul(ps[:, 4 + e % 2, :], r32(w[i]), r32(fs[:, m % 4, :]), start=(c == 0 and k == 0),
                                            stop=(c == FC - 1 and k == 2))
                last.then_inc(y_mm, 1)

            def turn_sum(j):
                pe.wait_ge(summed, (j + 1) * (E - 1))
                if known_block(j) != 0:
                    pe.wait_ge(x2_done, j)
                for t in range(TPB):
                    last = nc.tensor.transpose(ps[:, 6, t * P:(t + 1) * P], acc[:, t * P:(t + 1) * P], ident[:, :])
                last.then_inc(acc_turned, 1)
            pe.wait_ge(masked, G1)
            pe.wait_ge(copied, G1)
            pe.wait_ge(w1_lo, E)
            for m in range(AHEAD):
                hidden(0, m)

            def body(j):
                for m in range(UNITS):
                    if known_block(j) != NB - 1 or m + AHEAD < UNITS:
                        hidden(j, m + AHEAD)
                    output(j, m)
                    if m == 4 and known_block(j) != 0:
                        turn_sum(j - 1)
            run_blocks(pe, body)
            turn_sum(NB - 1)


_OUT = ((B, S, D), "float32")


def kernel(**inputs):
    import numpy as np
    import concourse.bacc as bacc
    from concourse.bass_utils import run_bass_kernel_spmd

    arrays = prepare(inputs, np)
    nc = bacc.Bacc("TRN2", target_bir_lowering=False, num_devices=1)
    aps = {k: nc.dram_tensor(f"in_{k}", v.shape, mybir.dt.from_np(v.dtype), kind="ExternalInput").ap() for k, v in arrays.items()}
    out = nc.dram_tensor("out_0", (N, D), F32, kind="ExternalOutput").ap()
    build(nc, aps, out)
    r = run_bass_kernel_spmd(nc, [{f"in_{k}": v for k, v in arrays.items()}], core_ids=[0])
    return r.results[0]["out_0"].reshape(B, S, D)


def prepare(inputs, np):
    i = {k: np.ascontiguousarray(v) for k, v in inputs.items()}
    at = np.arange(P)
    tables = np.zeros((P, 3, P), np.float32)
    tables[:, 0, :] = np.where(at[None, :] > at[:, None], np.float32(NEG), np.float32(0))
    tables[:, 1, :] = tables[:, 0, :].T
    tables[:, 2, :] = (at[:, None] < at[None, :])
    ex = np.arange(E)
    gamma = (1.0 - np.exp(np.linspace(np.log(1.0 / 512.0), np.log(1.0 / 32.0), H1))).astype(np.float32).astype(np.float64)
    place = np.arange(S)
    gam = np.stack([np.tile(gamma[:, None] ** k, (HD1, 1)) for k in (place[None, :], -place[None, :])], axis=1)

    def rows(v):
        return np.ascontiguousarray(np.broadcast_to(v, (P,) + v.shape))

    def by_depth(w, heads):
        return np.ascontiguousarray(w.reshape(P, heads, -1).transpose(0, 2, 1).reshape(P, P))

    def diagonal(w):
        m = np.zeros((H1, HD1, H1, HD1), np.float32)
        for h in range(H1):
            m[h, :, h, :] = w[h]
        return m.reshape(P, P)
    qvk = i["L0_attn_Wqvk"]
    return {
        "h": np.ascontiguousarray(i["L0_attn_h"].reshape(NT, P, D).transpose(1, 0, 2)),
        "ident": np.eye(P, dtype=np.float32),
        "tables": tables,
        "upto": (at[:, None] <= at[None, :]).astype(np.float32),
        "w_q": by_depth(qvk[:, 0:D], H0),
        "w_k": by_depth(qvk[:, 2 * D:3 * D], H0),
        "w_vr": np.concatenate([qvk[:, D:2 * D], i["L0_ffn_router_w"].T], axis=1),
        "w_o": i["L0_attn_Wo"],
        "rb0": rows(i["L0_ffn_router_b"]),
        "rank_e": rows(np.stack([ex, E - ex]).astype(np.float32)),
        "w_up": np.ascontiguousarray(np.stack([i["L0_ffn_W"], i["L0_ffn_V"]], axis=1).transpose(2, 0, 1, 3)),
        "w_dn": np.ascontiguousarray(i["L0_ffn_W_out"].reshape(E, 2, P, D).transpose(2, 0, 1, 3)),
        "w1_raw": np.concatenate([by_depth(diagonal(i["L1_attn_Wq"]), H1), by_depth(diagonal(i["L1_attn_Wk"]), H1),
                                  diagonal(i["L1_attn_Wv"]), i["L1_attn_W1"], i["L1_ffn_Wr"]], axis=1),
        "w2_a": i["L1_attn_W2"],
        "gn_w": rows(i["L1_attn_gn_w"]),
        "gn_b": rows(i["L1_attn_gn_b"]),
        "rb1": rows(i["L1_ffn_br"]),
        "gam": gam.astype(np.float32),
        "w1_e": np.ascontiguousarray(i["L1_ffn_W1"].transpose(1, 0, 2)),
        "w2_e": np.ascontiguousarray(i["L1_ffn_W2"].reshape(E, FC, P, D).transpose(2, 0, 1, 3).reshape(P, E, FC * D)),
        "b1": np.ascontiguousarray(i["L1_ffn_b1"].reshape(UNITS, P).T),
        "b2": np.ascontiguousarray(i["L1_ffn_b2"].T),
    }
```

```python
from contextlib import ExitStack

import concourse.bass as bass
from concourse import mybir

F32 = mybir.dt.float32
F32R = mybir.dt.float32r
BF16 = mybir.dt.bfloat16
U32 = mybir.dt.uint32
ALU = mybir.AluOpType
ACT = mybir.ActivationFunctionType
AX = mybir.AxisListType
ds = bass.ds

P = 128
B, S, D = 16, 256, 128
N = B * S
NT = N // P
TB = S // P
EPS = 1e-5
H0, HD0 = 16, 8
H1, HD1 = 8, 16
E = 8
FH0 = 256
CAP = 256
SLOTS = E * CAP
FH1 = 512
FC = FH1 // P
TOP_P = 0.8
NEG = -1e30
GH = 4
G0 = B * H0 // GH
G1 = B * H1 // GH
MIDDLE = 4
GPB0 = H0 // GH
RING = 8
PAIRS = RING // 2
R0 = 9 * HD0
R1 = 8 * HD1
BLK = 512
NB = N // BLK
TPB = BLK // P
ARRIVE = (0, 2, 4, 10, B)
PROJ1 = 2 * P + E


UNITS = E * FC
AHEAD = 3


def build(nc, a, out):
    ctx = ExitStack()
    with ctx:
        def sb(name, shape, dt=F32, where=ctx):
            return where.enter_context(nc.sbuf_tensor(name, shape, dt))

        def sem(name):
            return ctx.enter_context(nc.semaphore(name))

        def dram(name, shape, dt=F32):
            return nc.dram_tensor(name, shape, dt, kind="Internal").ap()

        qk_parts = dram("qk_parts", [B, 2, 3, P, S], BF16)

        o_rows = dram("o_rows", [B, GPB0, P, S])
        o_heads = o_rows.rearrange("b k (g r) t -> b (k g) r t", r=32)

        x = sb("x", [P, NT, D])
        ident = sb("ident", [P, P])
        upto = sb("upto", [P, P])
        rden_rows = dram("rden_rows", [B, H0, S])
        x_slots = dram("x_slots", [SLOTS, D])
        gate_rows = dram("gate_rows", [E, N])
        y_slots = dram("y_slots", [SLOTS + P, D])
        ident_h = sb("ident_h", [P, P], BF16)
        mask_qk = sb("mask_qk", [P, P], BF16)
        mask_kq = sb("mask_kq", [P, P], BF16)
        before = sb("before", [P, P], BF16)
        ones_h = sb("ones_h", [P, P], BF16)
        moments = sb("moments", [P, NT, 2])
        var = sb("var", [P, NT])
        std = sb("std", [P, NT])
        rstd = sb("rstd", [P, NT])
        shift = sb("shift", [P, NT])

        w1_raw = sb("w1_raw", [P, 2 * P + PROJ1])
        w1_qk = [sb(f"w1_qk_{i}", [P, 2 * P]) for i in ("hi", "lo")]
        w1_p = [sb(f"w1_p_{i}", [P, PROJ1]) for i in ("hi", "lo")]
        w2_a = sb("w2_a", [P, D])
        gn_w = sb("gn_w", [P, D])
        gn_b = sb("gn_b", [P, D])
        rb1 = sb("rb1", [P, E])
        b1 = sb("b1", [P, UNITS])
        b2 = sb("b2", [P, E])
        rank_e = sb("rank_e", [P, 2, E])
        eps = sb("eps", [P, 1])
        warm = sb("warm", [P, 1])
        rb1_s = sb("rb1_s", [P, H1])
        gates = sb("gates", [P, NT, E])
        pick_p = sb("pick_p", [P, 2, NT])

        era = ExitStack()
        xn = sb("xn", [P, NT, D], where=era)
        v_all = sb("v_all", [P, NT, H0, HD0], where=era)
        logits0 = sb("logits0", [P, NT, E], where=era)
        w_q = sb("w_q", [P, P], where=era)
        w_k = sb("w_k", [P, P], where=era)
        w_vr = sb("w_vr", [P, D + E], where=era)
        rb0 = sb("rb0", [P, E], where=era)
        w_o = sb("w_o", [P, D], where=era)
        zero = sb("zero", [P, D], where=era)
        w_up = sb("w_up", [P, E, 2, FH0], where=era)
        w_dn = sb("w_dn", [P, E, 2, D], where=era)
        picked = sb("picked", [P, 2, NT, E], where=era)
        r_a = sb("r_a", [P, 2, NT, E], where=era)
        r_b = sb("r_b", [P, 2, NT, E], where=era)
        r_s = sb("r_s", [P, 8, 2, NT], where=era)
        rank = sb("rank", [P, NT, E], where=era)
        chosen = sb("chosen", [P, NT, E], BF16, where=era)
        ones_t = sb("ones_t", [P, NT], where=era)
        slot_in = sb("slot_in", [P, 2, NT], U32, where=era)
        slot_out = sb("slot_out", [P, 2, NT], U32, where=era)
        y_more = sb("y_more", [P, NT, D], where=era)
        xg = y_more[:, 0:SLOTS // P, :]
        xgT = y_more[:, SLOTS // P:NT, :].rearrange("p t c -> p (t c)")
        y_sb = xg
        act_s = sb("act_s", [P, 2, FH0], where=era)
        act_t = sb("act_t", [P, 2, FH0], where=era)
        act_g = sb("act_g", [P, 2, 2, FH0], where=era)
        den = sb("den", [P, S * H0 // P], where=era)
        rden = sb("rden", [P, S * H0 // P], where=era)
        rden_ring = sb("rden_ring", [P, 2, S], where=era)
        wv_ring = sb("wv_ring", [P, 2, S], where=era)
        wvn = sb("wvn", [P, 2, S], where=era)
        at_ring = sb("at_ring", [P, 2, TB, D], where=era)
        v_ring = sb("v_ring", [P, 2, TB, H0, 2 * HD0], where=era)
        m8 = sb("m8", [P, 2, GH, TB], where=era)
        m_neg = sb("m_neg", [2 * GH, 4, P], BF16, where=era)
        q_st = sb("q_st", [P, PAIRS, 2 * GH, S], BF16, where=era)
        k_st = sb("k_st", [P, PAIRS, 2 * GH, S], BF16, where=era)
        with ExitStack() as part:
            tables = sb("tables", [P, 3, P], where=part)
            stats = sb("stats", [P, 4, TB, 6], where=part)
            mom0 = sb("mom0", [P, 4, TB, 2], where=part)
            xn_ring = sb("xn_ring", [P, 4, TB, D], where=part)
            xT = sb("xT", [P, 2, S], where=part)
            qk_p = sb("qk_p", [P, 4, 2, 3, S], BF16, where=part)
            qk_rest = sb("qk_rest", [P, 2, 2, S], where=part)
        with ExitStack() as part:
            stats1 = sb("stats1", [P, NT, 6], where=part)
            o_ring = sb("o_ring", [P, 4, S], where=part)
            probs = sb("probs", [P, 2, 3, 512], where=part)
        era.close()

        era = ExitStack()
        x_hl = sb("x_hl", [P, 2, N], where=era)
        w1_h = sb("w1_h", [P, E, FH1], where=era)
        w1_l = sb("w1_l", [P, E, FH1], where=era)
        w_raw = sb("w_raw", [P, 2, FH1], where=era)
        gT = sb("gT", [P, 2 * P], where=era)
        with ExitStack() as part:
            logits1 = sb("logits1", [P, NT, E], where=part)
            gam = sb("gam", [P, 2, S], where=part)
            v1 = sb("v1", [P, NT, H1, HD1], where=part)
            sg = sb("sg", [P, NT, D], where=part)
            q1_st = sb("q1_st", [P, PAIRS, H1, S], BF16, where=part)
            k1_st = sb("k1_st", [P, PAIRS, H1, S], BF16, where=part)
            p1 = sb("p1", [P, NT, E], where=part)
            p1_s = sb("p1_s", [P, 3, NT], where=part)
            p1_x = sb("p1_x", [P, 2, NT, E], where=part)
            order = sb("order", [P, NT, E, E], where=part)
            with ExitStack() as sub:
                xn1_ring = sb("xn1_ring", [P, 2, TB, D], where=sub)
                qk1_s = sb("qk1_s", [P, 2, 2, S], where=sub)
                xr = sb("xr", [P, 4, 2, S], where=sub)
                qk1_rest = sb("qk1_rest", [P, 2, 2, S], where=sub)
                qk1_p = sb("qk1_p", [P, 4, 2, 3, S], BF16, where=sub)
            with ExitStack() as sub:
                sc = sb("sc", [P, 2, 3, 512], where=sub)
                v1_ring = sb("v1_ring", [P, 2, TB, H1, HD1], where=sub)
                o1_ring = sb("o1_ring", [P, 2, S], where=sub)
                ret = sb("ret", [P, 4, TB, D], where=sub)
                sq = sb("sq", [P, 2, TB, D], where=sub)
                ss1, sd1, rs1 = (sb(n, [P, 2, TB, H1], where=sub) for n in ("ss1", "sd1", "rs1"))
                z = sb("z", [P, 2, TB, D], where=sub)
                zT = sb("zT", [P, 2, S], where=sub)
                at1_ring = sb("at1_ring", [P, 2, TB, D], where=sub)
        with ExitStack() as part:
            acc = sb("acc", [P, BLK], where=part)
            w2_h = sb("w2_h", [P, E, FH1], where=part)
            gate_b = sb("gate_b", [P, E, BLK], where=part)
            yt = sb("yt", [P, 2, BLK], where=part)
            f = sb("f", [P, 4, BLK], where=part)
            f_h = sb("f_h", [P, 4, BLK], where=part)
            f_l = sb("f_l", [P, 4, BLK], where=part)
            w2_l = sb("w2_l", [P, E, FH1], where=part)
        era.close()

        ps = ctx.enter_context(nc.psum_tensor("ps", [P, 8, 512], F32))

        x_in = [sem(f"x_in{c}") for c in range(len(ARRIVE) - 1)]
        w_in, late_in, experts_in = sem("w_in"), sem("late_in"), sem("experts_in")
        zeroed = sem("zeroed")
        consts_ready = sem("consts_ready")
        stats_done = sem("stats_done")
        moments_done = sem("moments_done")
        var_ready = sem("var_ready")
        std_ready = sem("std_ready")
        rstd_ready = sem("rstd_ready")
        xn_ready = sem("xn_ready")
        xn_second = sem("xn_second")
        kept = [sem(f"kept{v}") for v in range(4)]
        tr_done = sem("tr_done")
        xT_done = sem("xT_done")
        v_mm = sem("v_mm")
        qk_mm, qk_hi, qk_res, qk_mid, qk_lo = (sem(n) for n in ("qk_mm", "qk_hi", "qk_res", "qk_mid", "qk_lo"))
        v_put, lg_put = sem("v_put"), sem("lg_put")
        qk_stored = [sem(f"qk_stored{v}") for v in range(4)]
        stack_in = [sem(f"stack_in{r}") for r in range(PAIRS)]
        s_done, max_done, mtr_done, mneg_done = sem("s_done"), sem("max_done"), sem("mtr_done"), sem("mneg_done")
        mrow_in = [sem(f"mrow_in{r}") for r in range(4)]
        st_done, exp_done, pv_done, o_evac = sem("st_done"), sem("exp_done"), sem("pv_done"), sem("o_evac")
        o_moved = [sem(f"o_moved{u}") for u in range(2)]
        v_here = sem("v_here")
        wv_in = [sem(f"wv_in{u}") for u in range(2)]
        den_in, rden_done, rden_out = sem("den_in"), sem("rden_done"), sem("rden_out")
        wvn_done, wo_mm, at_put, x_attn, x1_done = (sem(n) for n in ("wvn_done", "wo_mm", "at_put", "x_attn", "x1_done"))
        out_done = sem("out_done")
        scattered, expert_rows, xgt_mm, xgt_put = (sem(n) for n in ("scattered", "expert_rows", "xgt_mm", "xgt_put"))
        up_mm, sig_done, gate_s, gated, down_mm, y_put = (sem(n) for n in ("up_mm", "sig_done", "gate_s", "gated", "down_mm", "y_put"))
        routed, counted, indexed, pick_d, pick_e = (sem(n) for n in ("routed", "counted", "indexed", "pick_d", "pick_e"))
        gathered = [sem(f"gathered{u}") for u in range(2)]
        x1_half = sem("x1_half")
        mixed = sem("mixed")

        xh_put, xl_put = sem("xh_put"), sem("xl_put")
        p1_mm = sem("p1_mm")
        qk1_mm, qk1_scaled, qk1_hi, qk1_res, qk1_mid, qk1_lo = (
            sem(n) for n in ("qk1_mm", "qk1_scaled", "qk1_hi", "qk1_res", "qk1_mid", "qk1_lo"))
        qk1_stored = [sem(f"qk1_stored{v}") for v in range(4)]
        sg_put, lg1_put, sg_done = (sem(n) for n in ("sg_put", "lg1_put", "sg_done"))
        stack1_in = [sem(f"stack1_in{r}") for r in range(PAIRS)]
        s1_done, masked, copied, v1_here, pv1_done, o1_evac, turned1, ret_put = (
            sem(n) for n in ("s1_done", "masked", "copied", "v1_here", "pv1_done", "o1_evac", "turned1", "ret_put"))
        ss_done, sd_done, z_a, z_b, z_done, zt_mm, zt_put = (
            sem(n) for n in ("ss_done", "sd_done", "z_a", "z_b", "z_done", "zt_mm", "zt_put"))
        gates_done, gt_mm, gt_put, gates_out = (
            sem(n) for n in ("gates_done", "gt_mm", "gt_put", "gates_out"))
        gate_in = [sem(f"gate_in{e}") for e in range(E)]
        raw_in = [sem(f"raw_in{u}") for u in range(2)]
        w1_hi, w1_lo, w2_hi, w2_lo = (sem(n) for n in ("w1_hi", "w1_lo", "w2_hi", "w2_lo"))
        h_mm, f_done, f_hi, y_mm, yv, summed, acc_turned, x2_done = (
            sem(n) for n in ("h_mm", "f_done", "f_hi", "y_mm", "yv", "summed", "acc_turned", "x2_done"))
        f_lo = [sem("f_lo_even"), sem("f_lo_odd")]

        CREDIT = 2
        credits = [qk_res, qk_lo, v_mm, lg_put, xl_put, qk1_scaled, qk1_res, qk1_lo, p1_mm, lg1_put]

        block = ctx.enter_context(nc.Block())

        def num(g): return g[0] * RING + g[1]
        def div(g, by): return g[0] * (RING // by) + g[1] // by
        def plus(g, k): return g[0], g[1] + k
        def at(g, size): return g[1] % size

        def known(g): return isinstance(g[0], int)

        def run_slots(eng, total, slot, middle=None, peel=1, tail=0):
            for n in range(peel * RING):
                slot((0, n))
            last = total // RING - 1
            stretches = [(peel, last)] if middle is None else [(peel, MIDDLE), (MIDDLE, MIDDLE + 1), (MIDDLE + 1, last)]
            for k, (first, end) in enumerate(stretches):
                if k == 1:
                    middle()
                with eng.Fori(first, end) as i:
                    for r in range(RING):
                        slot((i, r), late=k == 2)
            for n in range(total - RING, total + tail):
                slot((0, n), late=True)

        def half_ring(g, after):
            return (g[1] - after) // 2 % 2

        def past(g, n):
            return not known(g) or num(g) >= n

        def due(g, after):
            if (g[1] - after) % 2 or not past(g, after) or known(g) and num(g) - after >= 2 * B:
                return None
            return div(plus(g, -after), 2)

        def within(g, total):
            return not known(g) or num(g) < total

        def wait_kept(eng, times):
            for v in range(4):
                eng.wait_ge(kept[v], times * 16 * B // 4)

        def known_block(j): return j if isinstance(j, int) else None

        def run_blocks(eng, body):
            body(0)
            with eng.Fori(1, NB - 1) as j:
                body(j)
            body(NB - 1)

        def r32(ap):
            return ap.bitcast(F32R)

        def run_sequences(eng, step, peel=0):
            for b in range(peel):
                step(b, b % 4)
            with eng.Fori(peel // 4, B // 4 - 1) as ii:
                for v in range(4):
                    step(ii * 4 + v, v)
            for b in range(B - 4, B):
                step(b, b % 4)

        def filled(b, v, each):
            return b // 4 * each if isinstance(b, int) else (b - v) * (each // 4)

        def more(b, k):
            return not isinstance(b, int) or b + k < B

        def ps_t1(u): return ps[:, u, 0:S]
        def ps_qk1(u): return ps[:, 2 + u, :]
        def ps_p1(u, t): return ps[:, 4 + 2 * u + t, 0:PROJ1]
        def p1_both(u): return ps[:, 4 + 2 * u:6 + 2 * u, 0:PROJ1]
        def ps_sc(u, c): return ps[:, 3 * u + c, :]
        ps_o1 = ps[:, 6, 0:S]
        ps_at1 = ps[:, 6, S:2 * S]
        ps_r1 = ps[:, 7, 0:S]
        ps_zt = ps[:, 7, S:2 * S]
        EARLY, LATE = slice(0, NT * 3 // 4), slice(NT * 3 // 4, NT)
        LATE_OUT = {0: B - 3, 1: B - 2, 2: B - 1}
        TAIL1 = 7
        SUMS = 5
        PARTS = 8
        GATES = G1 + 1

        def ps_t(u): return ps[:, 4 * u, 0:S]
        def ps_qk(u): return ps[:, 4 * u + 1, :]
        def ps_v(u): return ps[:, 4 * u + 3, 0:TB * (D + E)].rearrange("p (t c) -> p t c", t=TB)
        def ps_s(c): return ps[:, c, :]
        def ps_st(c): return ps[:, 3 + c, :]
        def ahead_of_all(g): return known(g) and num(g) == 1
        ps_o = ps[:, 6, 0:S]
        ps_at = ps[:, 6, S:2 * S]
        ps_m = ps[0:2 * GH, 7, 0:P]
        def ps_count(n): return ps[:, 6 + n, S:2 * S]

        qk_rows = qk_parts.rearrange("b c i (d a h) t -> b c (i d) a (h t)", d=HD0, a=2)

        @block.sync
        def _(sp):
            for c, part_in in enumerate(x_in):
                tiles = slice(ARRIVE[c] * TB, ARRIVE[c + 1] * TB)
                sp.dma_start(x[:, tiles, :], a["h"][:, tiles, :]).then_inc(part_in, 16)
            for dst, name in ((tables[:, :, :], "tables"), (rank_e[:, :, :], "rank_e"), (w_o[:, :], "w_o"),
                              (w1_raw[:, :], "w1_raw"), (upto[:, :], "upto"), (w2_a[:, :], "w2_a"), (gn_w[:, :], "gn_w"),
                              (gn_b[:, :], "gn_b"), (rb1[:, :], "rb1"), (b1[:, :], "b1"), (b2[:, :], "b2")):
                sp.dma_start(dst, a[name]).then_inc(late_in, 16)

            def keep_parts(b, v):
                sp.wait_ge(qk_lo, b + 1 + CREDIT)
                sp.dma_start(qk_parts[ds(b, 1)].rearrange("o c i p t -> p (o c i) t"), qk_p[:, v, :, :, :].rearrange("p c i t -> p (c i) t"))\
                  .then_inc(qk_stored[v], 16)

            def load_pair(b, half, r):
                src = qk_rows[ds(b, 1), 0, :, half].rearrange("o r c -> (o r) c")
                sp.dma_start(q_st[0:R0, r, :, :].rearrange("p h t -> p (h t)"), src.unsqueeze(0).broadcast_to([3, 3 * HD0, 2 * GH * S]))\
                  .then_inc(stack_in[r], 16)
                for j in range(3):
                    src = qk_rows[ds(b, 1), 1, j * HD0:(j + 1) * HD0, half].rearrange("o d c -> (o d) c")
                    sp.dma_start(k_st[j * 3 * HD0:(j + 1) * 3 * HD0, r, :, :].rearrange("p h t -> p (h t)"),
                                 src.unsqueeze(0).broadcast_to([3, HD0, 2 * GH * S])).then_inc(stack_in[r], 16)

            def keep_xn(b, v):
                sp.wait_ge(xn_ready, (b + 1) * TB)
                sp.dma_start(xn[:, ds(b * TB, TB), :], xn_ring[:, v, :, :]).then_inc(kept[v], 16)
            for b in range(3):
                keep_xn(b, b)

            expert_weights = ((w_up, "w_up"), (w_dn, "w_dn"))

            def load_expert(which, e):
                w, name = expert_weights[which]
                sp.dma_start(w[:, ds(e, 1), :, :], a[name][:, ds(e, 1), :, :]).then_inc(experts_in, 16)

            def keep0(b, v):
                if more(b, 3):
                    keep_xn(b + 3, (v + 3) % 4)
                if isinstance(b, int) and b - (B - 4) in (0, 1):
                    sp.wait_ge(zeroed, 6)
                    sp.wait_ge(qk_stored[0], 32)
                    load_pair(0, b % 2, b % 2)
                keep_parts(b, v)
            for b in range(4):
                keep0(b, b)
                load_expert(0, b)
                load_expert(1, b)
            with sp.Fori(1, B // 4 - 1) as ii:
                for v in range(4):
                    keep0(ii * 4 + v, v)
                    load_expert(v % 2, ii * 2 + 2 + v // 2)
            for b in range(B - 4, B):
                keep0(b, b % 4)
            for v in range(4):
                sp.wait_ge(qk_stored[v], 16 * (B // 4 + 1))

            def move_max(g):
                r = at(g, RING)
                sp.wait_ge(mneg_done, num(g) + 1)
                sp.dma_start(q_st[R0:R0 + 1, r // 2, (r % 2) * GH:(r % 2) * GH + GH, :]
                             .rearrange("o h (t q) -> o (h t) q", t=TB),
                             m_neg[:, r % 4, :]).then_inc(mrow_in[r % 4], 16)

            def move_out(g):
                sp.wait_ge(o_evac, num(g) + 1)
                k, place = at(g, GPB0) - 1, at(g, 4) // 2
                sp.dma_start(o_rows[ds(div(g, GPB0), 1), k:k + 2].rearrange("o k p t -> p (o k) t"), o_ring[:, 2 * place:2 * place + 2, :])\
                  .then_inc(o_moved[place], 16)

            def bring_back(b, u):
                for place in range(2):
                    sp.wait_ge(o_moved[place], b * 16 + 16)
                if not isinstance(b, int) or b >= 2:
                    sp.wait_ge(wvn_done, b - 1)
                sp.dma_start(den[:, :], o_heads[ds(b, 1), :, HD0, :].rearrange("o h (a t) -> (o h) a t", t=S * H0 // P)).then_inc(den_in, 16)
                sp.dma_start(wv_ring[:, u, :], o_heads[ds(b, 1), :, 0:HD0, :].rearrange("o h d t -> (o h) d t")).then_inc(wv_in[u], 16)

            def keep_inverse(b):
                sp.wait_ge(rden_done, b + 1)
                sp.dma_start(rden_rows[ds(b, 1)].rearrange("o h (a t) -> (o h) a t", t=S * H0 // P), rden[:, :]).then_inc(rden_out, 16)

            def spread_inverse(b, u):
                sp.wait_ge(rden_out, b * 16 + 16)
                sp.dma_start(rden_ring[:, u, :], rden_rows[ds(b, 1)].rearrange("o h t -> (o h) t").unsqueeze(1).broadcast_to([H0, HD0, S]))\
                  .then_inc(wv_in[u], 16)

            for n in range(2):
                move_max((0, n))
                load_pair(1, n, 2 + n)

            def slot(g, late=False):
                if within(plus(g, 2), G0):
                    move_max(plus(g, 2))
                if g[1] % 2 == 0 and past(g, 2):
                    move_out(plus(g, -1))
                k, u = g[1] % GPB0, g[1] // GPB0 % 2
                if k == 2 and past(g, 6):
                    bring_back(div(plus(g, -6), GPB0), 1 - u)
                if k == 0 and past(g, 8):
                    keep_inverse(div(plus(g, -8), GPB0))
                if k == 1 and past(g, 9):
                    spread_inverse(div(plus(g, -9), GPB0), u)
                if g[1] % 2 == 1 and within(plus(g, 7), G0):
                    far = plus(g, 7)
                    sp.wait_ge(st_done, num(g) + 1)
                    load_pair(div(far, GPB0), at(far, GPB0) // 2, at(far, RING) // 2)
            run_slots(sp, G0, slot, lambda: None, peel=2)
            sp.wait_ge(x1_done, 2)
            sp.dma_start(gam[:, :, :], a["gam"]).then_inc(late_in, 16)

            def load_raw(name, e, u):
                sp.dma_start(w_raw[:, u, :], a[name][:, ds(e, 1), :].rearrange("p o f -> p (o f)")).then_inc(raw_in[u], 16)
            for u in range(2):
                load_raw("w1_e", u, u)

            def keep_parts1(b, v):
                sp.wait_ge(qk1_lo, b + 1 + CREDIT)
                sp.dma_start(qk_parts[ds(b, 1)].rearrange("o c i p t -> p (o c i) t"), qk1_p[:, v, :, :, :].rearrange("p c i t -> p (c i) t"))\
                  .then_inc(qk1_stored[v], 16)
            move_out((0, G0 - 1))
            keep_inverse(B - 2)
            spread_inverse(B - 2, 0)
            bring_back(B - 1, 1)
            keep_inverse(B - 1)
            spread_inverse(B - 1, 1)

            def keep_x(b, v):
                sp.wait_ge(xl_put, b + 1 + CREDIT)
                sp.dma_start(x_hl[:, :, ds(b * S, S)], xr[:, v, :, :]).then_inc(kept[v], 16)
            for b in range(2):
                keep_x(b, b)

            qk1_rows = qk_parts.rearrange("b c i (d h) t -> b c (i d) (h t)", d=HD1)

            def load_sequence(b, r, loaded):
                load_queries(b, r, loaded)
                load_keys(b, r, loaded)

            def load_queries(b, r, loaded):
                src, rows = qk1_rows[ds(b, 1), 0].rearrange("o r c -> (o r) c"), 3 * HD1
                sp.dma_start(q1_st[0:2 * rows, ds(r, 1), :, :].rearrange("p o h t -> p (o h t)"),
                             src.unsqueeze(0).broadcast_to([2, rows, H1 * S])).then_inc(loaded, 16)
                sp.dma_start(q1_st[2 * rows:R1, ds(r, 1), :, :].rearrange("p o h t -> p (o h t)"), src[0:R1 - 2 * rows]).then_inc(loaded, 16)

            def load_keys(b, r, loaded):
                rows = 3 * HD1
                for j, parts in enumerate((3, 3, 2)):
                    src = qk1_rows[ds(b, 1), 1, j * HD1:(j + 1) * HD1].rearrange("o d c -> (o d) c")
                    sp.dma_start(k1_st[j * rows:j * rows + parts * HD1, ds(r, 1), :, :].rearrange("p o h t -> p (o h t)"),
                                 src.unsqueeze(0).broadcast_to([parts, HD1, H1 * S])).then_inc(loaded, 16)

            def keep1(b, v):
                if more(b, 2):
                    keep_x(b + 2, (v + 2) % 4)
                keep_parts1(b, v)

            for b in range(4):
                if b == 2:
                    for n in range(2):
                        sp.wait_ge(qk1_stored[n], 32)
                        load_sequence(n, n, stack1_in[n])
                keep1(b, b)
            with sp.Fori(1, B // 4 - 1) as ii:
                for v in range(4):
                    keep1(ii * 4 + v, v)
            for b in range(B - 4, B):
                keep1(b, b % 4)
                for n, after in ((2, B - 4), (3, B - 1)):
                    if b == after:
                        sp.wait_ge(qk1_stored[n], 32)
                        load_sequence(n, n, stack1_in[n])
            for v in range(4):
                sp.wait_ge(qk1_stored[v], 16 * (B // 4 + 1))

            def slot(g, late=False):
                if g[1] % 2 == 1 and within(plus(g, 7), G1):
                    far = plus(g, 7)
                    sp.wait_ge(s1_done, num(g) + 1)
                    load_sequence(div(far, 2), at(far, RING) // 2, stack1_in[at(far, RING) // 2])
                if g[1] % 4 == 3 and past(g, 7) and within(plus(g, 8), G1 + 7):
                    e = div(plus(g, 1), 4)
                    sp.wait_ge(w1_lo, e - 1)
                    load_raw("w1_e", e, g[1] // 4 % 2 ^ 1)

            run_slots(sp, G1, slot)
            for u in range(2):
                sp.wait_ge(w1_lo, E - 1 + u)
                load_raw("w2_e", u, u)

            sp.wait_ge(gt_put, 1)
            for c in range(2):
                sp.dma_start(gate_rows[:, c * N // 2:(c + 1) * N // 2].rearrange("e (t k) -> t e k", k=P), gT[:, c * P:(c + 1) * P])\
                  .then_inc(gates_out, 16)
            sp.wait_ge(gates_out, 32)
            sp.wait_ge(z_done, B)

            def load_gate(j, e):
                sp.dma_start(gate_b[:, e, :], gate_rows[e:e + 1, ds(j * BLK, BLK)].broadcast_to([P, BLK])).then_inc(gate_in[e], 16)

            def store(j):
                sp.wait_ge(x2_done, j + 1)
                sp.dma_start(out[ds(j * BLK, BLK)].rearrange("(t p) d -> p t d", p=P), x[:, ds(j * TPB, TPB), :]).then_inc(out_done, 16)
            for e in range(E):
                if e in (2, 4):
                    for n in (e, e + 1):
                        sp.wait_ge(w2_lo, n - 1)
                        load_raw("w2_e", n, n % 2)
                load_gate(0, e)

            def body(j):
                for e in range(E):
                    if known_block(j) == 0 and e in (0, 1):
                        sp.wait_ge(w2_lo, e + 5)
                        load_raw("w2_e", e + 6, e % 2)
                    if known_block(j) != NB - 1:
                        sp.wait_ge(yv, j * E + e + 1)
                        load_gate(j + 1, e)
                    if e == 2 and known_block(j) != 0:
                        store(j - 1)
            run_blocks(sp, body)
            store(NB - 1)
            sp.wait_ge(out_done, 16 * NB)

        @block.gpsimd
        def _(pool):
            for s in credits:
                pool.sem_inc(s, CREDIT)
            for v in range(4):
                pool.sem_inc(qk_stored[v], 16)
                pool.sem_inc(qk1_stored[v], 16)
            nc.gpsimd.memset(v_ring[:, :, :, :, :], 1.0).then_inc(zeroed, 1)
            nc.gpsimd.memset(ones_h[:, :], 1.0).then_inc(zeroed, 1)
            nc.gpsimd.memset(zero[:, :], 0.0).then_inc(zeroed, 1)
            nc.gpsimd.memset(ones_t[:, :], 1.0).then_inc(zeroed, 1)
            nc.gpsimd.memset(eps[:, :], EPS).then_inc(zeroed, 1)
            pool.wait_ge(zeroed, 5)
            nc.gpsimd.memset(k_st[64:P, :, :, :], 1.0).then_inc(zeroed, 1)
            pool.wait_ge(zeroed, 6)
            pool.dma_start(x_slots.rearrange("(c p) d -> p c d", p=P),
                           zero[:, :].unsqueeze(1).broadcast_to([P, SLOTS // P, D])).then_inc(scattered, 16)
            pool.dma_start(y_slots[SLOTS:SLOTS + P], zero[:, :]).then_inc(scattered, 16)

            def low0(b, v):
                pool.wait_ge(qk_mid, b + 1)
                nc.gpsimd.tensor_tensor(qk_p[:, v, :, 2, :], qk_rest[:, v % 2, :, :], qk_p[:, v, :, 1, :], ALU.subtract).then_inc(qk_lo, 1)
            run_sequences(pool, low0)

            def put_values(b, u):
                for t in range(TB):
                    last = nc.gpsimd.tensor_copy(v_ring[:, u, t, :, 0:HD0],
                                                 v_all[:, ds(b * TB + t, 1), :, :].rearrange("p o h d -> p (o h) d"))
                last.then_inc(v_here, 1)
            pool.wait_ge(v_put, B)
            for u in range(2):
                put_values(u, u)

            def scatter(first, end):
                for t in range(first, min(end, NT)):
                    for c in range(2):
                        pool.indirect_dma_start(out=x_slots, out_offset=bass.IndirectOffsetOnAxis(ap=slot_in[:, c, t:t + 1], axis=0),
                                                in_=xn[:, t, :], in_offset=None, bounds_check=SLOTS - 1, oob_is_err=False)\
                            .then_inc(scattered, 16)

            def gather(first, end):
                for t in range(first, min(end, NT)):
                    k = t // (NT // 8)
                    if k >= 2 and t % (NT // 8) == 0:
                        pool.wait_ge(gathered[k % 2], k // 2 * 16 * 2 * NT // 8)
                    for c in range(2):
                        pool.indirect_dma_start(out=(xn, y_more)[c][:, t, :], out_offset=None, in_=y_slots,
                                                in_offset=bass.IndirectOffsetOnAxis(ap=slot_out[:, c, t:t + 1], axis=0))\
                            .then_inc(gathered[k % 2], 16)

            pool.wait_ge(indexed, 1)
            pool.wait_ge(scattered, 32)
            wait_kept(pool, 1)
            FIRST, EACH = 3, 5
            LAST = -(-(NT - FIRST) // EACH) - 1
            scatter(0, FIRST)
            for b in range(B - 1):
                if b + 2 < B:
                    pool.wait_ge(pv_done, (b + 1) * GPB0)
                    put_values(b + 2, b % 2)
                scatter(FIRST + b * EACH, FIRST + (b + 1) * EACH)
                if b == LAST:
                    pool.wait_ge(scattered, 32 + 16 * 2 * NT)
                    pool.dma_start(xg, x_slots.rearrange("(c p) d -> p c d", p=P)).then_inc(expert_rows, 16)
                if b == 7:
                    pool.wait_ge(y_put, E)
                    pool.dma_start(y_slots[0:SLOTS].rearrange("(c p) d -> p c d", p=P), y_sb).then_inc(expert_rows, 16)
                    pool.wait_ge(indexed, 2)
                    pool.wait_ge(expert_rows, 32)
                    pool.wait_ge(xgt_put, SLOTS // 512)
                if b >= 7:
                    gather((b - 7) * EACH, (b - 6) * EACH)

            for u in range(2):
                pool.wait_ge(gathered[u], 4 * 16 * 2 * NT // 8)
            for c, y in enumerate((xn, y_more)):
                nc.gpsimd.tensor_tensor(y[:, LATE, :], y[:, LATE, :], pick_p[:, c, LATE].unsqueeze(2).broadcast_to([P, NT // 4, D]), ALU.mult)\
                    .then_inc(mixed, 1)
            pool.wait_ge(mixed, 2)
            nc.gpsimd.tensor_tensor(xn[:, LATE, :], xn[:, LATE, :], y_more[:, LATE, :], ALU.add).then_inc(mixed, 1)

            def last_parts(b, v):
                u = v % 2
                pool.wait_ge(qk1_mid, b + 1)
                nc.gpsimd.tensor_tensor(qk1_p[:, v, :, 2, :], qk1_rest[:, u, :, :], qk1_p[:, v, :, 1, :], ALU.subtract).then_inc(qk1_lo, 1)
                pool.wait_ge(sg_put, b + 1)
                nc.gpsimd.tensor_tensor(sg[:, ds(b * TB, TB), :], sg[:, ds(b * TB, TB), :],
                                        gn_b[:, :].unsqueeze(1).broadcast_to([P, TB, D]), ALU.add).then_inc(sg_done, 1)
            run_sequences(pool, last_parts)

            def values(b, u):
                nc.gpsimd.tensor_copy(v1_ring[:, u, :, :, :], v1[:, ds(b * TB, TB), :, :]).then_inc(v1_here, 1)
            pool.wait_ge(lg1_put, B + CREDIT)
            pool.wait_ge(sg_done, B)
            wait_kept(pool, 2)
            for b in range(3, 5):
                values(b, b % 2)

            def step(b, u, e):
                if not isinstance(b, int) or b == 3:
                    pool.wait_ge(pv1_done, b * 2 + 2)
                    values(b + 2, u % 2)
                if more(b, -1) and (not isinstance(b, int) or b >= 1):
                    pool.wait_ge(z_a, b)
                    tiles = z[:, 1 - u % 2, :, :]
                    nc.gpsimd.tensor_tensor(tiles, tiles, gn_w[:, :].unsqueeze(1).broadcast_to([P, TB, D]), ALU.mult).then_inc(z_b, 1)
                    pool.wait_ge(z_b, b)
                    nc.gpsimd.tensor_tensor(tiles, tiles, sg[:, ds((b - 1) * TB, TB), :], ALU.add).then_inc(z_done, 1)
                if u % 2 == 0 and more(b, 0):
                    pool.wait_ge(w1_hi, e + 1)
                    nc.gpsimd.tensor_tensor(r32(w1_l[:, ds(e, 1), :].rearrange("p o f -> p (o f)")), w_raw[:, u // 2, :],
                                            w1_h[:, ds(e, 1), :].rearrange("p o f -> p (o f)"), ALU.subtract).then_inc(w1_lo, 1)
            def low_w2(e):
                pool.wait_ge(w2_hi, e + 1)
                nc.gpsimd.tensor_tensor(r32(w2_l[:, e, :]), w_raw[:, e % 2, :], w2_h[:, e, :], ALU.subtract).then_inc(w2_lo, 1)

            for b in range(4):
                step(b, b, b // 2)
            pool.wait_ge(gates_done, 1)
            with pool.Fori(1, 3) as ii:
                for u in range(4):
                    step(ii * 4 + u, u, ii * 2 + u // 2)
                    tiles = ds((ii * 4 + (u - 4)) * (NT // PARTS), NT // PARTS)
                    nc.gpsimd.tensor_tensor(order[:, tiles, :, :], order[:, tiles, :, :],
                                            p1[:, tiles, :].unsqueeze(2).broadcast_to([P, NT // PARTS, E, E]), ALU.mult).then_inc(gates_done, 1)
            for b in range(12, B + 1):
                step(b, b % 4, b // 2)
                if b >= B - 1:
                    low_w2(b - (B - 1))

            def add_expert(j, e):
                pool.wait_ge(yv, j * E + e + 1)
                if e:
                    if e > 1:
                        pool.wait_ge(summed, j * (E - 1) + e - 1)
                    nc.gpsimd.tensor_tensor(acc[:, :], acc[:, :], yt[:, e % 2, :], ALU.add).then_inc(summed, 1)
            def body(j):
                for m in range(1, UNITS, 2):
                    n = j * UNITS + m
                    if known_block(j) != NB - 1 or m < UNITS - 1:
                        pool.wait_ge(f_hi, n + 1)
                        if known_block(j) != 0 or m >= 4:
                            pool.wait_ge(y_mm, n - 3)
                        nc.gpsimd.tensor_tensor(r32(f_l[:, m % 4, :]), f[:, m % 4, :], f_h[:, m % 4, :], ALU.subtract).then_inc(f_lo[1], 1)
                    if m % FC == 3:
                        if m >= 7:
                            add_expert(j, (m - 7) // FC)
                        elif known_block(j) != 0:
                            add_expert(j - 1, E - 1)
            run_blocks(pool, body)

        @block.scalar
        def _(act):
            for dst, name in ((ident[:, :], "ident"), (w_q[:, :], "w_q"), (w_k[:, :], "w_k"), (w_vr[:, :], "w_vr"), (rb0[:, :], "rb0")):
                act.dma_start(dst, a[name]).then_inc(w_in, 16)

            def deviation(b, v):
                act.wait_ge(var_ready, b + 1)
                nc.scalar.activation(std[:, v * TB:(v + 1) * TB], var[:, v * TB:(v + 1) * TB], ACT.Sqrt).then_inc(std_ready, 1)

            def middle_parts(b, v):
                act.wait_ge(qk_res, b + 1 + CREDIT)
                nc.scalar.activation(qk_p[:, v, :, 1, :], qk_rest[:, v % 2, :, :], ACT.Copy).then_inc(qk_mid, 1)

            def turn_x(b, u):
                act.wait_ge(tr_done, b + 1)
                act.wait_ge(v_mm, b + 1)
                nc.scalar.activation(xT[:, u, :], ps_t(u), ACT.Copy).then_inc(xT_done, 1)

            def parts0(b, v):
                u = v % 2
                act.wait_ge(v_mm, b + 1 + CREDIT)
                nc.scalar.activation(v_all[:, ds(b * TB, TB), :, :].rearrange("p t h d -> p t (h d)"),
                                     ps_v(u)[:, :, 0:D], ACT.Copy).then_inc(v_put, 1)
                if more(b, 3):
                    deviation(b + 3, (v + 3) % 4)
                act.wait_ge(qk_mm, b + 1)
                act.wait_ge(qk_stored[v], filled(b, v, 16) + 16)
                nc.scalar.activation(qk_p[:, v, :, 0, :], ps_qk(u).rearrange("p (c t) -> p c t", c=2), ACT.Copy).then_inc(qk_hi, 1)
                if more(b, 2):
                    turn_x(b + 2, u)
                if not isinstance(b, int) or b >= 1:
                    middle_parts(b - 1, (v - 1) % 4)
            deviation(0, 0)
            deviation(1, 1)
            turn_x(0, 0)
            turn_x(1, 1)
            deviation(2, 2)
            run_sequences(act, parts0, peel=4)
            middle_parts(B - 1, 3)

            def negate_max(g):
                act.wait_ge(mtr_done, num(g) + 1)
                if past(g, 4):
                    act.wait_ge(mrow_in[at(g, 4)], div(g, 4) * 16)
                nc.scalar.activation(m_neg[:, at(g, 4), :], ps_m, ACT.Copy, scale=-1.0).then_inc(mneg_done, 1)

            def put_attention(b, u, src):
                act.wait_ge(wo_mm, b + 1)
                if not isinstance(b, int) or b >= 2:
                    act.wait_ge(x_attn, b - 1)
                nc.scalar.activation(at_ring[:, u, :, :].rearrange("p t c -> p (t c)"), src, ACT.Copy).then_inc(at_put, 1)

            def evacuate(g):
                act.wait_ge(pv_done, num(g) + 1)
                if past(g, 4):
                    act.wait_ge(o_moved[at(g, 4) // 2], div(g, 4) * 16)
                nc.scalar.activation(o_ring[:, at(g, 4), :], ps_o, ACT.Copy).then_inc(o_evac, 1)

            wait_kept(act, 1)
            act.wait_ge(qk_lo, B + CREDIT)
            for n in range(2):
                negate_max((0, n))

            def slot(g, late=False):
                if within(plus(g, 2), G0):
                    negate_max(plus(g, 2))
                act.wait_ge(st_done, num(g) + 1)
                if past(g, 2):
                    act.wait_ge(pv_done, num(g) - 1)
                nc.scalar.activation(probs[:, at(g, 2), :, :], ps[:, 3:6, :], ACT.Exp, scale=float(D) ** -0.5)\
                  .then_inc(exp_done, 1)
                if past(g, 1):
                    evacuate(plus(g, -1))
                if known(g) and num(g) == 1:
                    act.wait_ge(pick_d, 1)
                    nc.scalar.activation(r_s[:, 1, 0, :], r_s[:, 0, 0, :], ACT.Exp).then_inc(pick_e, 1)
                if g[1] % GPB0 == 2 and past(g, 14):
                    put_attention(div(plus(g, -14), GPB0), 1 - g[1] // GPB0 % 2, ps_at)

            def middle():
                for c in range(SLOTS // 512):
                    act.wait_ge(xgt_mm, c + 1)
                    nc.scalar.activation(xgT[:, c * 512:(c + 1) * 512], ps[:, c, :], ACT.Copy).then_inc(xgt_put, 1)
                for e in range(E):
                    act.wait_ge(up_mm, e + 1)
                    if e >= 1:
                        act.wait_ge(gate_s, e)
                    nc.scalar.activation(act_s[:, :, :].rearrange("p c t -> p (c t)"), ps[:, 2 + e % 2, :], ACT.Sigmoid)\
                      .then_inc(sig_done, 1)
                    if e >= 1:
                        put_down(e - 1)
                put_down(E - 1)

            def put_down(e):
                act.wait_ge(down_mm, e + 1)
                nc.scalar.activation(y_sb[:, 2 * e:2 * e + 2, :].rearrange("p c d -> p (c d)"), ps[:, 4 + e % 2, 0:2 * D], ACT.Copy)\
                  .then_inc(y_put, 1)
            run_slots(act, G0, slot, middle, peel=2)

            def deviation1(n, tiles):
                act.wait_ge(var_ready, B + n)
                nc.scalar.activation(std[:, tiles], var[:, tiles], ACT.Sqrt).then_inc(std_ready, 1)
            deviation1(1, EARLY)
            evacuate((0, G0 - 1))

            def middle_parts1(b, v):
                act.wait_ge(qk1_res, b + 1 + CREDIT)
                nc.scalar.activation(qk1_p[:, v, :, 1, :], qk1_rest[:, v % 2, :, :], ACT.Copy).then_inc(qk1_mid, 1)

            def normalise(b, u):
                if not isinstance(b, int) or b >= 7:
                    act.wait_ge(rstd_ready, B + 4)
                t = b * TB + 1
                nc.scalar.activation(xn1_ring[:, u, 1, :], x[:, ds(t, 1), :].rearrange("p o c -> p (o c)"), ACT.Identity,
                                     bias=shift[:, ds(t, 1)], scale=rstd[:, ds(t, 1)]).then_inc(xn_second, 1)

            def high_x(b, v):
                act.wait_ge(tr_done, B + b + 1)
                act.wait_ge(p1_mm, b + 1)
                act.wait_ge(kept[v], filled(b, v, 16) + 16 * B // 4)
                nc.scalar.activation(r32(xr[:, v, 0, :]), ps_t1(v % 2), ACT.Copy).then_inc(xh_put, 1)

            def parts(b, v):
                u = v % 2
                act.wait_ge(p1_mm, b + 1 + CREDIT)
                nc.scalar.activation(sg[:, ds(b * TB, TB), :], p1_both(u)[:, :, D:2 * D], ACT.Silu).then_inc(sg_put, 1)
                if isinstance(b, int) and b == 3:
                    deviation1(2, LATE)
                act.wait_ge(qk1_scaled, b + 1 + CREDIT)
                act.wait_ge(qk1_stored[v], filled(b, v, 16) + 16)
                nc.scalar.activation(qk1_p[:, v, :, 0, :], qk1_s[:, u, :, :], ACT.Copy).then_inc(qk1_hi, 1)
                if more(b, 2):
                    high_x(b + 2, (v + 2) % 4)
                if more(b, 3):
                    act.wait_ge(tr_done, B + b + 2)
                    normalise(b + 3, 1 - u)
                if not isinstance(b, int) or b >= 1:
                    middle_parts1(b - 1, (v - 1) % 4)
            act.wait_ge(rstd_ready, B + 2)
            act.wait_ge(pv_done, G0)
            normalise(0, 0)
            normalise(1, 1)
            high_x(0, 0)
            normalise(2, 0)
            high_x(1, 1)

            def step1(b, v):
                parts(b, v)
                if isinstance(b, int) and b == 3:
                    act.wait_ge(std_ready, B + 2)
                    nc.scalar.activation(warm[:, :], std[:, 0:1], ACT.Silu)
                if isinstance(b, int) and b in LATE_OUT:
                    put_attention(LATE_OUT[b], LATE_OUT[b] % 2, ps_t1((b + 1) % 2))
            run_sequences(act, step1, peel=4)
            middle_parts1(B - 1, 3)

            def hidden_unit(j, m):
                n = j * UNITS + m
                act.wait_ge(h_mm, n + 1)
                if known_block(j) != 0 or m >= 4:
                    act.wait_ge(f_hi, n - 3)
                    act.wait_ge(f_lo[m % 2], j * (UNITS // 2) + m // 2 - 1)
                nc.scalar.activation(f[:, m % 4, :], ps[:, m % 4, :], ACT.Relu, bias=b1[:, m:m + 1]).then_inc(f_done, 1)

            def put_heads(g):
                heads = ps_r1.rearrange("p (t h r) -> p t h r", t=TB, h=GH)[:, :, :, 0:HD1]
                if known(g) and num(g) == 0:
                    for v in range(4):
                        act.wait_ge(qk1_stored[v], 16 * (B // 4 + 1))
                act.wait_ge(turned1, num(g) + 1)
                if past(g, 8):
                    act.wait_ge(z_a, div(g, 2) - 3)
                nc.scalar.activation(ret[:, g[1] // 2 % 4, :, g[1] % 2 * GH * HD1:(g[1] % 2 + 1) * GH * HD1]
                                     .rearrange("p t (h d) -> p t h d", h=GH),
                                     heads, ACT.Copy)
                u = g[1] // 2 % 2
                if past(g, 4):
                    act.wait_ge(ss_done, div(g, 2) - 1)
                nc.scalar.activation(sq[:, u, :, g[1] % 2 * GH * HD1:(g[1] % 2 + 1) * GH * HD1]
                                     .rearrange("p t (h d) -> p t h d", h=GH), heads, ACT.Square).then_inc(ret_put, 1)

            def evacuate1(g):
                act.wait_ge(pv1_done, num(g) + 1)
                if past(g, 2):
                    act.wait_ge(turned1, num(g) - 1)
                nc.scalar.activation(o1_ring[:, at(g, 2), :], ps_o1, ACT.Copy).then_inc(o1_evac, 1)
            act.wait_ge(lg1_put, B + CREDIT)

            def slot(g, late=False):
                u = at(g, 2)
                if known(g) and num(g) == 1:
                    for v in range(3):
                        act.wait_ge(kept[v], 2 * 16 * B // 4)
                    act.wait_ge(qk1_lo, B + CREDIT)
                b = due(g, 5)
                if b is not None:
                    act.wait_ge(ss_done, b + 1)
                    if past(g, 9):
                        act.wait_ge(rden_done, B + b - 1)
                    nc.scalar.activation(sd1[:, half_ring(g, 5), :, :], ss1[:, half_ring(g, 5), :, :], ACT.Sqrt,
                                         bias=eps[:, 0:1], scale=1.0 / HD1).then_inc(sd_done, 1)
                if within(g, G1):
                    act.wait_ge(s1_done, num(g) + 1)
                    if past(g, 2):
                        act.wait_ge(pv1_done, num(g) - 1)
                    nc.scalar.activation(sc[:, u, 2, :], ps_sc(u, 2), ACT.Copy).then_inc(copied, 1)
                if past(g, 1) and within(plus(g, -1), G1):
                    evacuate1(plus(g, -1))
                if known(g) and num(g) == 1:
                    act.wait_ge(pick_d, 2)
                    nc.scalar.activation(p1_x[:, 1, :, :], p1_x[:, 0, :, :], ACT.Exp).then_inc(pick_e, 1)
                b = due(g, 8)
                if b is not None:
                    act.wait_ge(wo_mm, B + b + 1)
                    if past(g, 12):
                        act.wait_ge(x_attn, B + b - 1)
                    nc.scalar.activation(at1_ring[:, half_ring(g, 8), :, :].rearrange("p t c -> p (t c)"), ps_at1, ACT.Copy).then_inc(at_put, 1)
                if known(g) and num(g) == GATES:
                    act.wait_ge(gt_mm, 1)
                    nc.scalar.activation(gT[:, :], ps_at1, ACT.Copy).then_inc(gt_put, 1)
                if past(g, 2) and within(plus(g, -2), G1):
                    put_heads(plus(g, -2))
                b = due(g, 7)
                if b is not None:
                    act.wait_ge(zt_mm, b + 1)
                    if past(g, 11):
                        act.wait_ge(wo_mm, B + b - 1)
                    nc.scalar.activation(zT[:, half_ring(g, 7), :], ps_zt, ACT.Copy).then_inc(zt_put, 1)
                if g[1] % 4 == 2 and within(g, G1):
                    e, v = div(g, 4), g[1] // 4 % 2
                    act.wait_ge(raw_in[v], div(g, RING) * 16 + 16)
                    nc.scalar.activation(r32(w1_h[:, ds(e, 1), :].rearrange("p o f -> p (o f)")), w_raw[:, v, :], ACT.Copy).then_inc(w1_hi, 1)
                if known(g) and 0 <= num(g) - G1 - 2 < AHEAD:
                    hidden_unit(0, num(g) - G1 - 2)
            run_slots(act, G1, slot, tail=TAIL1)

            def body(j):
                for m in range(AHEAD if known_block(j) == 0 else 0, UNITS):
                    hidden_unit(j, m)
            run_blocks(act, body)

        @block.vector
        def _(dve):
            def moments_of(b, v):
                for t in range(TB):
                    nc.vector.bn_stats(stats[:, v, t, :], x[:, ds(b * TB + t, 1), :].rearrange("p o c -> p (o c)")).then_inc(stats_done, 1)

            def variance_of(b, v):
                for t in range(TB):
                    nc.vector.bn_aggr(mom0[:, v, t, :], stats[:, v, t, :]).then_inc(moments_done, 1)
                dve.wait_ge(moments_done, (b + 1) * TB)
                nc.vector.tensor_scalar(var[:, v * TB:(v + 1) * TB], mom0[:, v, :, 1], EPS, None, ALU.add).then_inc(var_ready, 1)

            def scale_of(b, v):
                dve.wait_ge(std_ready, b + 1)
                nc.vector.reciprocal(rstd[:, v * TB:(v + 1) * TB], std[:, v * TB:(v + 1) * TB]).then_inc(rstd_ready, 1)

            def normalise0(b, v):
                dve.wait_ge(rstd_ready, b + 1)
                for t in range(TB):
                    nc.vector.tensor_scalar(xn_ring[:, v, t, :], x[:, ds(b * TB + t, 1), :].rearrange("p o c -> p (o c)"),
                                            mom0[:, v, t, 0:1], rstd[:, v * TB + t:v * TB + t + 1], ALU.subtract, ALU.mult).then_inc(xn_ready, 1)

            def rest0(b, v):
                dve.wait_ge(qk_hi, b + 1)
                dve.wait_ge(qk_lo, b + 1)
                nc.vector.tensor_tensor(qk_rest[:, v % 2, :, :], ps_qk(v % 2).rearrange("p (c t) -> p c t", c=2), qk_p[:, v, :, 0, :], ALU.subtract)\
                    .then_inc(qk_res, 1)

            def parts0(b, v):
                if not isinstance(b, int) or b >= 1:
                    rest0(b - 1, (v - 1) % 4)
                dve.wait_ge(v_put, b + 1)
                nc.vector.tensor_tensor(logits0[:, ds(b * TB, TB), :], ps_v(v % 2)[:, :, D:D + E],
                                        rb0[:, :].unsqueeze(1).broadcast_to([P, TB, E]), ALU.add).then_inc(lg_put, 1)
                if isinstance(b, int) and b in (0, 3):
                    dve.wait_ge(x_in[2 + b // 3], 16)
                if more(b, 4):
                    moments_of(b + 4, v)
                if more(b, 3):
                    if more(b, 4):
                        dve.wait_ge(stats_done, (b + 5) * TB)
                    scale_of(b + 3, (v + 3) % 4)
                    if not isinstance(b, int) or b >= 1:
                        dve.wait_ge(tr_done, b)
                        dve.wait_ge(kept[(v + 3) % 4], filled(b + 3, (v + 3) % 4, 16))
                    normalise0(b + 3, (v + 3) % 4)
                if more(b, 4):
                    variance_of(b + 4, v)
                if isinstance(b, int) and b == B - 4:
                    dve.wait_ge(late_in, 11 * 16)
                    for dst, src in ((ident_h, ident[:, :]), (mask_qk, tables[:, 0, :]), (mask_kq, tables[:, 1, :]), (before, tables[:, 2, :])):
                        nc.vector.tensor_copy(dst[:, :], src).then_inc(consts_ready, 1)
                    nc.vector.memset(ps[:, 6, :], 0.0).then_inc(consts_ready, 1)
            for first in (0, 2):
                dve.wait_ge(x_in[first // 2], 16)
                for b in (first, first + 1):
                    moments_of(b, b)
                    dve.wait_ge(stats_done, (b + 1) * TB)
                    variance_of(b, b)
                for b in range(first, min(first + 2, 3)):
                    scale_of(b, b)
                    normalise0(b, b)
            dve.wait_ge(w_in, 5 * 16)
            run_sequences(dve, parts0, peel=4)
            rest0(B - 1, 3)

            step = [0]

            def then(instruction):
                step[0] += 1
                instruction.then_inc(routed, 1)
                dve.wait_ge(routed, step[0])
            by_expert = [P, NT, E]
            dve.wait_ge(lg_put, B + CREDIT)

            def mark_best(c):
                left = r_b[:, 0, :, :] if c else logits0[:, :, :]
                if c:
                    then(nc.vector.scalar_tensor_tensor(out=left, in0=picked[:, 0, :, :], scalar=-3e38, in1=logits0[:, :, :],
                                                        op0=ALU.mult, op1=ALU.add))
                best = r_s[:, 2 + c, 0, :]
                then(nc.vector.tensor_reduce(best, left, AX.X, ALU.max))
                then(nc.vector.tensor_tensor(r_a[:, 0, :, :], left, best.unsqueeze(2).broadcast_to(by_expert), ALU.is_equal))

            def pick_first(c):
                then(nc.vector.tensor_tensor(r_a[:, 1, :, :], r_a[:, 0, :, :], rank_e[:, 1, :].unsqueeze(1).broadcast_to(by_expert), ALU.mult))
                then(nc.vector.tensor_reduce(r_s[:, 4, 0, :], r_a[:, 1, :, :], AX.X, ALU.max))
                last = nc.vector.tensor_tensor(picked[:, c, :, :], r_a[:, 1, :, :], r_s[:, 4, 0, :].unsqueeze(2).broadcast_to(by_expert), ALU.is_equal)
                then(last)
                if c:
                    nc.vector.tensor_tensor(chosen[:, :, :], picked[:, 0, :, :], picked[:, 1, :, :], ALU.add).then_inc(counted, 1)
                    nc.vector.tensor_tensor(r_s[:, 0, 0, :], r_s[:, 3, 0, :], r_s[:, 2, 0, :], ALU.subtract).then_inc(pick_d, 1)
            ahead, totals, so_far = r_b[:, 0, :, :], r_a[:, 0, :, :], r_a[:, 1, :, :]

            def take_counts():
                dve.wait_ge(counted, 2)
                for n, dst in enumerate((ahead, totals)):
                    last = nc.vector.tensor_copy(dst, ps_count(n).rearrange("p (t e) -> p t e", e=E))
                last.then_inc(counted, 1)
            place, expert, full, row, keep = (r_s[:, k, :, :] for k in (3, 4, 5, 6, 7))

            def count_ahead():
                dve.wait_ge(counted, 3)
                for e in range(E):
                    scan = nc.vector.tensor_tensor_scan(so_far[:, :, e], ones_t[:, :], totals[:, :, e], 0.0, ALU.mult, ALU.add)
                then(scan)
                then(nc.vector.tensor_tensor(r_b[:, 1, :, :], so_far, totals, ALU.subtract))
                then(nc.vector.tensor_tensor(rank[:, :, :], ahead, r_b[:, 1, :, :], ALU.add))

            def pick_places():
                for c in range(2):
                    nc.vector.tensor_tensor(r_a[:, c, :, :], picked[:, c, :, :], rank[:, :, :], ALU.mult)
                    last = nc.vector.tensor_tensor(r_b[:, c, :, :], picked[:, c, :, :], rank_e[:, 0, :].unsqueeze(1).broadcast_to(by_expert), ALU.mult)
                then(last)

            def index_in():
                nc.vector.tensor_reduce(place, r_a[:, :, :, :], AX.X, ALU.add)
                then(nc.vector.tensor_reduce(expert, r_b[:, :, :, :], AX.X, ALU.add))
                nc.vector.scalar_tensor_tensor(out=row, in0=expert, scalar=float(CAP), in1=place, op0=ALU.mult, op1=ALU.add)
                then(nc.vector.tensor_scalar(full, place, CAP - 0.5, float(2 * SLOTS), ALU.is_gt, ALU.mult))
                nc.vector.tensor_tensor(slot_in[:, :, :], row, full, ALU.add).then_inc(indexed, 1)

            def index_out():
                dve.wait_ge(indexed, 1)
                nc.vector.tensor_scalar(keep, place, CAP - 0.5, None, ALU.is_lt)
                then(nc.vector.tensor_scalar(full, row, float(-SLOTS), None, ALU.add))
                then(nc.vector.tensor_tensor(row, full, keep, ALU.mult))
                nc.vector.tensor_scalar(slot_out[:, :, :], row, float(SLOTS), None, ALU.add).then_inc(indexed, 1)

            def weigh_experts():
                dve.wait_ge(pick_e, 1)
                then(nc.vector.tensor_scalar(r_s[:, 2, 0, :], r_s[:, 1, 0, :], 1.0, None, ALU.add))
                then(nc.vector.reciprocal(pick_p[:, 0, :], r_s[:, 2, 0, :]))
                then(nc.vector.tensor_tensor(pick_p[:, 1, :], r_s[:, 1, 0, :], pick_p[:, 0, :], ALU.mult))

            def centre_values():
                w_v = w1_raw[:, 2 * P:3 * P].rearrange("p (h d) -> p h d", h=H1)
                then(nc.vector.tensor_reduce(rb1_s[:, 0:H1], w_v, AX.X, ALU.add))
                then(nc.vector.scalar_tensor_tensor(out=w_v, in0=rb1_s[:, 0:H1].unsqueeze(2).broadcast_to([P, H1, HD1]), scalar=-1.0 / HD1,
                                                    in1=w_v, op0=ALU.mult, op1=ALU.add))

            def split_layer1(parts, src):
                hi, lo = parts
                then(nc.vector.tensor_copy(r32(hi[:, :]), src))
                nc.vector.tensor_tensor(r32(lo[:, :]), src, hi[:, :], ALU.subtract).then_inc(consts_ready, 1)

            def row_max(g):
                dve.wait_ge(s_done, num(g) + 1)
                if past(g, 2):
                    dve.wait_ge(mtr_done, num(g) - 1)
                first = 3 if ahead_of_all(g) else 0
                nc.vector.tensor_reduce(m8[:, at(g, 2), :, 0], ps[:, first, :].rearrange("p (h k) -> p h k", h=GH), AX.X, ALU.max)
                nc.vector.tensor_reduce(m8[:, at(g, 2), :, 1], ps[:, first + 1:first + 3, :].rearrange("p c (h k) -> p (c h) k", h=2),
                                        AX.X, ALU.max).then_inc(max_done, 1)
            mark_best(0)
            pick_first(0)
            row_max((0, 0))
            row_max((0, 1))
            row_max((0, 2))
            mark_best(1)

            def variance_of(tiles):
                dve.wait_ge(x1_done, tiles.stop // (NT // 8))
                for t in range(tiles.start, tiles.stop):
                    nc.vector.bn_aggr(moments[:, t, :], stats1[:, t, :]).then_inc(moments_done, 1)
                dve.wait_ge(moments_done, NT + tiles.stop)
                nc.vector.tensor_scalar(var[:, tiles], moments[:, tiles, 1], EPS, None, ALU.add).then_inc(var_ready, 1)

            def slot(g, late=False):
                if known(g) and num(g) == 1:
                    take_counts()
                if within(plus(g, 3), G0):
                    row_max(plus(g, 3))
                if known(g) and num(g) == 0:
                    pick_first(1)
                if known(g) and num(g) == 3:
                    count_ahead()
                    pick_places()
                if known(g) and num(g) == 4:
                    index_in()
                if known(g) and num(g) == 8:
                    index_out()
                if known(g) and num(g) == 10:
                    weigh_experts()
                if known(g) and num(g) == G0 - 1:
                    variance_of(EARLY)
                if g[1] % GPB0 == 3 and past(g, 11):
                    divide(div(plus(g, -11), GPB0), g[1] // GPB0 % 2)
                if g[1] % GPB0 == 3 and past(g, 15):
                    add_attention(div(plus(g, -15), GPB0), 1 - g[1] // GPB0 % 2)
                if g[1] % GPB0 == 3 and past(g, 7):
                    invert(div(plus(g, -7), GPB0))
                if late and g[1] % GPB0 < 2:
                    add_expert(div(plus(g, -(MIDDLE + 1) * RING), GPB0), g[1] // GPB0 % 2, g[1] % GPB0)
                if late and g[1] % GPB0 == 2:
                    stats_of(div(plus(g, -(MIDDLE + 1) * RING), GPB0))

            def invert(b):
                dve.wait_ge(den_in, b * 16 + 16)
                if not isinstance(b, int) or b >= 1:
                    dve.wait_ge(rden_out, b * 16)
                nc.vector.reciprocal(rden[:, :], den[:, :]).then_inc(rden_done, 1)

            def divide(b, u):
                dve.wait_ge(wv_in[u], (b - u) * 16 + 32)
                if not isinstance(b, int) or b >= 2:
                    dve.wait_ge(wo_mm, b - 1)
                nc.vector.tensor_tensor(wvn[:, u, :], wv_ring[:, u, :], rden_ring[:, u, :], ALU.mult).then_inc(wvn_done, 1)

            def add_attention(b, u):
                dve.wait_ge(at_put, b + 1)
                tiles = x[:, ds(b * TB, TB), :]
                nc.vector.tensor_tensor(tiles, tiles, at_ring[:, u, :, :], ALU.add).then_inc(x_attn, 1)

            def add_expert(k, u, c):
                if c == 0:
                    dve.wait_ge(x_attn, k * 2 + 2)
                    dve.wait_ge(gathered[u], (k - u) * 64 + 128)
                for v in range(NT // 8):
                    tile = ds(k * (NT // 8) + v, 1)
                    row = x[:, tile, :].rearrange("p o c -> p (o c)")
                    nc.vector.scalar_tensor_tensor(out=row, in0=(xn, y_more)[c][:, tile, :].rearrange("p o c -> p (o c)"),
                                                   scalar=pick_p[:, c, tile], in1=row, op0=ALU.mult, op1=ALU.add).then_inc(x1_half, 1)
                dve.wait_ge(x1_half, k * (NT // 4) + (c + 1) * (NT // 8))

            def add_mixed(k):
                dve.wait_ge(mixed, 3)
                dve.wait_ge(x_attn, k * 2 + 2)
                tiles = slice(k * NT // 8, (k + 1) * NT // 8)
                nc.vector.tensor_tensor(x[:, tiles, :], x[:, tiles, :], xn[:, tiles, :], ALU.add).then_inc(x1_half, 1)
                dve.wait_ge(x1_half, LATE.start * 2 + k - 5)

            def stats_of(k):
                for v in range(NT // 8):
                    tile = ds(k * (NT // 8) + v, 1)
                    last = nc.vector.bn_stats(stats1[:, tile, :].rearrange("p o c -> p (o c)"), x[:, tile, :].rearrange("p o c -> p (o c)"))
                last.then_inc(x1_done, 1)

            def middle():
                for e in range(E):
                    dve.wait_ge(sig_done, e + 1)
                    if e >= 1:
                        dve.wait_ge(gated, e)
                    nc.vector.tensor_tensor(act_t[:, :, :].rearrange("p c t -> p (c t)"), ps[:, 2 + e % 2, :],
                                            act_s[:, :, :].rearrange("p c t -> p (c t)"), ALU.mult).then_inc(gate_s, 1)
                    dve.wait_ge(gate_s, e + 1)
                    if e >= 2:
                        dve.wait_ge(down_mm, e - 1)
                    nc.vector.tensor_tensor(act_g[:, e % 2, :, :].rearrange("p c t -> p (c t)"), ps[:, e % 2, :],
                                            act_t[:, :, :].rearrange("p c t -> p (c t)"), ALU.mult).then_inc(gated, 1)
                    if e == 2:
                        centre_values()
                    if e == 3:
                        split_layer1(w1_qk, w1_raw[:, 0:2 * P])
                    if e == 4:
                        split_layer1(w1_p, w1_raw[:, 2 * P:])
            run_slots(dve, G0, slot, middle, peel=2)

            def shift_of(n, tiles):
                dve.wait_ge(std_ready, B + n)
                nc.vector.reciprocal(rstd[:, tiles], std[:, tiles]).then_inc(rstd_ready, 1)
                dve.wait_ge(rstd_ready, B + 2 * n - 1)
                nc.vector.scalar_tensor_tensor(out=shift[:, tiles], in0=moments[:, tiles, 0], scalar=-1.0, in1=rstd[:, tiles],
                                               op0=ALU.mult, op1=ALU.mult).then_inc(rstd_ready, 1)
            shift_of(1, EARLY)

            def normalise(b, u):
                t = b * TB
                nc.vector.tensor_scalar(xn1_ring[:, u, 0, :], x[:, ds(t, 1), :].rearrange("p o c -> p (o c)"),
                                        moments[:, ds(t, 1), 0], rstd[:, ds(t, 1)], ALU.subtract, ALU.mult).then_inc(xn_ready, 1)

            def low_x(b, v):
                dve.wait_ge(xh_put, b + 1)
                nc.vector.tensor_tensor(r32(xr[:, v, 1, :]), ps_t1(v % 2), xr[:, v, 0, :], ALU.subtract).then_inc(xl_put, 1)
            dve.wait_ge(pv_done, G0)
            normalise(0, 0)
            normalise(1, 1)
            dve.wait_ge(tr_done, B + 1)
            normalise(2, 0)
            low_x(0, 0)
            low_x(1, 1)
            dve.wait_ge(late_in, 12 * 16)
            invert(B - 1)

            def rest1(b, v):
                dve.wait_ge(qk1_hi, b + 1)
                dve.wait_ge(qk1_lo, b + 1)
                nc.vector.tensor_tensor(qk1_rest[:, v % 2, :, :], qk1_s[:, v % 2, :, :], qk1_p[:, v, :, 0, :], ALU.subtract).then_inc(qk1_res, 1)

            def parts(b, v):
                u = v % 2
                dve.wait_ge(qk1_mm, b + 1)
                dve.wait_ge(qk1_res, b + 1)
                nc.vector.tensor_tensor(qk1_s[:, u, :, :], ps_qk1(u).rearrange("p (c t) -> p c t", c=2), gam[:, :, :], ALU.mult).then_inc(qk1_scaled, 1)
                if not isinstance(b, int) or b >= 1:
                    rest1(b - 1, (v - 1) % 4)
                dve.wait_ge(sg_put, b + 1)
                nc.vector.tensor_copy(v1[:, ds(b * TB, TB), :, :].rearrange("p t h d -> p t (h d)"), p1_both(u)[:, :, 0:D])
                nc.vector.tensor_tensor(logits1[:, ds(b * TB, TB), :], p1_both(u)[:, :, 2 * D:PROJ1],
                                        rb1[:, :].unsqueeze(1).broadcast_to([P, TB, E]), ALU.add).then_inc(lg1_put, 1)
                if more(b, 3):
                    dve.wait_ge(tr_done, B + b + 2)
                    normalise(b + 3, 1 - u)
                if more(b, 2):
                    low_x(b + 2, (v + 2) % 4)

            def step1(b, v):
                parts(b, v)
                if isinstance(b, int) and b == 0:
                    divide(B - 2, 0)
                if isinstance(b, int) and b == 1:
                    divide(B - 1, 1)
                    add_attention(B - 3, 1)
                    add_mixed(6)
                if isinstance(b, int) and b == 2:
                    add_attention(B - 2, 0)
                    stats_of(6)
                    add_attention(B - 1, 1)
                    add_mixed(7)
                    stats_of(7)
                    variance_of(LATE)
                if isinstance(b, int) and b == 3:
                    shift_of(2, LATE)
            run_sequences(dve, step1, peel=4)
            rest1(B - 1, 3)

            dve.wait_ge(qk1_res, B + CREDIT)

            def slot(g, late=False):
                u = at(g, 2)
                if known(g) and num(g) == 1:
                    for v in range(2):
                        dve.wait_ge(kept[v], 2 * 16 * B // 4)
                if within(g, G1):
                    dve.wait_ge(s1_done, num(g) + 1)
                    if past(g, 2):
                        dve.wait_ge(pv1_done, num(g) - 1)
                    nc.vector.tensor_tensor(sc[:, u, 0:2, :].rearrange("p c (h t) -> p (c h) t", h=GH),
                                            ps[:, 3 * u:3 * u + 2, :].rearrange("p c (h t) -> p (c h) t", h=GH),
                                            upto[:, :].unsqueeze(1).broadcast_to([P, 2 * GH, P]), ALU.mult).then_inc(masked, 1)
                b, v = due(g, 4), half_ring(g, 4)
                if b is not None:
                    dve.wait_ge(ret_put, b * 2 + 2)
                    if past(g, 8):
                        dve.wait_ge(sd_done, b - 1)
                    nc.vector.tensor_reduce(ss1[:, v, :, :], sq[:, v, :, :].rearrange("p t (h d) -> p t h d", h=H1), AX.X, ALU.add)\
                        .then_inc(ss_done, 1)
                b, v = due(g, 5), half_ring(g, 5)
                if b is not None:
                    dve.wait_ge(sd_done, b + 1)
                    if past(g, 9):
                        dve.wait_ge(z_a, b - 1)
                        dve.wait_ge(zt_mm, b - 1)
                    nc.vector.reciprocal(rs1[:, v, :, :], sd1[:, v, :, :]).then_inc(rden_done, 1)
                    dve.wait_ge(rden_done, B + b + 1)
                    nc.vector.tensor_tensor(z[:, v, :, :].rearrange("p t (h d) -> p t h d", h=H1),
                                            ret[:, (g[1] - 5) // 2 % 4, :, :].rearrange("p t (h d) -> p t h d", h=H1),
                                            rs1[:, v, :, :].unsqueeze(3).broadcast_to([P, TB, H1, HD1]), ALU.mult).then_inc(z_a, 1)
                b, v = due(g, 8), half_ring(g, 8)
                if b is not None:
                    dve.wait_ge(at_put, B + b + 1)
                    tiles = x[:, ds(b * TB, TB), :]
                    nc.vector.tensor_tensor(tiles, tiles, at1_ring[:, v, :, :], ALU.add).then_inc(x_attn, 1)
                if known(g) and num(g) == 0:
                    less_max()
                if known(g) and num(g) == 2:
                    normalise_probs()
                if known(g) and 3 <= num(g) < RING:
                    for j in ((0, 1), (2, 3), (4, 5), (6,), (7,))[num(g) - 3]:
                        compare(j)
                if known(g) and 0 <= num(g) - (G1 - RING) < SUMS:
                    sum_before(num(g) - (G1 - RING))
                if known(g) and num(g) == GATES - 2:
                    keep_experts()
                if known(g) and num(g) == G1 + 1:
                    dve.wait_ge(pv1_done, G1)
                    split_weights(0)
                if known(g) and num(g) == G1 + 4:
                    split_unit(0, 0)
                if known(g) and num(g) == G1 + 5:
                    split_unit(0, 1)
                    split_weights(1)

            def less_max():
                dve.wait_ge(lg1_put, B + CREDIT)
                then(nc.vector.tensor_reduce(p1_s[:, 0, :], logits1[:, :, :], AX.X, ALU.max))
                nc.vector.tensor_tensor(p1_x[:, 0, :, :], logits1[:, :, :], p1_s[:, 0, :].unsqueeze(2).broadcast_to(by_expert), ALU.subtract)\
                    .then_inc(pick_d, 1)

            def normalise_probs():
                dve.wait_ge(pick_e, 2)
                then(nc.vector.tensor_reduce(p1_s[:, 1, :], p1_x[:, 1, :, :], AX.X, ALU.add))
                then(nc.vector.reciprocal(p1_s[:, 2, :], p1_s[:, 1, :]))
                then(nc.vector.tensor_tensor(p1[:, :, :], p1_x[:, 1, :, :], p1_s[:, 2, :].unsqueeze(2).broadcast_to(by_expert), ALU.mult))

            def split_weights(e):
                dve.wait_ge(raw_in[e % 2], E // 2 * 16 + e // 2 * 16 + 16)
                nc.vector.tensor_copy(r32(w2_h[:, e, :]), w_raw[:, e % 2, :]).then_inc(w2_hi, 1)
                if e >= 2:
                    dve.wait_ge(w2_hi, e + 1)
                    dve.wait_ge(w2_lo, 2)
                    nc.vector.tensor_tensor(r32(w2_l[:, e, :]), w_raw[:, e % 2, :], w2_h[:, e, :], ALU.subtract).then_inc(w2_lo, 1)

            def split_unit(j, m):
                n = j * UNITS + m
                dve.wait_ge(f_done, n + 1)
                if known_block(j) != 0 or m >= 4:
                    dve.wait_ge(y_mm, n - 3)
                nc.vector.tensor_copy(r32(f_h[:, m % 4, :]), f[:, m % 4, :]).then_inc(f_hi, 1)
                final = known_block(j) == NB - 1 and m == UNITS - 1
                if m % 2 == 0 or final:
                    dve.wait_ge(f_hi, n + 1)
                    if final:
                        dve.wait_ge(f_lo[1], n // 2)
                    nc.vector.tensor_tensor(r32(f_l[:, m % 4, :]), f[:, m % 4, :], f_h[:, m % 4, :], ALU.subtract).then_inc(f_lo[m % 2], 1)

            def compare(j):
                if j:
                    nc.vector.tensor_tensor(order[:, :, 0:j, j], p1[:, :, j:j + 1].broadcast_to([P, NT, j]), p1[:, :, 0:j], ALU.is_gt)
                last = nc.vector.tensor_tensor(order[:, :, j:E, j], p1[:, :, j:j + 1].broadcast_to([P, NT, E - j]), p1[:, :, j:E], ALU.is_ge)
                if j == E - 1:
                    last.then_inc(gates_done, 1)

            def sum_before(k):
                tiles = slice(k * NT // SUMS, (k + 1) * NT // SUMS)
                dve.wait_ge(gates_done, 1 + -(-tiles.stop * PARTS // NT))
                last = nc.vector.tensor_reduce(p1_x[:, 0, tiles, :], order[:, tiles, :, :], AX.X, ALU.add)
                if k == SUMS - 1:
                    then(last)

            def keep_experts():
                up_to = p1_x[:, 0, :, :]
                then(nc.vector.tensor_tensor(p1_x[:, 1, :, :], up_to, p1[:, :, :], ALU.is_equal))
                then(nc.vector.scalar_tensor_tensor(out=up_to, in0=up_to, scalar=TOP_P, in1=p1_x[:, 1, :, :], op0=ALU.is_lt, op1=ALU.max))
                nc.vector.tensor_tensor(gates[:, :, :], up_to, p1[:, :, :], ALU.mult).then_inc(gates_done, 1)
            run_slots(dve, G1, slot, tail=TAIL1)

            def gate_expert(j, e):
                dve.wait_ge(y_mm, j * UNITS + e * FC + FC)
                dve.wait_ge(gate_in[e], j * 16 + 16)
                if e == 0:
                    if known_block(j) != 0:
                        dve.wait_ge(acc_turned, j)
                elif e >= 3:
                    dve.wait_ge(summed, j * (E - 1) + e - 2)
                elif known_block(j) != 0:
                    dve.wait_ge(summed, j * (E - 1))
                nc.vector.scalar_tensor_tensor(out=acc[:, :] if e == 0 else yt[:, e % 2, :], in0=ps[:, 4 + e % 2, :], scalar=b2[:, e:e + 1],
                                               in1=gate_b[:, e, :], op0=ALU.add, op1=ALU.mult).then_inc(yv, 1)

            def finish(j):
                dve.wait_ge(acc_turned, j + 1)
                tiles = x[:, ds(j * TPB, TPB), :]
                nc.vector.tensor_tensor(tiles, tiles, ps[:, 6, :].rearrange("p (t c) -> p t c", t=TPB), ALU.add).then_inc(x2_done, 1)
            dve.wait_ge(x_attn, 2 * B)

            def body(j):
                for m in range(2 if known_block(j) == 0 else 0, UNITS):
                    split_unit(j, m)
                    if known_block(j) == 0 and m % FC == 3 and m // FC + 2 < E:
                        split_weights(m // FC + 2)
                    if m % FC == 2:
                        if m >= 6:
                            gate_expert(j, (m - 6) // FC)
                        elif known_block(j) != 0:
                            gate_expert(j - 1, E - 1)
                    if m == 8 and known_block(j) != 0:
                        finish(j - 1)
            run_blocks(dve, body)
            gate_expert(NB - 1, E - 1)
            dve.wait_ge(yv, NB * E)
            dve.wait_ge(summed, NB * (E - 1) - 1)
            nc.vector.tensor_tensor(acc[:, :], acc[:, :], yt[:, (E - 1) % 2, :], ALU.add).then_inc(summed, 1)
            finish(NB - 1)

        @block.tensor
        def _(pe):
            def transposes0(b, v):
                pe.wait_ge(xn_ready, (b + 1) * TB)
                for t in range(TB):
                    last = nc.tensor.transpose(ps_t(v % 2)[:, t * P:(t + 1) * P], xn_ring[:, v, t, :], ident[:, :])
                last.then_inc(tr_done, 1)

            def products0(b, v):
                u = v % 2
                pe.wait_ge(xT_done, b + 1)
                pe.wait_ge(qk_res, b + 1)
                for c, w in enumerate((w_q, w_k)):
                    last = nc.tensor.matmul(ps_qk(u)[:, c * S:(c + 1) * S], w[:, :], xT[:, u, :], start=True, stop=True)
                last.then_inc(qk_mm, 1)
                pe.wait_ge(lg_put, b + 1)
                for t in range(TB):
                    last = nc.tensor.matmul(ps_v(u)[:, t, :], xT[:, u, t * P:(t + 1) * P], w_vr[:, :], start=True, stop=True)
                last.then_inc(v_mm, 1)
                if more(b, 2):
                    transposes0(b + 2, (v + 2) % 4)
            pe.wait_ge(w_in, 5 * 16)
            transposes0(0, 0)
            transposes0(1, 1)
            run_sequences(pe, products0)
            pe.wait_ge(consts_ready, 5)
            pe.wait_ge(qk_res, B + CREDIT)
            pe.wait_ge(lg_put, B + CREDIT)

            def scores(g):
                r = at(g, RING)
                qs, ks = (st[:, r // 2, (r % 2) * GH:(r % 2) * GH + GH, :] for st in (q_st, k_st))
                if r % 2 == 0:
                    pe.wait_ge(stack_in[r // 2], div(g, RING) * 64 + 64)
                dst = ps_st if ahead_of_all(g) else ps_s
                if past(g, 2):
                    pe.wait_ge(max_done, 1 if known(g) and num(g) == 2 else num(g))
                nc.tensor.matmul(dst(0).rearrange("p (h k) -> p h k", h=GH), ident_h[:, :],
                                 mask_qk[:, :].unsqueeze(1).broadcast_to([P, GH, P]), start=True, stop=False, skip_group_check=True)
                for c in (1, 2):
                    nc.tensor.matmul(dst(c).rearrange("p (h k) -> p h k", h=2)[:, :, P:S], ident_h[:, :],
                                     mask_qk[:, :].unsqueeze(1).broadcast_to([P, 2, P]), start=True, stop=False, skip_group_check=True)
                for h in range(GH):
                    nc.tensor.matmul(dst(0)[:, h * P:(h + 1) * P], qs[0:R0, h, 0:P], ks[0:R0, h, 0:P],
                                     start=False, stop=True, skip_group_check=True)
                for h in range(GH):
                    last = nc.tensor.matmul(dst(1 + h // 2)[:, h % 2 * S:(h % 2 + 1) * S], qs[0:R0, h, P:S], ks[0:R0, h, :],
                                            start=False, stop=True, skip_group_check=True)
                last.then_inc(s_done, 1)

            def turn_max(g):
                pe.wait_ge(max_done, num(g) + 1)
                if past(g, 1):
                    pe.wait_ge(mneg_done, num(g))
                nc.tensor.transpose(ps_m, m8[:, at(g, 2), :, :].rearrange("p h t -> p (h t)"), ident[:, :]).then_inc(mtr_done, 1)

            def scores_t(g):
                r = at(g, RING)
                qs, ks = (st[0:R0 + 1, r // 2, (r % 2) * GH:(r % 2) * GH + GH, :] for st in (q_st, k_st))
                if past(g, 1):
                    pe.wait_ge(exp_done, num(g))
                else:
                    pe.wait_ge(max_done, 2)
                nc.tensor.matmul(ps_st(0).rearrange("p (h k) -> p h k", h=GH), ident_h[:, :],
                                 mask_kq[:, :].unsqueeze(1).broadcast_to([P, GH, P]), start=True, stop=False, skip_group_check=True)
                for c in (1, 2):
                    nc.tensor.matmul(ps_st(c).rearrange("p (h k) -> p h k", h=2)[:, :, 0:P], ident_h[:, :],
                                     mask_kq[:, :].unsqueeze(1).broadcast_to([P, 2, P]), start=True, stop=False, skip_group_check=True)
                pe.wait_ge(mrow_in[r % 4], div(g, 4) * 16 + 16)
                for h in range(GH):
                    nc.tensor.matmul(ps_st(0)[:, h * P:(h + 1) * P], ks[:, h, P:S], qs[:, h, P:S],
                                     start=False, stop=True, skip_group_check=True)
                for h in range(GH):
                    last = nc.tensor.matmul(ps_st(1 + h // 2)[:, h % 2 * S:(h % 2 + 1) * S], ks[:, h, 0:P], qs[:, h, :],
                                            start=False, stop=True, skip_group_check=True)
                last.then_inc(st_done, 1)

            def weigh(g):
                k, u = at(g, GPB0), at(g, RING) // GPB0
                pe.wait_ge(exp_done, num(g) + 1)
                if k == 0:
                    pe.wait_ge(v_here, div(g, GPB0) + 1)
                if past(g, 1):
                    pe.wait_ge(o_evac, num(g))
                if k == 2 and past(g, 14):
                    pe.wait_ge(at_put, div(plus(g, -14), GPB0) + 1)
                for h in range(GH):
                    nc.tensor.matmul(ps_o[32 * h:32 * h + 2 * HD0, :], v_ring[:, u, 0, k * GH + h, :],
                                     probs[:, at(g, 2), 1 + h // 2, h % 2 * S:(h % 2 + 1) * S],
                                     start=True, stop=False, skip_group_check=True)
                for h in range(GH):
                    last = nc.tensor.matmul(ps_o[32 * h:32 * h + 2 * HD0, P:S], v_ring[:, u, 1, k * GH + h, :],
                                            probs[:, at(g, 2), 0, h * P:(h + 1) * P],
                                            start=False, stop=True, skip_group_check=True)
                last.then_inc(pv_done, 1)

            def count():
                pe.wait_ge(counted, 1)
                pe.wait_ge(mneg_done, 3)
                for n, lhs in enumerate((before, ones_h)):
                    last = nc.tensor.matmul(ps_count(n), lhs[:, :], chosen[:, :, :].rearrange("p t e -> p (t e)"), start=True, stop=True)
                last.then_inc(counted, 1)

            for n in range(3):
                scores((0, n))
                if n:
                    turn_max((0, n - 1))

            def slot(g, late=False):
                if known(g) and num(g) == 1:
                    count()
                if within(plus(g, 3), G0):
                    scores(plus(g, 3))
                if known(g) and num(g) == 1:
                    pe.wait_ge(counted, 3)
                if within(plus(g, 2), G0):
                    turn_max(plus(g, 2))
                scores_t(g)
                if g[1] % GPB0 == 2 and past(g, 14):
                    pe.wait_ge(o_evac, num(g) - 1)
                    attention_out(div(plus(g, -14), GPB0), 1 - g[1] // GPB0 % 2, ps_at)
                if past(g, 1):
                    weigh(plus(g, -1))

            def attention_out(b, u, dst):
                pe.wait_ge(wvn_done, b + 1)
                for t in range(TB):
                    last = nc.tensor.matmul(dst[:, t * P:(t + 1) * P], wvn[:, u, t * P:(t + 1) * P], w_o[:, :], start=True, stop=True)
                last.then_inc(wo_mm, 1)

            def middle():
                n = MIDDLE * RING
                pe.wait_ge(experts_in, 2 * E * 16)
                pe.wait_ge(expert_rows, 16)
                pe.wait_ge(max_done, n + 3)
                pe.wait_ge(exp_done, n)
                for c in range(SLOTS // P):
                    last = nc.tensor.transpose(ps[:, c // 4, c % 4 * P:(c % 4 + 1) * P], xg[:, c, :], ident[:, :])
                    if c % 4 == 3:
                        last.then_inc(xgt_mm, 1)
                pe.wait_ge(xgt_put, SLOTS // 512)

                def up(e):
                    if e >= 2:
                        pe.wait_ge(gated, e - 1)
                    for m, bank in ((0, e % 2), (1, 2 + e % 2)):
                        for c in range(2):
                            last = nc.tensor.matmul(ps[:, bank, c * CAP:(c + 1) * CAP], w_up[:, e, m, c * P:(c + 1) * P],
                                                    xgT[:, e * CAP:(e + 1) * CAP], start=True, stop=True)
                    last.then_inc(up_mm, 1)

                def down(e):
                    pe.wait_ge(gated, e + 1)
                    if e >= 2:
                        pe.wait_ge(y_put, e - 1)
                    for t in range(CAP // P):
                        for c in range(2):
                            last = nc.tensor.matmul(ps[:, 4 + e % 2, t * D:(t + 1) * D], act_g[:, e % 2, c, t * P:(t + 1) * P],
                                                    w_dn[:, e, c, :], start=(c == 0), stop=(c == 1))
                    last.then_inc(down_mm, 1)
                up(0)
                for e in range(E):
                    if e + 1 < E:
                        up(e + 1)
                    down(e)
                pe.wait_ge(y_put, E)
            run_slots(pe, G0, slot, middle, peel=2)
            weigh((0, G0 - 1))
            pe.wait_ge(o_evac, G0)

            def transposes(b, u):
                pe.wait_ge(xn_ready, B * TB + b + 1)
                pe.wait_ge(xn_second, b + 1)
                pe.wait_ge(xl_put, b + 1)
                for t in range(TB):
                    last = nc.tensor.transpose(ps_t1(u)[:, t * P:(t + 1) * P], xn1_ring[:, u, t, :], ident[:, :])
                last.then_inc(tr_done, 1)

            def three(dst, lhs, rhs):
                for k, (i, j) in enumerate(((0, 0), (1, 0), (0, 1))):
                    last = nc.tensor.matmul(dst, r32(lhs[i]), r32(rhs[j]), start=(k == 0), stop=(k == 2))
                return last

            def products(b, v):
                u = v % 2
                pe.wait_ge(xl_put, b + 1 + CREDIT)
                rhs = [xr[:, v, i, :] for i in range(2)]
                pe.wait_ge(qk1_scaled, b + 1)
                for c in range(2):
                    last = three(ps_qk1(u)[:, c * S:(c + 1) * S], [w[:, c * P:(c + 1) * P] for w in w1_qk], rhs)
                last.then_inc(qk1_mm, 1)
                pe.wait_ge(lg1_put, b + 1)
                for t in range(TB):
                    last = three(ps_p1(u, t), [x_[:, t * P:(t + 1) * P] for x_ in rhs], [w[:, :] for w in w1_p])
                last.then_inc(p1_mm, 1)
            pe.wait_ge(consts_ready, 7)
            transposes(0, 0)
            transposes(1, 1)

            def step(b, v):
                products(b, v)
                if isinstance(b, int) and b - 1 in LATE_OUT:
                    pe.wait_ge(at_put, LATE_OUT[b - 1] + 1)
                if more(b, 2):
                    transposes(b + 2, v % 2)
                if isinstance(b, int) and b in LATE_OUT:
                    pe.wait_ge(xl_put, b + 2 + CREDIT)
                    attention_out(LATE_OUT[b], LATE_OUT[b] % 2, ps_t1((b + 1) % 2))
            run_sequences(pe, step, peel=4)

            def scores1(g):
                r, u = at(g, RING), at(g, 2)
                qs, ks = (st[:, r // 2, u * GH:(u + 1) * GH, :] for st in (q1_st, k1_st))
                if r % 2 == 0:
                    pe.wait_ge(stack1_in[r // 2], div(g, RING) * 80 + 80)
                if past(g, 2):
                    pe.wait_ge(masked, num(g) - 1)
                    pe.wait_ge(copied, num(g) - 1)
                for c, (k, q) in enumerate(((1, 1), (0, 0), (0, 1))):
                    for h in range(GH):
                        last = nc.tensor.matmul(ps_sc(u, c)[:, h * P:(h + 1) * P], ks[:, h, k * P:(k + 1) * P], qs[:, h, q * P:(q + 1) * P],
                                                start=True, stop=True)
                last.then_inc(s1_done, 1)

            def weigh1(g, projected=None):
                u, half = at(g, RING) // 2 % 2, g[1] % 2
                pe.wait_ge(masked, num(g) + 1)
                pe.wait_ge(copied, num(g) + 1)
                if known(g) and num(g) == 0:
                    pe.wait_ge(lg1_put, B + CREDIT)
                if not known(g):
                    pe.wait_ge(v1_here, div(g, 2) - 2)

                def value(t, h):
                    return v1[:, num(g) // 2 * TB + t, h, :] if known(g) else v1_ring[:, u, t, h, :]
                if past(g, 1):
                    pe.wait_ge(o1_evac, num(g))
                if projected is not None:
                    pe.wait_ge(at_put, B + projected + 1)
                for h in range(GH):
                    nc.tensor.matmul(ps_o1[32 * h:32 * h + HD1, :].rearrange("p (c t) -> p c t", c=2), value(0, half * GH + h),
                                     sc[:, at(g, 2), 1:3, h * P:(h + 1) * P], start=True, stop=False, skip_group_check=True)
                for h in range(GH):
                    last = nc.tensor.matmul(ps_o1[32 * h:32 * h + HD1, P:S], value(1, half * GH + h),
                                            sc[:, at(g, 2), 0, h * P:(h + 1) * P], start=False, stop=True, skip_group_check=True)
                last.then_inc(pv1_done, 1)

            def turn1(g):
                pe.wait_ge(o1_evac, num(g) + 1)
                if past(g, 1):
                    pe.wait_ge(ret_put, num(g))
                for t in range(TB):
                    last = nc.tensor.transpose(ps_r1[:, t * P:(t + 1) * P], o1_ring[:, at(g, 2), t * P:(t + 1) * P], ident[:, :])
                last.then_inc(turned1, 1)

            pe.wait_ge(lg1_put, B + CREDIT)

            def hidden(j, m):
                if m >= UNITS:
                    j, m = j + 1, m - UNITS
                n, (e, c) = j * UNITS + m, divmod(m, FC)
                if known_block(j) == 0 and c == 0:
                    pe.wait_ge(w1_lo, e + 1)
                if known_block(j) != 0 or m >= 4:
                    pe.wait_ge(f_done, n - 3)
                three(ps[:, m % 4, :], [w[:, e, c * P:(c + 1) * P] for w in (w1_h, w1_l)],
                      [x_hl[:, i, ds(j * BLK, BLK)] for i in range(2)]).then_inc(h_mm, 1)

            def slot(g, late=False):
                if within(g, G1):
                    scores1(g)
                if known(g) and num(g) == G1 + 1:
                    pe.wait_ge(masked, G1)
                    pe.wait_ge(copied, G1)
                if known(g) and 0 <= num(g) - G1 - 1 <= AHEAD:
                    hidden(0, num(g) - G1 - 1)
                b = due(g, 8)
                if b is not None:
                    pe.wait_ge(o1_evac, G1 if not within(plus(g, -2), G1) else num(g) - 1)
                    pe.wait_ge(zt_put, b + 1)
                    if known(g) and num(g) == GATES + 1:
                        pe.wait_ge(gt_put, 1)
                    u = half_ring(g, 8)
                    for t in range(TB):
                        last = nc.tensor.matmul(ps_at1[:, t * P:(t + 1) * P], zT[:, u, t * P:(t + 1) * P], w2_a[:, :], start=True, stop=True)
                    last.then_inc(wo_mm, 1)
                projected = due(g, 9)
                weighs = past(g, 1) and within(plus(g, -1), G1)
                if projected is not None and not weighs:
                    pe.wait_ge(at_put, B + projected + 1)
                if known(g) and num(g) == GATES:
                    pe.wait_ge(gates_done, PARTS + 2)
                    pe.wait_ge(o1_evac, num(g) - 1)
                    for c in range(2):
                        last = nc.tensor.transpose(ps_at1[:, c * P:(c + 1) * P],
                                                   gates[:, c * NT // 2:(c + 1) * NT // 2, :].rearrange("p t e -> p (t e)"), ident[:, :])
                    last.then_inc(gt_mm, 1)
                if weighs:
                    weigh1(plus(g, -1), projected)
                b = due(g, 7)
                if b is not None:
                    pe.wait_ge(z_done, b + 1)
                    pe.wait_ge(ret_put, G1 if not within(plus(g, -3), G1) else num(g) - 2)
                    for t in range(TB):
                        last = nc.tensor.transpose(ps_zt[:, t * P:(t + 1) * P], z[:, half_ring(g, 7), t, :], ident[:, :])
                    last.then_inc(zt_mm, 1)
                b = due(g, 8)
                if b is not None:
                    pe.wait_ge(zt_put, b + 1)
                if past(g, 2) and within(plus(g, -2), G1):
                    turn1(plus(g, -2))
            run_slots(pe, G1, slot, tail=TAIL1)

            def output(j, m):
                n, (e, c) = j * UNITS + m, divmod(m, FC)
                if c == 0:
                    if known_block(j) == 0:
                        pe.wait_ge(w2_lo, e + 1)
                    if known_block(j) != 0 or e >= 2:
                        pe.wait_ge(yv, j * E + e - 1)
                pe.wait_ge(f_hi, n + 1)
                w = [w_[:, e, c * P:(c + 1) * P] for w_ in (w2_h, w2_l)]
                for k, (i, fs) in enumerate(((0, f_h), (1, f_h), (0, f_l))):
                    if k == 2:
                        pe.wait_ge(f_lo[m % 2], j * (UNITS // 2) + m // 2 + 1)
                    last = nc.tensor.matmul(ps[:, 4 + e % 2, :], r32(w[i]), r32(fs[:, m % 4, :]), start=(c == 0 and k == 0),
                                            stop=(c == FC - 1 and k == 2))
                last.then_inc(y_mm, 1)

            def turn_sum(j):
                pe.wait_ge(summed, (j + 1) * (E - 1))
                if known_block(j) != 0:
                    pe.wait_ge(x2_done, j)
                for t in range(TPB):
                    last = nc.tensor.transpose(ps[:, 6, t * P:(t + 1) * P], acc[:, t * P:(t + 1) * P], ident[:, :])
                last.then_inc(acc_turned, 1)
            def body(j):
                for m in range(UNITS):
                    if (known_block(j) != 0 or m > 0) and (known_block(j) != NB - 1 or m + AHEAD < UNITS):
                        hidden(j, m + AHEAD)
                    output(j, m)
                    if m == 4 and known_block(j) != 0:
                        turn_sum(j - 1)
            run_blocks(pe, body)
            turn_sum(NB - 1)


_OUT = ((B, S, D), "float32")


def kernel(**inputs):
    import numpy as np
    import concourse.bacc as bacc
    from concourse.bass_utils import run_bass_kernel_spmd

    arrays = prepare(inputs, np)
    nc = bacc.Bacc("TRN2", target_bir_lowering=False, num_devices=1)
    aps = {k: nc.dram_tensor(f"in_{k}", v.shape, mybir.dt.from_np(v.dtype), kind="ExternalInput").ap() for k, v in arrays.items()}
    out = nc.dram_tensor("out_0", (N, D), F32, kind="ExternalOutput").ap()
    build(nc, aps, out)
    r = run_bass_kernel_spmd(nc, [{f"in_{k}": v for k, v in arrays.items()}], core_ids=[0])
    return r.results[0]["out_0"].reshape(B, S, D)


def prepare(inputs, np):
    i = {k: np.ascontiguousarray(v) for k, v in inputs.items()}
    at = np.arange(P)
    tables = np.zeros((P, 3, P), np.float32)
    tables[:, 0, :] = np.where(at[None, :] > at[:, None], np.float32(NEG), np.float32(0))
    tables[:, 1, :] = tables[:, 0, :].T
    tables[:, 2, :] = (at[:, None] < at[None, :])
    ex = np.arange(E)
    gamma = (1.0 - np.exp(np.linspace(np.log(1.0 / 512.0), np.log(1.0 / 32.0), H1))).astype(np.float32).astype(np.float64)
    place = np.arange(S)
    gam = np.stack([np.tile(gamma[:, None] ** k, (HD1, 1)) for k in (place[None, :], -place[None, :])], axis=1)

    def rows(v):
        return np.ascontiguousarray(np.broadcast_to(v, (P,) + v.shape))

    def by_depth(w, heads):
        return np.ascontiguousarray(w.reshape(P, heads, -1).transpose(0, 2, 1).reshape(P, P))

    def diagonal(w):
        m = np.zeros((H1, HD1, H1, HD1), np.float32)
        for h in range(H1):
            m[h, :, h, :] = w[h]
        return m.reshape(P, P)
    qvk = i["L0_attn_Wqvk"]
    return {
        "h": np.ascontiguousarray(i["L0_attn_h"].reshape(NT, P, D).transpose(1, 0, 2)),
        "ident": np.eye(P, dtype=np.float32),
        "tables": tables,
        "upto": (at[:, None] <= at[None, :]).astype(np.float32),
        "w_q": by_depth(qvk[:, 0:D], H0),
        "w_k": by_depth(qvk[:, 2 * D:3 * D], H0),
        "w_vr": np.concatenate([qvk[:, D:2 * D], i["L0_ffn_router_w"].T], axis=1),
        "w_o": i["L0_attn_Wo"],
        "rb0": rows(i["L0_ffn_router_b"]),
        "rank_e": rows(np.stack([ex, E - ex]).astype(np.float32)),
        "w_up": np.ascontiguousarray(np.stack([i["L0_ffn_W"], i["L0_ffn_V"]], axis=1).transpose(2, 0, 1, 3)),
        "w_dn": np.ascontiguousarray(i["L0_ffn_W_out"].reshape(E, 2, P, D).transpose(2, 0, 1, 3)),
        "w1_raw": np.concatenate([by_depth(diagonal(i["L1_attn_Wq"]), H1), by_depth(diagonal(i["L1_attn_Wk"]), H1),
                                  diagonal(i["L1_attn_Wv"]), i["L1_attn_W1"], i["L1_ffn_Wr"]], axis=1),
        "w2_a": i["L1_attn_W2"],
        "gn_w": rows(i["L1_attn_gn_w"]),
        "gn_b": rows(i["L1_attn_gn_b"]),
        "rb1": rows(i["L1_ffn_br"]),
        "gam": gam.astype(np.float32),
        "w1_e": np.ascontiguousarray(i["L1_ffn_W1"].transpose(1, 0, 2)),
        "w2_e": np.ascontiguousarray(i["L1_ffn_W2"].reshape(E, FC, P, D).transpose(2, 0, 1, 3).reshape(P, E, FC * D)),
        "b1": np.ascontiguousarray(i["L1_ffn_b1"].reshape(UNITS, P).T),
        "b2": np.ascontiguousarray(i["L1_ffn_b2"].T),
    }
```
